# Optimizing a Trainium2 kernel written in Bass

```python
import numpy as np
import jax
import jax.numpy as jnp

def _softmax(x, axis=-1):
    return jax.nn.softmax(x, axis=axis)

def _gelu(x):
    return jax.nn.gelu(x, approximate=True)

def _silu(x):
    return jax.nn.silu(x)

def _sigmoid(x):
    return jax.nn.sigmoid(x)

def _layernorm(x, axis=-1, eps=1e-05):
    m = jnp.mean(x, axis=axis, keepdims=True)
    v = jnp.var(x, axis=axis, keepdims=True)
    return (x - m) / jnp.sqrt(v + eps)

def _scatter_add(tgt, idx, src, axis=0):
    return tgt.at[idx].add(src)

def _segment_sum(src, seg, n):
    return jax.ops.segment_sum(src, seg, n)
kernel_name = 'mk_hybrid_d1_jaxref_r8_6d8276'

def setup_inputs(seed: int=0):
    np.random.seed(seed)
    _w = jnp.asarray

    def _L0_attn_a_setup():
        import jax, jax.numpy as jnp
        import numpy as np
        B, T, C = (8, 128, 256)

        def wkv(time_decay, time_first, k, v):
            w = -jnp.exp(time_decay)
            u = time_first
            b, t, c = k.shape
            k_t = jnp.transpose(k, (1, 0, 2))
            v_t = jnp.transpose(v, (1, 0, 2))

            def step(carry, kv):
                p, q, o = carry
                kt, vt = kv
                no = jnp.maximum(o, u + kt)
                A = jnp.exp(o - no)
                Bc = jnp.exp(u + kt - no)
                y = (A * p + Bc * vt) / (A * q + Bc)
                no2 = jnp.maximum(w + o, kt)
                A2 = jnp.exp(w + o - no2)
                B2 = jnp.exp(kt - no2)
                return ((A2 * p + B2 * vt, A2 * q + B2, no2), y)
            init = (jnp.zeros((b, c), k.dtype), jnp.zeros((b, c), k.dtype), jnp.full((b, c), -1e+38, k.dtype))
            _, y = jax.lax.scan(step, init, (k_t, v_t))
            return jnp.transpose(y, (1, 0, 2))
        key = jax.random.key(seed)
        k1, k2, k3, k4, k5 = jax.random.split(key, 5)
        x = jax.random.normal(k1, (B, T, C), dtype=jnp.float32)
        W_rvk = jax.random.normal(k2, (3 * C, C), dtype=jnp.float32) / np.sqrt(C).astype(np.float32)
        W_out = jax.random.normal(k3, (C, C), dtype=jnp.float32) / np.sqrt(C).astype(np.float32)
        time_decay = jax.random.normal(k4, (C,), dtype=jnp.float32) * 0.1
        time_first = jax.random.normal(k5, (C,), dtype=jnp.float32) * 0.1
        return {'x': x, 'W_rvk': W_rvk, 'W_out': W_out, 'time_decay': time_decay, 'time_first': time_first}
    _L0_attn_a_in = _L0_attn_a_setup()

    def _L0_attn_b_setup():
        import jax, jax.numpy as jnp
        import numpy as np
        B, S, HID, QK, H = (2, 256, 256, 256, 16)
        DK, DV = (QK // H, HID // H)
        EPS = 1e-05
        key = jax.random.key(seed)
        ks = jax.random.split(key, 8)
        sd = 1.0 / np.sqrt(HID)
        inp = {'x': jax.random.normal(ks[0], (B, S, HID), jnp.float32), 'wq': jax.random.normal(ks[1], (HID, QK), jnp.float32) * sd, 'bq': jnp.zeros((QK,), jnp.float32), 'wk': jax.random.normal(ks[2], (HID, QK), jnp.float32) * sd, 'bk': jnp.zeros((QK,), jnp.float32), 'wv': jax.random.normal(ks[3], (HID, HID), jnp.float32) * sd, 'bv': jnp.zeros((HID,), jnp.float32), 'wg': jax.random.normal(ks[4], (HID, HID), jnp.float32) * sd, 'bg': jnp.zeros((HID,), jnp.float32), 'wo': jax.random.normal(ks[5], (HID, HID), jnp.float32) * sd, 'bo': jnp.zeros((HID,), jnp.float32), 'gn_w': jnp.ones((HID,), jnp.float32), 'gn_b': jnp.zeros((HID,), jnp.float32), 'gamma': 1.0 - jnp.exp(jnp.linspace(-np.log(32.0), -np.log(512.0), H)).astype(jnp.float32)}
        return inp
    _L0_attn_b_in = _L0_attn_b_setup()

    def _L0_ffn_setup():
        import jax, jax.numpy as jnp
        import numpy as np
        B, T, D = (2, 128, 256)
        E, F, K = (64, 64, 4)
        S, HS = (2, 64 * 4)
        key = jax.random.key(seed)
        ks = jax.random.split(key, 9)
        s = 0.02
        f32 = jnp.float32
        return {'x': jax.random.normal(ks[0], (B, T, D), f32), 'router_w': jax.random.normal(ks[1], (D, E), f32) * s, 'router_bias': jnp.zeros((E,), f32), 'wg': jax.random.normal(ks[2], (E, D, F), f32) * s, 'wu': jax.random.normal(ks[3], (E, D, F), f32) * s, 'wd': jax.random.normal(ks[4], (E, F, D), f32) * s, 'swg': jax.random.normal(ks[5], (S, D, HS), f32) * s, 'swu': jax.random.normal(ks[6], (S, D, HS), f32) * s, 'swd': jax.random.normal(ks[7], (S, HS, D), f32) * s}
    _L0_ffn_in = _L0_ffn_setup()
    _d = {'L0_attn_a_x': _L0_attn_a_in['x'], 'L0_attn_a_W_rvk': _L0_attn_a_in['W_rvk'], 'L0_attn_a_W_out': _L0_attn_a_in['W_out'], 'L0_attn_a_time_decay': _L0_attn_a_in['time_decay'], 'L0_attn_a_time_first': _L0_attn_a_in['time_first'], 'L0_attn_b_wq': _L0_attn_b_in['wq'], 'L0_attn_b_bq': _L0_attn_b_in['bq'], 'L0_attn_b_wk': _L0_attn_b_in['wk'], 'L0_attn_b_bk': _L0_attn_b_in['bk'], 'L0_attn_b_wv': _L0_attn_b_in['wv'], 'L0_attn_b_bv': _L0_attn_b_in['bv'], 'L0_attn_b_wg': _L0_attn_b_in['wg'], 'L0_attn_b_bg': _L0_attn_b_in['bg'], 'L0_attn_b_wo': _L0_attn_b_in['wo'], 'L0_attn_b_bo': _L0_attn_b_in['bo'], 'L0_attn_b_gn_w': _L0_attn_b_in['gn_w'], 'L0_attn_b_gn_b': _L0_attn_b_in['gn_b'], 'L0_attn_b_gamma': _L0_attn_b_in['gamma'], 'L0_ffn_router_w': _L0_ffn_in['router_w'], 'L0_ffn_router_bias': _L0_ffn_in['router_bias'], 'L0_ffn_wg': _L0_ffn_in['wg'], 'L0_ffn_wu': _L0_ffn_in['wu'], 'L0_ffn_wd': _L0_ffn_in['wd'], 'L0_ffn_swg': _L0_ffn_in['swg'], 'L0_ffn_swu': _L0_ffn_in['swu'], 'L0_ffn_swd': _L0_ffn_in['swd']}
    _x0 = _d['L0_attn_a_x']
    _d['L0_attn_a_x'] = jax.random.normal(jax.random.fold_in(jax.random.key(seed), 1), (4, 1024, 256), dtype=_x0.dtype)
    del _x0
    return _d

def reference(L0_attn_a_x, L0_attn_a_W_rvk, L0_attn_a_W_out, L0_attn_a_time_decay, L0_attn_a_time_first, L0_attn_b_wq, L0_attn_b_bq, L0_attn_b_wk, L0_attn_b_bk, L0_attn_b_wv, L0_attn_b_bv, L0_attn_b_wg, L0_attn_b_bg, L0_attn_b_wo, L0_attn_b_bo, L0_attn_b_gn_w, L0_attn_b_gn_b, L0_attn_b_gamma, L0_ffn_router_w, L0_ffn_router_bias, L0_ffn_wg, L0_ffn_wu, L0_ffn_wd, L0_ffn_swg, L0_ffn_swu, L0_ffn_swd):

    def _L0_attn_a_ref(x, W_rvk, W_out, time_decay, time_first):
        import jax, jax.numpy as jnp
        import numpy as np
        B, T, C = (8, 128, 256)

        def wkv(time_decay, time_first, k, v):
            w = -jnp.exp(time_decay)
            u = time_first
            b, t, c = k.shape
            k_t = jnp.transpose(k, (1, 0, 2))
            v_t = jnp.transpose(v, (1, 0, 2))

            def step(carry, kv):
                p, q, o = carry
                kt, vt = kv
                no = jnp.maximum(o, u + kt)
                A = jnp.exp(o - no)
                Bc = jnp.exp(u + kt - no)
                y = (A * p + Bc * vt) / (A * q + Bc)
                no2 = jnp.maximum(w + o, kt)
                A2 = jnp.exp(w + o - no2)
                B2 = jnp.exp(kt - no2)
                return ((A2 * p + B2 * vt, A2 * q + B2, no2), y)
            init = (jnp.zeros((b, c), k.dtype), jnp.zeros((b, c), k.dtype), jnp.full((b, c), -1e+38, k.dtype))
            _, y = jax.lax.scan(step, init, (k_t, v_t))
            return jnp.transpose(y, (1, 0, 2))
        rvk = jnp.einsum('btc,dc->btd', x, W_rvk)
        r, v, k = jnp.split(rvk, 3, axis=-1)
        y = jax.nn.sigmoid(r) * wkv(time_decay, time_first, k, v)
        return jnp.einsum('btc,dc->btd', y, W_out)

    def _L0_attn_b_ref(x, wq, bq, wk, bk, wv, bv, wg, bg, wo, bo, gn_w, gn_b, gamma):
        import jax, jax.numpy as jnp
        import numpy as np
        B, S, HID, QK, H = (2, 256, 256, 256, 16)
        DK, DV = (QK // H, HID // H)
        EPS = 1e-05
        b, s, hid = x.shape
        h = gamma.shape[0]
        dk = wq.shape[1] // h
        dv = hid // h
        q = (x @ wq + bq).reshape(b, s, h, dk).transpose(0, 2, 1, 3)
        k = (x @ wk + bk).reshape(b, s, h, dk).transpose(0, 2, 1, 3)
        v = (x @ wv + bv).reshape(b, s, h, dv).transpose(0, 2, 1, 3)
        idx = jnp.arange(s)
        diff = idx[:, None] - idx[None, :]
        expn = jnp.maximum(diff, 0).astype(x.dtype)
        dmask = jnp.where(diff >= 0, gamma[:, None, None] ** expn, 0.0)
        scores = jnp.einsum('bhnd,bhmd->bhnm', q, k) * dmask
        ret = jnp.einsum('bhnm,bhmv->bhnv', scores, v)
        mean = ret.mean(axis=(2, 3), keepdims=True)
        var = ((ret - mean) ** 2).mean(axis=(2, 3), keepdims=True)
        norm = (ret - mean) * jax.lax.rsqrt(var + EPS)
        norm = norm * gn_w.reshape(h, dv)[None, :, None, :] + gn_b.reshape(h, dv)[None, :, None, :]
        ro = norm.transpose(0, 2, 1, 3).reshape(b, s, hid)
        gate = jax.nn.silu(x @ wg + bg)
        out = gate * ro @ wo + bo
        return out

    def _L0_ffn_ref(x, router_w, router_bias, wg, wu, wd, swg, swu, swd):
        import jax, jax.numpy as jnp
        import numpy as np
        B, T, D = (2, 128, 256)
        E, F, K = (64, 64, 4)
        S, HS = (2, 64 * 4)
        b, t, d = x.shape
        flat = x.reshape(b * t, d)
        n = flat.shape[0]
        logits = flat @ router_w
        scores = jax.nn.softmax(logits, axis=-1)
        _, topk_idx = jax.lax.top_k(logits + router_bias, K)
        topk_scores = jnp.take_along_axis(scores, topk_idx, axis=-1)
        topk_scores = topk_scores / topk_scores.sum(axis=-1, keepdims=True)
        comb = jnp.zeros((n, E), dtype=flat.dtype).at[jnp.arange(n)[:, None], topk_idx].set(topk_scores)
        g = jax.nn.silu(jnp.einsum('nd,edf->nef', flat, wg))
        u = jnp.einsum('nd,edf->nef', flat, wu)
        routed = jnp.einsum('ne,nef,efd->nd', comb, g * u, wd)
        sg = jax.nn.silu(jnp.einsum('nd,sdh->nsh', flat, swg))
        su = jnp.einsum('nd,sdh->nsh', flat, swu)
        shared = jnp.einsum('nsh,shd->nd', sg * su, swd)
        return (routed + shared).reshape(b, t, d)
    x = L0_attn_a_x
    x = x + _L0_attn_a_ref(_layernorm(x, axis=-1), L0_attn_a_W_rvk, L0_attn_a_W_out, L0_attn_a_time_decay, L0_attn_a_time_first)
    x = x + _L0_ffn_ref(_layernorm(x, axis=-1), L0_ffn_router_w, L0_ffn_router_bias, L0_ffn_wg, L0_ffn_wu, L0_ffn_wd, L0_ffn_swg, L0_ffn_swu, L0_ffn_swd)
    x = x + _L0_attn_b_ref(_layernorm(x, axis=-1), L0_attn_b_wq, L0_attn_b_bq, L0_attn_b_wk, L0_attn_b_bk, L0_attn_b_wv, L0_attn_b_bv, L0_attn_b_wg, L0_attn_b_bg, L0_attn_b_wo, L0_attn_b_bo, L0_attn_b_gn_w, L0_attn_b_gn_b, L0_attn_b_gamma)
    x = x + _L0_ffn_ref(_layernorm(x, axis=-1), L0_ffn_router_w, L0_ffn_router_bias, L0_ffn_wg, L0_ffn_wu, L0_ffn_wd, L0_ffn_swg, L0_ffn_swu, L0_ffn_swd)
    return x

_drawn_inputs = setup_inputs


def setup_inputs(seed=0):
    import zlib

    import numpy as np

    out = dict(_drawn_inputs(seed))
    spreads = {'L0_attn_b_bq': (0.0, 0.1),
     'L0_attn_b_bk': (0.0, 0.1),
     'L0_attn_b_bv': (0.0, 0.1),
     'L0_attn_b_bg': (0.0, 0.1),
     'L0_attn_b_bo': (0.0, 0.1),
     'L0_attn_b_gn_w': (1.0, 0.2),
     'L0_attn_b_gn_b': (0.0, 0.1),
     'L0_ffn_router_bias': (0.0, 0.8)}
    factors = {'L0_attn_a_time_decay': 2.845,
     'L0_attn_a_time_first': 3.613,
     'L0_ffn_router_w': 8.0,
     'L0_ffn_wg': 8.0,
     'L0_ffn_wu': 8.0,
     'L0_ffn_wd': 8.0}
    for name, (base, spread) in spreads.items():
        noise = np.random.default_rng([zlib.crc32(name.encode()), seed]).standard_normal(out[name].shape)
        drawn = base * np.exp(spread * noise) if base else spread * noise
        out[name] = jnp.asarray(drawn.astype(out[name].dtype))
    for name, factor in factors.items():
        out[name] = (out[name] * factor).astype(out[name].dtype)
    return out
```

```python
from contextlib import ExitStack

import concourse.bass as bass
from concourse import mybir

P = 128
F32 = mybir.dt.float32
BF16 = mybir.dt.bfloat16
I32 = mybir.dt.int32
U32 = mybir.dt.uint32
ALU = mybir.AluOpType
ACT = mybir.ActivationFunctionType
AX_X = mybir.AxisListType.X
EPS = 1e-5


class Arena:

    def __init__(self, tensor, floats):
        self.tensor, self.floats, self.at = tensor, floats, 0

    def take(self, *shape, at=None):
        n = 1
        for s in shape:
            n *= s
        start = self.at if at is None else at
        assert start + n <= self.floats, (start, n, self.floats)
        if at is None:
            self.at += n
        piece = self.tensor[:, start:start + n]
        if len(shape) == 2:
            piece = piece.rearrange("p (a b) -> p a b", a=shape[0])
        if len(shape) == 3:
            piece = piece.rearrange("p (a b c) -> p a b c", a=shape[0], b=shape[1])
        if len(shape) == 4:
            piece = piece.rearrange("p (a b c d) -> p a b c d", a=shape[0], b=shape[1], c=shape[2])
        return piece


class Sems:

    def __init__(self, nc, ctx, phase):
        self.nc, self.phase, self.known = nc, phase, {}
        ctx.callback(self.release)

    def __call__(self, name):
        if name not in self.known:
            self.known[name] = self.nc.alloc_semaphore(name=f"{self.phase}_{name}")
        return self.known[name]

    def release(self):
        self.nc.clear_and_free_semaphores(list(self.known.values()))
        self.nc.all_engine_barrier()


class Chain:

    def __init__(self, engine, sem, per_turn=0, turn=0, before=0):
        self.engine, self.sem, self.n = engine, sem, 0
        self.base = per_turn * turn + before

    def step(self, instruction):
        self.n += 1
        instruction.then_inc(self.sem, 1)

    def settled(self):
        self.engine.wait_ge(self.sem, self.base + self.n)

    def link(self, instruction):
        self.step(instruction)
        self.settled()


def one_tile(ap, t):
    names = " ".join("abc"[:len(ap.shape) - 2])
    return ap[(slice(None), bass.ds(t, 1)) + (slice(None),) * (len(ap.shape) - 2)].rearrange(
        f"p o {names} -> p (o {names.split()[0]}) {' '.join(names.split()[1:])}")




def time_mix(nc, k, x, w_rvk, w_out, time_decay, time_first):
    B, T, C = x.shape
    TB = T // P
    CH = C // P
    N = 512
    H = T // N
    UNITS = H * CH
    arena = k.arena
    arena.at = 0
    wrvk = arena.take(CH, 3 * C)
    wout = arena.take(CH, C)
    decay = arena.take(CH)
    first = arena.take(CH)
    stats = arena.take(TB, 6)
    moments = arena.take(TB, 2)
    mean = arena.take(B * TB)
    rstd = arena.take(B * TB)
    xn = arena.take(TB, C)
    xnt = arena.take(CH, CH, N)
    o = arena.take(CH, T + 1)
    p = arena.take(CH, T + 1)
    q = arena.take(CH, T + 1)
    dif = arena.take(UNITS, N)
    neg = arena.take(UNITS, N)
    a2 = arena.take(UNITS, N)
    b2 = arena.take(UNITS, N)
    er = arena.take(UNITS, N)
    vs = arena.take(UNITS, N)
    num = arena.take(UNITS, N)
    bv2 = arena.take(CH, N)
    yt = arena.take(H, CH, N)

    xv = x.rearrange("b (t p) c -> b p t c", p=P)
    BLK = N // P
    assert H == 2 and CH == 2
    with ExitStack() as ctx:
        sem = Sems(nc, ctx, "mix")
        rkv = [[ctx.enter_context(nc.psum_tensor(f"mix_{g}{c}", [P, N], F32)) for g in "kvr"] for c in range(CH)]
        tp = ctx.enter_context(nc.psum_tensor("mix_tp", [P, N], F32))
        op = ctx.enter_context(nc.psum_tensor("mix_op", [P, 2, C], F32))
        block = ctx.enter_context(nc.Block())

        @block.sync
        def _(sp):
            k.zero_slots(sp)
            for b in range(B):
                sp.dma_start(k.res[:, b * TB:(b + 1) * TB, :], xv[b]).then_inc(sem(f"x{b}"), 16)
                if b == 0:
                    sp.dma_start(wrvk, w_rvk.rearrange("(h p) n -> p h n", p=P)).then_inc(sem("w"), 16)
                    sp.dma_start(wout, w_out.rearrange("(h p) n -> p h n", p=P)).then_inc(sem("w"), 16)

        @block.scalar
        def _(act):
            act.dma_start(decay, time_decay.rearrange("(h p) -> p h", p=P), allow_slow_non_contiguous=True)\
                .then_inc(sem("tm"), 16)
            act.dma_start(first, time_first.rearrange("(h p) -> p h", p=P), allow_slow_non_contiguous=True)\
                .then_inc(sem("tm"), 16)
            act.preload_act_table(ACT.Exp)
            act.sem_inc(sem("tp_read"), 1)
            act.sem_inc(sem("rkv_free"), CH)
            act.wait_ge(sem("tm"), 32)
            act.activation(decay, decay, ACT.Exp).then_inc(sem("exp_decay"), 1)

            def copy_transposes(b, h):
                for half in range(CH):
                    act.wait_ge(sem("tp_full"), UNITS * b + CH * h + half + 1)
                    act.activation(xnt[:, h, half, :], tp[:, :], ACT.Copy).then_inc(sem("tp_read"), 1)

            def exps(b, u):
                _, pv, pr = rkv[u % CH]
                act.wait_ge(sem("dif_ready"), UNITS * b + u + 1)
                act.activation(a2[:, u, :], a2[:, u, :], ACT.Exp)
                act.activation(b2[:, u, :], b2[:, u, :], ACT.Exp)
                act.activation(vs[:, u, :], pv[:, :], ACT.Copy).then_inc(sem("exp2"), 1)
                act.activation(neg[:, u, :], neg[:, u, :], ACT.Exp)
                act.activation(dif[:, u, :], dif[:, u, :], ACT.Exp).then_inc(sem("exp1"), 1)
                act.activation(er[:, u, :], pr[:, :], ACT.Exp, scale=-1.0).then_inc(sem("rkv_free"), 1)

            copy_transposes(0, 0)
            exps(0, 0)
            copy_transposes(0, 1)
            exps(0, 1)
            exps(0, 2)
            with act.Fori(1, B) as b:
                copy_transposes(b, 0)
                exps(b - 1, 3)
                exps(b, 0)
                copy_transposes(b, 1)
                exps(b, 1)
                exps(b, 2)
            exps(B - 1, 3)

        @block.tensor
        def _(pe):
            pe.wait_ge(k.const_ready, k.CONSTS)
            pe.wait_ge(sem("w"), 32)

            def transposes(b, h):
                for half in range(CH):
                    pe.wait_ge(sem("tp_read"), UNITS * b + CH * h + half + 1)
                    for j in range(BLK):
                        t = h * BLK + j
                        if half == 0:
                            pe.wait_ge(sem("xn_ready"), TB * b + t + 1)
                        last = pe.transpose(tp[:, j * P:(j + 1) * P], xn[:, t, half * P:(half + 1) * P], k.ident[:, :])
                    last.then_inc(sem("tp_full"), 1)

            def project(b, h):
                pe.wait_ge(sem("tp_read"), UNITS * b + CH * h + CH + 1)
                for c in range(CH):
                    pe.wait_ge(sem("rkv_free"), UNITS * b + CH * h + c + 1)
                    for g, bank in zip((2, 1, 0), rkv[c]):
                        at = g * C + c * P
                        for half in range(CH):
                            last = pe.matmul(bank[:, :], wrvk[:, half, at:at + P], xnt[:, h, half, :],
                                             start=half == 0, stop=half == CH - 1)
                    last.then_inc(sem("rkv_ready"), 1)

            def output(b, h):
                pe.wait_ge(sem("y_ready"), UNITS * b + CH * h + CH)
                for j in range(BLK):
                    if j % 2 == 0:
                        pe.wait_ge(sem("op_read"), TB // 2 * b + (h * BLK + j) // 2 + 1)
                    for half in range(CH):
                        last = pe.matmul(op[:, j % 2, :], yt[:, h, half, j * P:(j + 1) * P], wout[:, half, :],
                                         start=half == 0, stop=half == CH - 1)
                    if j % 2 == 1:
                        last.then_inc(sem("op_full"), 1)

            transposes(0, 0)
            project(0, 0)
            transposes(0, 1)
            project(0, 1)
            with pe.Fori(1, B) as b:
                transposes(b, 0)
                output(b - 1, 0)
                project(b, 0)
                transposes(b, 1)
                output(b - 1, 1)
                project(b, 1)
            output(B - 1, 0)
            output(B - 1, 1)

        @block.gpsimd
        def _(pool):
            k.make_constants(pool)
            pool.wait_ge(k.const_made, k.CONSTS)
            with pool.Fori(0, B) as b:
                pool.wait_ge(sem("var_ready"), b + 1)
                pool.tensor_tensor(rstd[:, bass.ds(b * TB, TB)], rstd[:, bass.ds(b * TB, TB)], k.minus_half[:, 0:TB],
                                   ALU.pow).then_inc(sem("rstd_ready"), 1)
            with pool.Fori(0, B) as b:
                for u in range(UNITS):
                    h, c = u // CH, u % CH
                    n = UNITS * b + u
                    before = slice(h * N, (h + 1) * N)
                    steps = Chain(pool, sem("pool_steps"), 5 * UNITS, b, 5 * u)
                    pool.wait_ge(sem("pq_ready"), n + 1)
                    pool.wait_ge(sem("exp1"), n + 1)
                    steps.step(pool.tensor_tensor(num[:, u, :], neg[:, u, :], p[:, c, before], ALU.mult))
                    steps.step(pool.tensor_tensor(vs[:, u, :], dif[:, u, :], vs[:, u, :], ALU.mult))
                    steps.step(pool.tensor_tensor(neg[:, u, :], neg[:, u, :], q[:, c, before], ALU.mult))
                    steps.settled()
                    steps.step(pool.tensor_tensor(num[:, u, :], num[:, u, :], vs[:, u, :], ALU.add))
                    steps.step(pool.tensor_tensor(neg[:, u, :], neg[:, u, :], dif[:, u, :], ALU.add))
                    steps.settled()
                    pool.sem_inc(sem("sums_ready"), 1)

        @block.vector
        def _(dve):
            dve.wait_ge(sem("exp_decay"), 1)
            dve.tensor_scalar(decay, decay, -1.0, None, ALU.mult).then_inc(sem("setup"), 1)
            for c in range(CH):
                dve.memset(o[:, c, 0:1], -1e38).then_inc(sem("setup"), 1)
                dve.memset(p[:, c, 0:1], 0.0).then_inc(sem("setup"), 1)
                dve.memset(q[:, c, 0:1], 0.0).then_inc(sem("setup"), 1)
            dve.wait_ge(sem("setup"), 1 + 3 * CH)
            dve.sem_inc(sem("op_read"), 1)

            def statistics(b):
                steps = Chain(dve, sem("stat_steps"), 2 * TB + 2, b)
                for t in range(TB):
                    steps.step(dve.bn_stats(stats[:, t, :], one_tile(k.res, b * TB + t)))
                steps.settled()
                dve.sem_inc(sem("stats_complete"), 1)
                for t in range(TB):
                    steps.step(dve.bn_aggr(moments[:, t, :], stats[:, t, :]))
                steps.settled()
                steps.step(dve.tensor_copy(mean[:, bass.ds(b * TB, TB)], moments[:, :, 0]))
                steps.step(dve.tensor_scalar(rstd[:, bass.ds(b * TB, TB)], moments[:, :, 1], EPS, None, ALU.add))
                steps.settled()
                dve.sem_inc(sem("var_ready"), 1)

            def normalise(b):
                dve.wait_ge(sem("rstd_ready"), b + 1)
                for t in range(TB):
                    dve.tensor_scalar(xn[:, t, :], one_tile(k.res, b * TB + t), mean[:, bass.ds(b * TB + t, 1)],
                                      rstd[:, bass.ds(b * TB + t, 1)], ALU.subtract, ALU.mult).then_inc(sem("xn_ready"), 1)

            def differences(b, u):
                h, c = u // CH, u % CH
                before, after = slice(h * N, (h + 1) * N), slice(h * N + 1, (h + 1) * N + 1)
                pk = rkv[c][0]
                steps = Chain(dve, sem("dif_steps"), 6 * UNITS, b, 6 * u)
                dve.wait_ge(sem("rkv_ready"), UNITS * b + u + 1)
                steps.link(dve.tensor_tensor_scan(o[:, c, after], decay[:, c:c + 1].to_broadcast([P, N]), pk[:, :],
                                                  o[:, c, h * N:h * N + 1], ALU.add, ALU.max))
                steps.step(dve.scalar_tensor_tensor(dif[:, u, :], pk[:, :], first[:, c:c + 1], o[:, c, before],
                                                    ALU.add, ALU.subtract))
                steps.step(dve.scalar_tensor_tensor(a2[:, u, :], o[:, c, before], decay[:, c:c + 1], o[:, c, after],
                                                    ALU.add, ALU.subtract))
                steps.step(dve.tensor_tensor(b2[:, u, :], pk[:, :], o[:, c, after], ALU.subtract))
                steps.settled()
                steps.step(dve.tensor_scalar(neg[:, u, :], dif[:, u, :], -1.0, 0.0, ALU.mult, ALU.min))
                steps.settled()
                steps.link(dve.tensor_scalar(dif[:, u, :], dif[:, u, :], 0.0, None, ALU.min))
                dve.sem_inc(sem("dif_ready"), 1)

            def states(b, u):
                h, c = u // CH, u % CH
                after, start = slice(h * N + 1, (h + 1) * N + 1), slice(h * N, h * N + 1)
                steps = Chain(dve, sem("state_steps"), 3 * UNITS, b, 3 * u)
                dve.wait_ge(sem("exp2"), UNITS * b + u + 1)
                steps.link(dve.tensor_tensor(bv2[:, c, :], b2[:, u, :], vs[:, u, :], ALU.mult))
                steps.step(dve.tensor_tensor_scan(p[:, c, after], a2[:, u, :], bv2[:, c, :], p[:, c, start],
                                                  ALU.mult, ALU.add))
                steps.step(dve.tensor_tensor_scan(q[:, c, after], a2[:, u, :], b2[:, u, :], q[:, c, start],
                                                  ALU.mult, ALU.add))
                steps.settled()
                dve.sem_inc(sem("pq_ready"), 1)

            def outputs(b, u):
                h, c = u // CH, u % CH
                steps = Chain(dve, sem("y_steps"), 3 * UNITS, b, 3 * u)
                dve.wait_ge(sem("sums_ready"), UNITS * b + u + 1)
                dve.wait_ge(sem("rkv_free"), CH + UNITS * b + u + 1)
                steps.link(dve.scalar_tensor_tensor(neg[:, u, :], er[:, u, :], 1.0, neg[:, u, :], ALU.add, ALU.mult))
                steps.link(dve.reciprocal(neg[:, u, :], neg[:, u, :]))
                steps.link(dve.tensor_tensor(yt[:, h, c, :], num[:, u, :], neg[:, u, :], ALU.mult))
                dve.sem_inc(sem("y_ready"), 1)

            def add_output(b, h):
                for j in range(BLK // 2):
                    pair = b * (TB // 2) + h * (BLK // 2) + j
                    dve.wait_ge(sem("op_full"), pair + 1)
                    tiles = k.res[:, bass.ds(2 * pair, 2), :]
                    dve.tensor_tensor(tiles, tiles, op[:, :, :], ALU.add).then_inc(sem("op_read"), 1)

            def batch(b, is_first=False, is_last=False):
                differences(b, 0)
                differences(b, 1)
                states(b, 0)
                if not is_first:
                    add_output(b - 1, 1)
                states(b, 1)
                differences(b, 2)
                outputs(b, 0)
                differences(b, 3)
                outputs(b, 1)
                if not is_last:
                    normalise(b + 1)
                states(b, 2)
                add_output(b, 0)
                states(b, 3)
                outputs(b, 2)
                outputs(b, 3)

            dve.wait_ge(sem("x0"), 16)
            statistics(0)
            normalise(0)
            for b in range(1, B):
                dve.wait_ge(sem(f"x{b}"), 16)
            with dve.Fori(1, B) as b:
                statistics(b)
            batch(0, is_first=True)
            with dve.Fori(1, B - 1) as b:
                batch(b)
            batch(B - 1, is_last=True)
            add_output(B - 1, 1)
            dve.wait_ge(sem("op_read"), 1 + B * TB // 2)




class Slots:

    def __init__(self, nc, tokens, width, experts, choices):
        self.tiles = tokens * choices // P + experts
        self.x = nc.dram_tensor("slots_x", (self.tiles * P, width), F32, kind="Internal").ap()
        self.y = nc.dram_tensor("slots_y", (self.tiles * P, width), F32, kind="Internal").ap()
        self.expert = nc.dram_tensor("slots_expert", (self.tiles,), I32, kind="Internal").ap()


def experts(nc, k, phase, router_w, router_bias, w_gu, w_d, sw_gu, sw_d, out=None):
    NT, D = k.res.shape[1], k.res.shape[2]
    E = router_w.shape[1]
    F = w_d.shape[1]
    K = 4
    KH = D // P
    BLK = 4
    N = BLK * P
    NB = NT // BLK
    SH = sw_d.shape[0] // P
    NX = k.slots.tiles
    slots = k.slots
    arena = k.arena
    arena.at = 0
    xn = arena.take(NT, D)
    xnt = arena.take(KH, NT * P)
    wd = arena.take(E, D, at=0)
    assert NT * D + KH * NT * P >= E * D
    big = arena.at
    wgu = arena.take(KH, E, 2 * F)
    after_big = arena.at
    arena.at = big
    hot = [arena.take(NT * E // 2).bitcast(BF16).rearrange("p (t e) -> p t e", e=E) for _ in range(K)]
    chosen = arena.take(NT * E // 2).bitcast(BF16)
    count = arena.take(E, NT)
    before = arena.take(E, NT)
    restart = arena.take(E, NT)
    pos = arena.take(NT, E)
    picked = arena.take(NT, E)
    assert arena.at <= after_big
    arena.at = after_big
    small = arena.at
    slot = arena.take(NT, K).bitcast(I32)
    gate = arena.take(NT, K)
    expert_row = arena.take(NX).bitcast(I32)
    logit = arena.take(NT, E)
    choice = arena.take(NT, 8)
    sgu = arena.take(KH, 2 * SH * P)
    sd = arena.take(SH, D)
    rw = arena.take(KH, E)
    bias = arena.take(BLK, E)
    at_work = arena.at
    stats = arena.take(BLK, 6)
    moments = arena.take(BLK, 2)
    rstd = arena.take(BLK)
    xs = arena.take(BLK, D)
    xst = arena.take(KH, N)
    biased = arena.take(BLK, E)
    best = arena.take(BLK, 8)
    which = arena.take(BLK, 8).bitcast(U32)
    arena.at = at_work
    total = arena.take(E)
    tiles_f = arena.take(E)
    tiles_i = arena.take(E).bitcast(I32)
    ends = arena.take(E)
    base = arena.take(E)
    row_max = arena.take(NT)
    gate_sum = arena.take(NT)
    slot_f = arena.take(NT)
    tile_no = arena.take(2)
    tile_expert = arena.take(2)
    tile_expert_i = arena.take(2).bitcast(I32)
    passed = arena.take(2, E)
    sg = arena.take(2, N)
    sht = arena.take(SH, N)
    arena.at = at_work
    xin = arena.take(4, D)
    xt = arena.take(2, KH, P)
    sig = arena.take(2, F)
    hid = arena.take(2, P)
    ht = arena.take(2, P)
    ytile = arena.take(4, D)
    arena.at = at_work
    G = 8
    gathered = arena.take(G, D)

    with ExitStack() as ctx:
        sem = Sems(nc, ctx, phase + "_route")
        tp = [ctx.enter_context(nc.psum_tensor(f"{phase}_tp{h}", [P, N], F32)) for h in range(KH)]
        lg = ctx.enter_context(nc.psum_tensor(f"{phase}_lg", [P, BLK, E], F32))
        block = ctx.enter_context(nc.Block())

        @block.sync
        def _(sp):
            sp.dma_start(rw, router_w.rearrange("(h p) n -> p h n", p=P)).then_inc(sem("rw"), 16)
            for j in range(BLK):
                sp.dma_start(bias[:, j, :], router_bias.rearrange("(o e) -> o e", o=1).to_broadcast([P, E]))\
                    .then_inc(sem("rw"), 16)
            sp.dma_start(sgu, sw_gu.rearrange("(h p) n -> p h n", p=P)).then_inc(sem("shared_w"), 16)
            sp.dma_start(sd, sw_d.rearrange("(j p) n -> p j n", p=P)).then_inc(sem("shared_w"), 16)
            sp.wait_ge(sem("shared_w"), 32)

        @block.tensor
        def _(pe):
            pe.wait_ge(sem("rw"), 16 * (1 + BLK))
            with pe.Fori(0, NB) as n:
                for h in range(KH):
                    pe.wait_ge(sem("tp_read"), KH * n + h + 1)
                    for j in range(BLK):
                        if h == 0:
                            pe.wait_ge(sem("xs_ready"), BLK * n + j + 1)
                        last = pe.transpose(tp[h][:, j * P:(j + 1) * P], xs[:, j, h * P:(h + 1) * P], k.ident[:, :])
                    last.then_inc(sem("tp_full"), 1)
                pe.wait_ge(sem("xst_ready"), KH * n + KH)
                pe.wait_ge(sem("lg_read"), n + 1)
                for j in range(BLK):
                    for h in range(KH):
                        last = pe.matmul(lg[:, j, :], xst[:, h, j * P:(j + 1) * P], rw[:, h, :],
                                         start=h == 0, stop=h == KH - 1)
                last.then_inc(sem("lg_full"), 1)

        @block.scalar
        def _(act):
            act.sem_inc(sem("tp_read"), KH)
            with act.Fori(0, NB) as n:
                for h in range(KH):
                    act.wait_ge(sem("tp_full"), KH * n + h + 1)
                    act.wait_ge(sem("xst_free"), n + 1)
                    act.activation(xst[:, h, :], tp[h][:, :], ACT.Copy).then_inc(sem("xst_ready"), 1)
                    act.activation(xnt[:, h, bass.ds(N * n, N)], tp[h][:, :], ACT.Copy).then_inc(sem("tp_read"), 1)
                act.activation(xn[:, bass.ds(BLK * n, BLK), :], xs[:, :, :], ACT.Copy).then_inc(sem("xn_kept"), 1)

        @block.gpsimd
        def _(pool):
            with pool.Fori(0, NB) as n:
                pool.wait_ge(sem("var_ready"), n + 1)
                pool.tensor_tensor(rstd, rstd, k.minus_half[:, 0:BLK], ALU.pow).then_inc(sem("rstd_ready"), 1)

        @block.vector
        def _(dve):
            dve.sem_inc(sem("lg_read"), 1)
            dve.sem_inc(sem("xst_free"), 1)

            def normalise(n):
                steps = Chain(dve, sem("ln_steps"), 2 * BLK + 1, n)
                for j in range(BLK):
                    steps.step(dve.bn_stats(stats[:, j, :], one_tile(k.res, BLK * n + j)))
                steps.settled()
                dve.sem_inc(sem("stats_complete"), 1)
                for j in range(BLK):
                    steps.step(dve.bn_aggr(moments[:, j, :], stats[:, j, :]))
                steps.settled()
                steps.step(dve.tensor_scalar(rstd, moments[:, :, 1], EPS, None, ALU.add))
                steps.settled()
                dve.sem_inc(sem("var_ready"), 1)
                dve.wait_ge(sem("rstd_ready"), n + 1)
                dve.wait_ge(sem("xs_free"), n + 1)
                for j in range(BLK):
                    dve.tensor_scalar(xs[:, j, :], one_tile(k.res, BLK * n + j), moments[:, j, 0:1], rstd[:, j:j + 1],
                                      ALU.subtract, ALU.mult).then_inc(sem("xs_ready"), 1)

            def choose(n):
                steps = Chain(dve, sem("top_steps"), 2 * BLK + 3, n)
                dve.wait_ge(sem("lg_full"), n + 1)
                steps.step(dve.tensor_tensor(biased, lg[:, :, :], bias, ALU.add))
                steps.step(dve.tensor_copy(logit[:, bass.ds(BLK * n, BLK), :], lg[:, :, :]))
                steps.settled()
                dve.sem_inc(sem("lg_read"), 1)
                dve.sem_inc(sem("xst_free"), 1)
                for j in range(BLK):
                    steps.step(dve.max(best[:, j, :], biased[:, j, :]))
                steps.settled()
                dve.sem_inc(sem("best_complete"), 1)
                for j in range(BLK):
                    steps.step(dve.max_index(which[:, j, :], best[:, j, :], biased[:, j, :]))
                steps.settled()
                dve.sem_inc(sem("which_complete"), 1)
                steps.step(dve.tensor_copy(choice[:, bass.ds(BLK * n, BLK), :], which))

            dve.sem_inc(sem("xs_free"), 1)
            normalise(0)
            with dve.Fori(0, NB - 1) as n:
                dve.wait_ge(sem("tp_full"), KH * n + KH)
                dve.wait_ge(sem("xn_kept"), n + 1)
                dve.sem_inc(sem("xs_free"), 1)
                normalise(n + 1)
                choose(n)
            choose(NB - 1)
            dve.wait_ge(sem("top_steps"), NB * (2 * BLK + 3))

    with ExitStack() as ctx:
        sem = Sems(nc, ctx, phase + "_disp")
        ps = [ctx.enter_context(nc.psum_tensor(f"{phase}_d{i}", [P, N], F32)) for i in range(8)]
        rank_ps, count_ps = ps[0:2], ps[2:4]
        gate_ps, up_ps = ps[0:2], ps[2:4]
        down_ps = [x[:, :].rearrange("p (j d) -> p j d", d=D) for x in ps[4:6]]
        QUARTERS = NT * E // N
        TQ = NT // QUARTERS
        block = ctx.enter_context(nc.Block())

        @block.tensor
        def _(pe):
            pe.wait_ge(sem("chosen"), 1)
            for g in range(QUARTERS):
                if g >= 2:
                    pe.wait_ge(sem("counts_read"), g - 1)
                pe.matmul(rank_ps[g % 2][:, :], k.tri_bf[:, :], chosen[:, g * N:(g + 1) * N], start=True, stop=True)
                pe.matmul(count_ps[g % 2][:, :], k.ones_bf[:, :], chosen[:, g * N:(g + 1) * N], start=True, stop=True)\
                    .then_inc(sem("counted"), 1)
            pe.wait_ge(sem("counts_read"), QUARTERS)
            with pe.Fori(0, NB) as n:
                for j in range(SH):
                    pe.wait_ge(sem("sht_ready"), SH * n + j + 1)
                    for bank, at in ((gate_ps[j % 2], j * P), (up_ps[j % 2], (SH + j) * P)):
                        for h in range(KH):
                            last = pe.matmul(bank[:, :], sgu[:, h, at:at + P], xnt[:, h, bass.ds(N * n, N)],
                                             start=h == 0, stop=h == KH - 1)
                    last.then_inc(sem("gu_full"), 1)
                pe.wait_ge(sem("sht_ready"), 2 + SH * n + SH)
                for j in range(BLK):
                    if j % 2 == 0:
                        pe.wait_ge(sem("down_read"), 2 * n + j // 2 + 1)
                    for m in range(SH):
                        last = pe.matmul(down_ps[j // 2][:, j % 2, :], sht[:, m, j * P:(j + 1) * P], sd[:, m, :],
                                         start=m == 0, stop=m == SH - 1)
                    if j % 2 == 1:
                        last.then_inc(sem("down_full"), 1)

        @block.scalar
        def _(act):
            act.wait_ge(sem("shifted"), 1)
            act.activation(logit, logit, ACT.Exp).then_inc(sem("exp"), 1)
            act.preload_act_table(ACT.Silu)
            act.sem_inc(sem("sg_free"), 2)
            with act.Fori(0, NB) as n:
                for j in range(SH):
                    act.wait_ge(sem("gu_full"), SH * n + j + 1)
                    act.wait_ge(sem("sht_ready"), SH * n + j + 1)
                    act.activation(sg[:, j % 2, :], gate_ps[j % 2][:, :], ACT.Silu).then_inc(sem("sg_ready"), 1)

        @block.vector
        def _(dve):
            c = Chain(dve, sem("steps"))
            c.step(dve.memset(restart, 1.0))
            for i in range(K):
                c.step(dve.tensor_tensor(hot[i], k.iota64[:, 0:E].unsqueeze(1).to_broadcast([P, NT, E]),
                                         choice[:, :, i:i + 1].to_broadcast([P, NT, E]), ALU.is_equal))
            c.settled()
            c.step(dve.memset(restart[:, :, 0:1], 0.0))
            flat = [x.rearrange("p t e -> p (t e)") for x in hot]
            both = before.rearrange("p e t -> p (e t)")[:, 0:NT * E // 2].bitcast(BF16)
            c.step(dve.tensor_tensor(chosen, flat[0], flat[1], ALU.add))
            c.step(dve.tensor_tensor(both, flat[2], flat[3], ALU.add))
            c.settled()
            c.link(dve.tensor_tensor(chosen, chosen, both, ALU.add))
            dve.sem_inc(sem("chosen"), 1)
            c.link(dve.tensor_reduce(row_max, logit, AX_X, ALU.max))
            c.link(dve.tensor_tensor(logit, logit, row_max.unsqueeze(2).to_broadcast([P, NT, E]), ALU.subtract))
            dve.sem_inc(sem("shifted"), 1)
            for g in range(QUARTERS):
                dve.wait_ge(sem("counted"), g + 1)
                tiles = slice(g * TQ, (g + 1) * TQ)
                c.step(dve.tensor_copy(pos[:, tiles, :], rank_ps[g % 2][:, :].rearrange("p (t e) -> p t e", e=E)))
                c.step(dve.tensor_copy(count[:, :, tiles], count_ps[g % 2][:, :].rearrange("p (t e) -> p e t", e=E)))
                c.settled()
                dve.sem_inc(sem("counts_read"), 1)
            c.link(dve.tensor_tensor_scan(before.rearrange("p e t -> p (e t)"), restart.rearrange("p e t -> p (e t)"),
                                          count.rearrange("p e t -> p (e t)"), 0.0, ALU.mult, ALU.add))
            c.link(dve.tensor_scalar(tiles_i, before[:, :, NT - 1], float(P - 1), None, ALU.add))
            c.link(dve.tensor_scalar(tiles_i, tiles_i, P.bit_length() - 1, None, ALU.logical_shift_right))
            c.link(dve.tensor_copy(tiles_f, tiles_i))
            c.link(dve.tensor_tensor_scan(ends, restart[:, 0, 1:2].to_broadcast([P, E]), tiles_f, 0.0,
                                          ALU.mult, ALU.add))
            c.link(dve.tensor_tensor(base, ends, tiles_f, ALU.subtract))
            c.link(dve.tensor_scalar(base, base, float(P), None, ALU.mult))
            c.link(dve.tensor_tensor(before, before, count, ALU.subtract))
            c.link(dve.tensor_tensor(before, before, base.unsqueeze(2).to_broadcast([P, E, NT]), ALU.add))
            c.link(dve.tensor_tensor(pos, pos, before.rearrange("p e t -> p t e"), ALU.add))
            for i in range(K):
                c.link(dve.tensor_tensor(picked, hot[i], pos, ALU.mult))
                c.link(dve.tensor_reduce(slot_f, picked, AX_X, ALU.add))
                c.link(dve.tensor_copy(slot[:, :, i], slot_f))
                dve.sem_inc(sem("slots_ready"), 1)
            dve.wait_ge(sem("tile_no"), 1)
            HALF = NX // 2
            c.link(dve.tensor_tensor(passed[0:HALF], tile_no[0:HALF].unsqueeze(2).to_broadcast([HALF, 2, E]),
                                     ends[0:HALF].unsqueeze(1).to_broadcast([HALF, 2, E]), ALU.is_ge))
            c.link(dve.tensor_reduce(tile_expert[0:HALF], passed[0:HALF], AX_X, ALU.add))
            c.link(dve.tensor_scalar(tile_expert_i[0:HALF], tile_expert[0:HALF], float(E - 1), None, ALU.min))
            dve.sem_inc(sem("tile_expert"), 1)
            dve.wait_ge(sem("exp"), 1)
            for i in range(K):
                c.link(dve.tensor_tensor(picked, hot[i], logit, ALU.mult))
                c.link(dve.tensor_reduce(gate[:, :, i], picked, AX_X, ALU.add))
            c.link(dve.tensor_reduce(gate_sum, gate, AX_X, ALU.add))
            c.link(dve.reciprocal(gate_sum, gate_sum))
            c.link(dve.tensor_tensor(gate, gate, gate_sum.unsqueeze(2).to_broadcast([P, NT, K]), ALU.mult))
            dve.sem_inc(sem("dispatched"), 1)

            dve.sem_inc(sem("sht_ready"), 2)
            dve.sem_inc(sem("down_read"), 2)
            with dve.Fori(0, NB) as n:
                for j in range(SH):
                    dve.wait_ge(sem("sg_ready"), SH * n + j + 1)
                    dve.tensor_tensor(sht[:, j, :], sg[:, j % 2, :], up_ps[j % 2][:, :], ALU.mult)\
                        .then_inc(sem("sht_ready"), 1)
                for j in range(2):
                    dve.wait_ge(sem("down_full"), 2 * n + j + 1)
                    tiles = k.res[:, bass.ds(BLK * n + 2 * j, 2), :]
                    dve.tensor_tensor(tiles, tiles, down_ps[j], ALU.add).then_inc(sem("down_read"), 1)
            dve.wait_ge(sem("down_read"), 2 + 2 * NB)

        @block.sync
        def _(sp):
            sp.wait_ge(sem("tile_expert"), 1)
            sp.dma_start(slots.expert.rearrange("(p j) -> p j", j=2), tile_expert_i[0:NX // 2])\
                .then_inc(sem("expert_out"), 16)
            sp.wait_ge(sem("expert_out"), 16)
            sp.dma_start(expert_row[0:1], slots.expert.rearrange("(o n) -> o n", o=1)).then_inc(sem("expert_in"), 16)
            sp.wait_ge(sem("dispatched"), 1)
            sp.dma_start(wgu, w_gu.rearrange("(h p) e n -> p h e n", p=P)).then_inc(sem("wgu"), 16)
            sp.wait_ge(sem("expert_in"), 16)
            sp.wait_ge(sem("wgu"), 16)

        @block.gpsimd
        def _(pool):
            pool.iota(tile_no[0:NX // 2], [[1, 2]], base=0, channel_multiplier=2,
                      allow_small_or_imprecise_dtypes=True).then_inc(sem("tile_no_made"), 1)
            pool.wait_ge(sem("tile_no_made"), 1)
            pool.sem_inc(sem("tile_no"), 1)
            pool.wait_ge(k.slots_zeroed, k.ZEROINGS * 16)
            for i in range(K):
                pool.wait_ge(sem("slots_ready"), i + 1)
                for t in range(NT):
                    pool.indirect_dma_start(out=slots.x, out_offset=bass.IndirectOffsetOnAxis(ap=slot[:, t, i:i + 1], axis=0),
                                            in_=xn[:, t, :], in_offset=None).then_inc(sem("scattered"), 16)
            pool.wait_ge(sem("scattered"), 16 * K * NT)

    with ExitStack() as ctx:
        sem = Sems(nc, ctx, phase + "_exp")
        xt_ps, h_ps, ht_ps, y_ps = [[ctx.enter_context(nc.psum_tensor(f"{phase}_{g}{i}", [P, 512], F32))
                                     for i in range(2)] for g in ("ext", "eh", "eht", "ey")]
        x_v = slots.x.rearrange("(t p) d -> t p d", p=P)
        y_v = slots.y.rearrange("(t p) d -> t p d", p=P)
        RING = 4
        PEEL = 2
        block = ctx.enter_context(nc.Block())
        LAG = 3

        def all_steps(engine, step, lag):
            for s in range(PEEL * RING):
                step(s // RING, s % RING, s)
            with engine.Fori(PEEL, NX // RING) as g:
                for r in range(RING):
                    step(g, r, None)
            for s in range(NX, NX + lag):
                step(s // RING, s % RING, s)

        def tile_of(g, r, s, back):
            if s is not None and not 0 <= s - back < NX:
                return None
            turn = g if r >= back % RING else g - 1
            turn = turn - back // RING
            place = (r - back) % RING
            return RING * turn + place, turn, place

        @block.sync
        def _(sp):
            sp.dma_start(wd[0:F], w_d.rearrange("e f d -> f e d")).then_inc(sem("wd"), 16)

            def step(g, r, s):
                now = tile_of(g, r, s, 0)
                if now is not None:
                    i, _, place = now
                    if s is None or s >= RING:
                        sp.wait_ge(sem("xt_full"), i + 1 - RING)
                    sp.dma_start(xin[:, place, :], x_v[bass.ds(i, 1)].rearrange("o p d -> (o p) d"))\
                        .then_inc(sem(f"x_in{place}"), 16)
                old = tile_of(g, r, s, 2 * RING)
                if old is not None:
                    i, _, place = old
                    sp.wait_ge(sem("y_read"), 2 + i + 1)
                    sp.dma_start(y_v[bass.ds(i, 1)].rearrange("o p d -> (o p) d"), ytile[:, place, :])\
                        .then_inc(sem(f"y_out{place}"), 16)

            all_steps(sp, step, 2 * RING)
            for place in range(RING):
                sp.wait_ge(sem(f"y_out{place}"), 16 * NX // RING)

        @block.tensor
        def _(pe):
            pe.wait_ge(sem("wd"), 16)

            def step(g, r, s):
                tile = tile_of(g, r, s, 0)
                if tile is not None:
                    i, turn, place = tile
                    pe.wait_ge(sem(f"x_in{place}"), 16 * turn + 16)
                    pe.wait_ge(sem("xt_read"), i + 1)
                    for h in range(KH):
                        last = pe.transpose(xt_ps[place % 2][:, h * P:(h + 1) * P], xin[:, place, h * P:(h + 1) * P],
                                            k.ident[:, :])
                    last.then_inc(sem("xt_full"), 1)
                tile = tile_of(g, r, s, 1)
                if tile is not None:
                    i, turn, place = tile
                    expert = pe.value_load(expert_row[0:1, bass.ds(i, 1)], min_val=0, max_val=E - 1)
                    pe.wait_ge(sem("xt_read"), 2 + i + 1)
                    pe.wait_ge(sem("hid_ready"), i + 1)
                    for h in range(KH):
                        last = pe.matmul(h_ps[place % 2][:, 0:2 * F], xt[:, place % 2, h, :],
                                         wgu[:, h].rearrange("p e n -> p (e n)")[:, bass.ds(expert * (2 * F), 2 * F)],
                                         start=h == 0, stop=h == KH - 1)
                    last.then_inc(sem("h_full"), 1)
                tile = tile_of(g, r, s, 2)
                if tile is not None:
                    i, turn, place = tile
                    pe.wait_ge(sem("hid_ready"), 2 + i + 1)
                    pe.wait_ge(sem("ht_read"), i + 1)
                    pe.transpose(ht_ps[place % 2][:, 0:P], hid[:, place % 2, :], k.ident[:, :])\
                        .then_inc(sem("ht_full"), 1)
                tile = tile_of(g, r, s, 3)
                if tile is not None:
                    i, turn, place = tile
                    expert = pe.value_load(expert_row[0:1, bass.ds(i, 1)], min_val=0, max_val=E - 1)
                    pe.wait_ge(sem("ht_read"), 2 + i + 1)
                    pe.wait_ge(sem("y_read"), i + 1)
                    pe.matmul(y_ps[place % 2][:, 0:D], ht[0:F, place % 2, :],
                              wd[0:F].rearrange("f e d -> f (e d)")[:, bass.ds(expert * D, D)], start=True, stop=True)\
                        .then_inc(sem("y_full"), 1)

            all_steps(pe, step, LAG)

        @block.scalar
        def _(act):
            act.preload_act_table(ACT.Silu)
            act.sem_inc(sem("xt_read"), 2)
            act.sem_inc(sem("ht_read"), 2)

            def step(g, r, s):
                tile = tile_of(g, r, s, 0)
                if tile is not None:
                    i, turn, place = tile
                    act.wait_ge(sem("xt_full"), i + 1)
                    if s is None or s >= 2:
                        act.wait_ge(sem("h_full"), i - 1)
                    act.activation(xt[:, place % 2].rearrange("p h n -> p (h n)"), xt_ps[place % 2][:, 0:D], ACT.Copy)\
                        .then_inc(sem("xt_read"), 1)
                tile = tile_of(g, r, s, 1)
                if tile is not None:
                    i, turn, place = tile
                    act.wait_ge(sem("h_full"), i + 1)
                    act.wait_ge(sem("hid_ready"), i + 1)
                    act.activation(sig[:, place % 2, :], h_ps[place % 2][:, 0:F], ACT.Silu).then_inc(sem("sig_ready"), 1)
                tile = tile_of(g, r, s, 2)
                if tile is not None:
                    i, turn, place = tile
                    act.wait_ge(sem("ht_full"), i + 1)
                    if s is None or s >= 4:
                        act.wait_ge(sem("y_full"), i - 1)
                    act.activation(ht[0:F, place % 2, :], ht_ps[place % 2][0:F, 0:P], ACT.Copy)\
                        .then_inc(sem("ht_read"), 1)

            all_steps(act, step, 2)

        @block.vector
        def _(dve):
            dve.memset(hid, 0.0).then_inc(sem("hid_cleared"), 1)
            dve.wait_ge(sem("hid_cleared"), 1)
            dve.sem_inc(sem("hid_ready"), 2)
            dve.sem_inc(sem("y_read"), 2)

            def step(g, r, s):
                tile = tile_of(g, r, s, 1)
                if tile is not None:
                    i, turn, place = tile
                    dve.wait_ge(sem("sig_ready"), i + 1)
                    if s is None or s >= 3:
                        dve.wait_ge(sem("ht_full"), i - 1)
                    dve.tensor_tensor(hid[:, place % 2, 0:F], sig[:, place % 2, :], h_ps[place % 2][:, F:2 * F],
                                      ALU.mult).then_inc(sem("hid_ready"), 1)
                tile = tile_of(g, r, s, 3)
                if tile is not None:
                    i, turn, place = tile
                    dve.wait_ge(sem("y_full"), i + 1)
                    if s is None or s >= RING + 3:
                        dve.wait_ge(sem(f"y_out{place}"), 16 * turn)
                    dve.tensor_copy(ytile[:, place, :], y_ps[place % 2][:, 0:D]).then_inc(sem("y_read"), 1)

            all_steps(dve, step, LAG)

    with ExitStack() as ctx:
        sem = Sems(nc, ctx, phase + "_sum")
        block = ctx.enter_context(nc.Block())
        TPG = G // K

        @block.gpsimd
        def _(pool):
            for t in range(NT):
                for i in range(K):
                    n = K * t + i
                    if n >= G:
                        pool.wait_ge(sem("added"), n - G + 1)
                    pool.indirect_dma_start(out=gathered[:, n % G, :], out_offset=None, in_=slots.y,
                                            in_offset=bass.IndirectOffsetOnAxis(ap=slot[:, t, i:i + 1], axis=0))\
                        .then_inc(sem(f"in{n % G}"), 16)

        @block.vector
        def _(dve):
            with dve.Fori(0, NT // TPG) as g:
                for r in range(TPG):
                    t = TPG * g + r
                    for i in range(K):
                        n = K * r + i
                        dve.wait_ge(sem(f"in{n}"), 16 * g + 16)
                        if i:
                            dve.wait_ge(sem("added"), G * g + n)
                        dve.scalar_tensor_tensor(one_tile(k.res, t), gathered[:, n, :],
                                                 gate[:, bass.ds(t, 1), i:i + 1].rearrange("p o i -> p (o i)"),
                                                 one_tile(k.res, t), ALU.mult, ALU.add).then_inc(sem("added"), 1)

        @block.sync
        def _(sp):
            if out is not None:
                OUTS = 4
                view = out.rearrange("b (t p) c -> p (b t) c", p=P)
                for g in range(OUTS):
                    tiles = slice(g * NT // OUTS, (g + 1) * NT // OUTS)
                    sp.wait_ge(sem("added"), K * NT * (g + 1) // OUTS)
                    sp.dma_start(view[:, tiles, :], k.res[:, tiles, :]).then_inc(sem("stored"), 16)
                sp.wait_ge(sem("stored"), 16 * OUTS)




def retention(nc, k, w_qk, w_vg, w_o, b_q, b_k, b_vg, b_o, gn_w, gn_b, gamma, batches):
    B = batches
    NT, D = k.res.shape[1], k.res.shape[2]
    TB = NT // B
    HEADS = gamma.shape[0]
    DH = D // HEADS
    CH = D // P
    HC = HEADS // CH
    GR = 4
    BLK = 4
    N = BLK * P
    H = TB // BLK
    COUNT = float(TB * P * DH)
    assert DH * 2 * GR == P and H == 2 and CH == 2

    arena = k.arena
    arena.at = 0
    wqk = arena.take(CH, 2 * D)
    wvg = arena.take(CH, 2 * D)
    wo = arena.take(CH, D)
    bias_qk = arena.take(2, CH)
    bias_vg = arena.take(2 * D)
    bias_o = arena.take(D)
    gnw = arena.take(D)
    gnb = arena.take(D)
    decay = arena.take(GR, CH, 2, P)
    q_decay = arena.take(CH, P)
    powers = arena.take(2 * P + 1)
    parity = arena.take(2)
    row_i = arena.take(1).bitcast(I32)
    blocks = arena.take(P)
    stats = arena.take(BLK, 6)
    moments = arena.take(BLK, 2)
    rstd = arena.take(BLK)
    xn = arena.take(TB, D)
    xnt = arena.take(H, CH, N)
    qt = arena.take(CH, TB * P)
    qst = arena.take(CH, TB * P)
    kt = arena.take(CH, TB * P)
    ktp = arena.take(2, CH, TB * P)
    vg = arena.take(TB, 2 * D)
    gates = arena.take(NT, D)
    kd = arena.take(2, D)
    masked_at = arena.at
    masked = arena.take(2, GR, 4 * P)
    turned = arena.take(GR, CH, 2, P, at=masked_at)
    reverse = arena.take(P, at=masked_at + GR * 4 * P)
    state = arena.take(2, CH, P)
    update = arena.take(CH, P)
    ret = arena.take(TB, D)
    square = arena.take(TB, D, at=masked_at)
    sums = arena.take(HEADS)
    group_scale = arena.take(HEADS)
    scale = arena.take(D)
    rnt = arena.take(2, 2, CH, P)
    powers_dram = nc.dram_tensor("gamma_powers", (HEADS, 2 * P + 1), F32, kind="Internal").ap()

    with ExitStack() as ctx:
        sem = Sems(nc, ctx, "ret")

        def bank(name):
            return ctx.enter_context(nc.psum_tensor(f"ret_{name}", [P, N], F32))

        tp, rt = bank("tp"), bank("rt")
        pj = [bank(f"pj{i}") for i in range(2)]
        sc = [bank(f"sc{g}") for g in range(GR)]

        TP_CHUNKS, TP_TURN = 2 * TB - 1, 2 * TB - 1 + 2 * H + TB // 2

        def tp_chunks(b):
            return 2 * H + TP_TURN * b

        def tp_project(b, first):
            return 0 if first else 2 * H + TP_TURN * (b - 1) + TP_CHUNKS

        def tp_output(b, last):
            return 2 * H + TP_TURN * b + TP_CHUNKS + (0 if last else 2 * H)

        PJ_TURN = H * (2 * CH + BLK)
        RT_TURN = TB + 2 + TB // 2
        block = ctx.enter_context(nc.Block())

        @block.sync
        def _(sp):
            def rows(dst, src, width):
                sp.dma_start(dst, src.rearrange("(o n) -> o n", o=1).to_broadcast([P, width])).then_inc(sem("w"), 16)

            sp.dma_start(powers[0:HEADS, P + 1:P + 2], gamma.rearrange("(h o) -> h o", o=1),
                         allow_slow_non_contiguous=True).then_inc(sem("gamma"), 16)
            sp.dma_start(wqk, w_qk.rearrange("(h p) n -> p h n", p=P)).then_inc(sem("w"), 16)
            sp.dma_start(wvg, w_vg.rearrange("(h p) n -> p h n", p=P)).then_inc(sem("w"), 16)
            sp.dma_start(wo, w_o.rearrange("(h p) n -> p h n", p=P)).then_inc(sem("w"), 16)
            sp.dma_start(bias_qk[:, 0, :], b_q.rearrange("(h p) -> p h", p=P), allow_slow_non_contiguous=True)\
                .then_inc(sem("w"), 16)
            sp.dma_start(bias_qk[:, 1, :], b_k.rearrange("(h p) -> p h", p=P), allow_slow_non_contiguous=True)\
                .then_inc(sem("w"), 16)
            rows(bias_vg, b_vg, 2 * D)
            rows(bias_o, b_o, D)
            rows(gnw, gn_w, D)
            rows(gnb, gn_b, D)
            sp.wait_ge(sem("powers"), 1)
            sp.dma_start(powers_dram, powers[0:HEADS, :]).then_inc(sem("powers_out"), 16)
            sp.wait_ge(sem("powers_out"), 16)
            W = 2 * P + 1
            for c in range(CH):
                for par in range(2):
                    src = bass.AP(tensor=powers_dram.tensor, offset=(c * HC + par) * W + 1,
                                  ap=[[1, P], [2 * W, GR], [1, P]])
                    sp.dma_start(turned[:, :, c, par, :], src).then_inc(sem("decay"), 16)
                src = bass.AP(tensor=powers_dram.tensor, offset=c * HC * W + P + 1, ap=[[W, HC], [0, DH], [1, P]])
                sp.dma_start(q_decay[:, c, :], src).then_inc(sem("decay"), 16)
            sp.wait_ge(sem("decay"), 16 * 3 * CH)

        @block.tensor
        def _(pe):
            pe.wait_ge(sem("w"), 16 * 9)

            def project(b, h, first=False):
                at = tp_project(b, first) + CH * h
                for c in range(CH):
                    pe.wait_ge(sem("tp_read"), at + c + 1)
                    for j in range(BLK):
                        if c == 0:
                            pe.wait_ge(sem("xn_ready"), TB * b + BLK * h + j + 1)
                        last = pe.transpose(tp[:, j * P:(j + 1) * P], xn[:, BLK * h + j, c * P:(c + 1) * P], k.ident[:, :])
                    last.then_inc(sem("tp_full"), 1)
                pe.wait_ge(sem("xnt_ready"), CH * (H * b + h + 1))
                use = PJ_TURN * b + (2 * CH + BLK) * h
                for m in range(2 * CH):
                    pe.wait_ge(sem("pj_read"), use + m + 1)
                    for c in range(CH):
                        last = pe.matmul(pj[m % 2][:, :], wqk[:, c, m * P:(m + 1) * P], xnt[:, h, c, :],
                                         start=c == 0, stop=c == CH - 1)
                    last.then_inc(sem("pj_full"), 1)
                for j in range(BLK):
                    pe.wait_ge(sem("pj_read"), use + 2 * CH + j + 1)
                    for c in range(CH):
                        last = pe.matmul(pj[j % 2][:, :], xnt[:, h, c, j * P:(j + 1) * P], wvg[:, c, :],
                                         start=c == 0, stop=c == CH - 1)
                    last.then_inc(sem("pj_full"), 1)

            def chunks(b):
                def output_of(j):
                    pe.wait_ge(sem("rt_read"), RT_TURN * b + j + 1)
                    pe.wait_ge(sem("masked_ready"), GR * (TB * b + j + 1))
                    if j:
                        pe.wait_ge(sem("state_ready"), TB * b + j + 1)
                        pe.wait_ge(sem("qst_ready"), CH * H * b + CH * (j // BLK + 1))
                    for c in range(CH):
                        cols = slice(c * P, (c + 1) * P)
                        if j:
                            pe.matmul(rt[:, cols], qst[:, c, j * P:(j + 1) * P], state[:, j % 2, c, :],
                                      start=True, stop=False, skip_group_check=True)
                        for g in range(GR):
                            for par in range(2):
                                head = c * HC + 2 * g + par
                                cols = slice(head * DH, (head + 1) * DH)
                                last = pe.matmul(rt[:, cols], masked[:, j % 2, g, (2 * c + par) * P:(2 * c + par + 1) * P],
                                                 vg[:, j, cols], start=j == 0, stop=True, skip_group_check=True)
                    last.then_inc(sem("rt_full"), 1)

                pe.wait_ge(sem("pj_read"), 2 + PJ_TURN * (b + 1))
                pe.wait_ge(sem("ktp_ready"), CH * H * (b + 1))
                for j in range(TB):
                    here = slice(j * P, (j + 1) * P)
                    pe.wait_ge(sem("tp_read"), tp_chunks(b) + 2 * j + 1)
                    for c in range(CH):
                        last = pe.transpose(tp[:, c * P:(c + 1) * P], kt[:, c, here], k.ident[:, :])
                    last.then_inc(sem("tp_full"), 1)
                    for g in range(GR):
                        pe.wait_ge(sem("sc_read"), GR * (TB * b + j) + g + 1)
                        rows = slice(32 * g, 32 * (g + 1))
                        for c in range(CH):
                            for par in range(2):
                                last = pe.matmul(sc[g][:, (2 * c + par) * P:(2 * c + par + 1) * P],
                                                 ktp[rows, par, c, here], qt[rows, c, here], start=True, stop=True)
                        last.then_inc(sem("sc_full"), 1)
                    if j:
                        output_of(j - 1)
                    if j < TB - 1:
                        pe.wait_ge(sem("tp_read"), tp_chunks(b) + 2 * j + 2)
                        for c in range(CH):
                            cols = slice(c * P, (c + 1) * P)
                            last = pe.matmul(tp[:, 2 * P + c * P:2 * P + (c + 1) * P], kd[:, j % 2, cols], vg[:, j, cols],
                                             start=True, stop=True)
                        last.then_inc(sem("tp_full"), 1)
                output_of(TB - 1)

            def group_sum(b, i, src, ready):
                pe.wait_ge(sem("rt_read"), RT_TURN * b + TB + i + 1)
                pe.wait_ge(ready, b + 1)
                for j in range(TB):
                    last = pe.matmul(rt[:, 0:D], k.ones[:, :], src[:, j, :], start=j == 0, stop=j == TB - 1)
                last.then_inc(sem("rt_full"), 1)

            def output(b, last_one=False):
                def project_pair(i):
                    pe.wait_ge(sem("rt_read"), RT_TURN * b + TB + 2 + i + 1)
                    pe.wait_ge(sem("rnt_ready"), TB // 2 * b + i + 1)
                    for j in range(2):
                        for c in range(CH):
                            last = pe.matmul(rt[:, j * D:(j + 1) * D], rnt[:, i % 2, j, c, :], wo[:, c, :],
                                             start=c == 0, stop=c == CH - 1)
                    last.then_inc(sem("rt_full"), 1)

                pe.wait_ge(sem("gated"), b + 1)
                for i in range(TB // 2):
                    pe.wait_ge(sem("tp_read"), tp_output(b, last_one) + i + 1)
                    for j in range(2):
                        for c in range(CH):
                            last = pe.transpose(tp[:, (2 * j + c) * P:(2 * j + c + 1) * P],
                                                ret[:, 2 * i + j, c * P:(c + 1) * P], k.ident[:, :])
                    last.then_inc(sem("tp_full"), 1)
                    if i:
                        project_pair(i - 1)
                project_pair(TB // 2 - 1)

            project(0, 0, first=True)
            project(0, 1, first=True)
            pe.wait_ge(sem("decay"), 16 * 3 * CH)
            pe.wait_ge(sem("reverse"), 2)
            for g in range(GR):
                pe.matmul(sc[g][:, :], reverse, turned[:, g].rearrange("p c q n -> p (c q n)"), start=True, stop=True)\
                    .then_inc(sem("decay_turned"), 1)
            with pe.Fori(0, B - 1) as b:
                chunks(b)
                group_sum(b, 0, ret, sem("ret_kept"))
                project(b + 1, 0)
                group_sum(b, 1, square, sem("squared"))
                project(b + 1, 1)
                output(b)
            chunks(B - 1)
            group_sum(B - 1, 0, ret, sem("ret_kept"))
            group_sum(B - 1, 1, square, sem("squared"))
            output(B - 1, last_one=True)

        @block.scalar
        def _(act):
            act.preload_act_table(ACT.Silu)
            act.wait_ge(sem("w"), 16 * 9)
            act.sem_inc(sem("pj_read"), 2)

            def project(b, h, first=False):
                at = tp_project(b, first) + CH * h
                for c in range(CH):
                    act.wait_ge(sem("tp_full"), at + c + 1)
                    act.activation(xnt[:, h, c, :], tp[:, :], ACT.Copy).then_inc(sem("tp_read"), 1)
                    act.wait_ge(sem("tp_read"), at + c + 2)
                    act.sem_inc(sem("xnt_ready"), 1)
                use = PJ_TURN * b + (2 * CH + BLK) * h
                for m in range(2 * CH):
                    act.wait_ge(sem("pj_full"), use + m + 1)
                    dst = (qt if m < CH else kt)[:, m % CH, h * N:(h + 1) * N]
                    act.activation(dst, pj[m % 2][:, :], ACT.Identity, bias=bias_qk[:, m // CH, m % CH:m % CH + 1])\
                        .then_inc(sem("pj_read"), 1)
                for j in range(BLK):
                    act.wait_ge(sem("pj_read"), 2 + use + 2 * CH + j + 1)
                    act.sem_inc(sem("gate_in"), 1)
                    t = BLK * h + j
                    act.activation(one_tile(gates, TB * b + t), vg[:, t, D:2 * D], ACT.Silu).then_inc(sem("gates"), 1)

            def chunks(b):
                for j in range(TB):
                    act.wait_ge(sem("rt_full"), RT_TURN * b + j + 1)
                    act.activation(ret[:, j, :], rt[:, 0:D], ACT.Copy).then_inc(sem("rt_read"), 1)
                act.wait_ge(sem("rt_read"), 1 + RT_TURN * b + TB)
                act.sem_inc(sem("ret_kept"), 1)

            def squares(b):
                act.wait_ge(sem("centred"), b + 1)
                act.activation(square, ret, ACT.Square).then_inc(sem("squared"), 1)

            def output(b, last_one=False):
                for i in range(TB // 2):
                    act.wait_ge(sem("tp_full"), tp_output(b, last_one) + i + 1)
                    act.activation(rnt[:, i % 2].rearrange("p j c n -> p (j c n)"), tp[:, :], ACT.Copy)\
                        .then_inc(sem("tp_read"), 1)
                    act.wait_ge(sem("tp_read"), tp_output(b, last_one) + i + 2)
                    act.sem_inc(sem("rnt_ready"), 1)

            project(0, 0, first=True)
            project(0, 1, first=True)
            for g in range(GR):
                act.wait_ge(sem("decay_turned"), g + 1)
                act.activation(decay[:, g].rearrange("p c q n -> p (c q n)"), sc[g][:, :], ACT.Copy)\
                    .then_inc(sem("decay_ready"), 1)
            with act.Fori(0, B - 1) as b:
                chunks(b)
                squares(b)
                project(b + 1, 0)
                project(b + 1, 1)
                output(b)
            chunks(B - 1)
            squares(B - 1)
            output(B - 1, last_one=True)

        @block.gpsimd
        def _(pool):
            pool.iota(row_i, [[0, 1]], base=0, channel_multiplier=1).then_inc(sem("row_i"), 1)
            pool.memset(blocks, 1.0).then_inc(sem("blocks"), 1)
            pool.memset(reverse, 0.0).then_inc(sem("reverse"), 1)
            pool.wait_ge(sem("reverse"), 1)
            pool.affine_select(out=reverse, in_=reverse, compare_op=ALU.not_equal, fill=1.0, base=1 - P,
                               pattern=[[1, P]], channel_multiplier=1).then_inc(sem("reverse"), 1)
            pool.wait_ge(sem("blocks"), 1)
            cells = blocks.rearrange("p (a b) -> p a b", b=DH)
            pool.affine_select(out=cells, in_=cells, compare_op=ALU.is_ge, fill=0.0, base=0,
                               pattern=[[-DH, HC], [0, DH]], channel_multiplier=1).then_inc(sem("blocks"), 1)
            pool.wait_ge(sem("blocks"), 2)
            pool.affine_select(out=cells, in_=cells, compare_op=ALU.is_ge, fill=0.0, base=DH - 1,
                               pattern=[[DH, HC], [0, DH]], channel_multiplier=-1).then_inc(sem("blocks"), 1)
            pool.wait_ge(sem("decay"), 16 * 3 * CH)
            pool.wait_ge(sem("w"), 16 * 9)

            def layernorm_power(n):
                pool.wait_ge(sem("var_ready"), n + 1)
                pool.tensor_tensor(rstd, rstd, k.minus_half[:, 0:BLK], ALU.pow).then_inc(sem("rstd_ready"), 1)

            def decay_q(b, h):
                pool.wait_ge(sem("pj_read"), 2 + PJ_TURN * b + (2 * CH + BLK) * h + CH)
                for c in range(CH):
                    q4 = qt[:, c, h * N:(h + 1) * N].rearrange("p (j n) -> p j n", n=P)
                    s4 = qst[:, c, h * N:(h + 1) * N].rearrange("p (j n) -> p j n", n=P)
                    pool.tensor_tensor(s4, q4, q_decay[:, c, :].unsqueeze(1).to_broadcast([P, BLK, P]), ALU.mult)\
                        .then_inc(sem("qst_ready"), 1)

            def group_power(b):
                pool.wait_ge(sem("group_var"), b + 1)
                pool.tensor_tensor(group_scale, group_scale, k.minus_half[:, 0:HEADS], ALU.pow)\
                    .then_inc(sem("group_rstd"), 1)

            for h in range(H):
                layernorm_power(h)
            for h in range(H):
                decay_q(0, h)
            with pool.Fori(0, B - 1) as b:
                for h in range(H):
                    layernorm_power(H * (b + 1) + h)
                decay_q(b + 1, 0)
                group_power(b)
                decay_q(b + 1, 1)
            group_power(B - 1)

        @block.vector
        def _(dve):
            dve.sem_inc(sem("tp_read"), 1)
            dve.sem_inc(sem("rt_read"), 1)

            def normalise(b, h):
                steps = Chain(dve, sem("ln_steps"), (2 * BLK + 1) * H, b, (2 * BLK + 1) * h)
                for j in range(BLK):
                    steps.step(dve.bn_stats(stats[:, j, :], one_tile(k.res, TB * b + BLK * h + j)))
                steps.settled()
                dve.sem_inc(sem("stats_complete"), 1)
                for j in range(BLK):
                    steps.step(dve.bn_aggr(moments[:, j, :], stats[:, j, :]))
                steps.settled()
                steps.step(dve.tensor_scalar(rstd, moments[:, :, 1], EPS, None, ALU.add))
                steps.settled()
                dve.sem_inc(sem("var_ready"), 1)
                dve.wait_ge(sem("rstd_ready"), H * b + h + 1)
                for j in range(BLK):
                    t = BLK * h + j
                    dve.tensor_scalar(xn[:, t, :], one_tile(k.res, TB * b + t), moments[:, j, 0:1], rstd[:, j:j + 1],
                                      ALU.subtract, ALU.mult).then_inc(sem("xn_ready"), 1)

            def project(b, h):
                use = PJ_TURN * b + (2 * CH + BLK) * h
                here = slice(h * N, (h + 1) * N)
                dve.wait_ge(sem("pj_read"), 2 + use + 2 * CH)
                for c in range(CH):
                    dve.tensor_scalar(ktp[:, 0, c, here], kt[:, c, here], parity[:, 0:1], None, ALU.mult)
                    dve.tensor_scalar(ktp[:, 1, c, here], kt[:, c, here], parity[:, 1:2], None, ALU.mult)\
                        .then_inc(sem("ktp_ready"), 1)
                for j in range(BLK):
                    dve.wait_ge(sem("pj_full"), use + 2 * CH + j + 1)
                    dve.tensor_tensor(vg[:, BLK * h + j, :], pj[j % 2][:, :], bias_vg, ALU.add)\
                        .then_inc(sem("pj_read"), 1)

            def chunk(b, j):
                dve.wait_ge(sem("tp_full"), tp_chunks(b) + 2 * j + 1)
                for c in range(CH):
                    last = dve.tensor_tensor(
                        kd[:, j % 2, c * P:(c + 1) * P].rearrange("p (g q d) -> p g q d", g=GR, q=2),
                        tp[:, c * P:(c + 1) * P].rearrange("p (g q d) -> p g q d", g=GR, q=2),
                        decay[:, :, c, :, P - 1:P].to_broadcast([P, GR, 2, DH]), ALU.mult)
                last.then_inc(sem("tp_read"), 1)
                for g in range(GR):
                    dve.wait_ge(sem("sc_full"), GR * (TB * b + j) + g + 1)
                    dve.tensor_tensor(masked[:, j % 2, g, :], sc[g][:, :], decay[:, g].rearrange("p c q n -> p (c q n)"),
                                      ALU.mult).then_inc(sem("sc_read"), 1)
                dve.wait_ge(sem("sc_read"), GR + GR * (TB * b + j + 1))
                dve.sem_inc(sem("masked_ready"), GR)
                steps = Chain(dve, sem("state_steps"), 2 * (TB - 1), b, 2 * j)
                if j < TB - 1:
                    dve.wait_ge(sem("tp_full"), tp_chunks(b) + 2 * j + 2)
                    dve.tensor_tensor(update, tp[:, 2 * P:4 * P].rearrange("p (c n) -> p c n", c=CH),
                                      blocks.unsqueeze(1).to_broadcast([P, CH, P]), ALU.mult).then_inc(sem("tp_read"), 1)
                    dve.wait_ge(sem("tp_read"), 1 + tp_chunks(b) + 2 * j + 2)
                    for c in range(CH):
                        if j == 0:
                            steps.step(dve.tensor_copy(state[:, 1, c, :], update[:, c, :]))
                        else:
                            steps.step(dve.scalar_tensor_tensor(state[:, (j + 1) % 2, c, :], state[:, j % 2, c, :],
                                                                q_decay[:, c, P - 1:P], update[:, c, :],
                                                                ALU.mult, ALU.add))
                    steps.settled()
                if j == 0:
                    dve.sem_inc(sem("state_ready"), 1)
                if j < TB - 1:
                    dve.sem_inc(sem("state_ready"), 1)

            def group_reduce(b, i):
                dve.wait_ge(sem("rt_full"), RT_TURN * b + TB + i + 1)
                dve.tensor_reduce(sums, rt[:, 0:D].rearrange("p (h d) -> p h d", d=DH), AX_X, ALU.add)\
                    .then_inc(sem("rt_read"), 1)
                dve.wait_ge(sem("rt_read"), 1 + RT_TURN * b + TB + i + 1)

            by_head = ret.rearrange("p t (h d) -> p t h d", d=DH)

            def centre(b):
                steps = Chain(dve, sem("centre_steps"), 1 + TB, b)
                group_reduce(b, 0)
                steps.link(dve.tensor_scalar(sums, sums, 1.0 / COUNT, None, ALU.mult))
                for t in range(TB):
                    steps.step(dve.tensor_tensor(by_head[:, t], by_head[:, t],
                                                 sums.unsqueeze(2).to_broadcast([P, HEADS, DH]), ALU.subtract))
                steps.settled()
                dve.sem_inc(sem("centred"), 1)

            def variance(b):
                steps = Chain(dve, sem("var_steps"), 1, b)
                group_reduce(b, 1)
                steps.link(dve.tensor_scalar(group_scale, sums, 1.0 / COUNT, EPS, ALU.mult, ALU.add))
                dve.sem_inc(sem("group_var"), 1)

            def gated(b):
                steps = Chain(dve, sem("gate_steps"), 4, b)
                dve.wait_ge(sem("group_rstd"), b + 1)
                steps.link(dve.tensor_tensor(scale.rearrange("p (h d) -> p h d", d=DH), gnw.rearrange("p (h d) -> p h d", d=DH),
                                             group_scale.unsqueeze(2).to_broadcast([P, HEADS, DH]), ALU.mult))
                steps.link(dve.tensor_tensor(ret, ret, scale.unsqueeze(1).to_broadcast([P, TB, D]), ALU.mult))
                steps.link(dve.tensor_tensor(ret, ret, gnb.unsqueeze(1).to_broadcast([P, TB, D]), ALU.add))
                dve.wait_ge(sem("gates"), TB * (b + 1))
                steps.link(dve.tensor_tensor(ret, ret, gates[:, bass.ds(TB * b, TB), :], ALU.mult))
                dve.sem_inc(sem("gated"), 1)
                tiles = k.res[:, bass.ds(TB * b, TB), :]
                dve.tensor_tensor(tiles, tiles, bias_o.unsqueeze(1).to_broadcast([P, TB, D]), ALU.add)\
                    .then_inc(sem("bias_added"), 1)
                dve.wait_ge(sem("bias_added"), b + 1)

            def output(b):
                for i in range(TB // 2):
                    dve.wait_ge(sem("rt_full"), RT_TURN * b + TB + 2 + i + 1)
                    tiles = k.res[:, bass.ds(TB * b + 2 * i, 2), :]
                    dve.tensor_tensor(tiles, tiles, rt[:, :].rearrange("p (j d) -> p j d", d=D), ALU.add)\
                        .then_inc(sem("rt_read"), 1)

            dve.wait_ge(sem("gamma"), 16)
            c = Chain(dve, sem("setup"))
            c.step(dve.memset(powers[0:HEADS, 0:P], 0.0))
            c.step(dve.memset(powers[0:HEADS, P:P + 1], 1.0))
            m = 1
            while m < P:
                c.link(dve.tensor_scalar(powers[0:HEADS, P + m + 1:P + 2 * m + 1], powers[0:HEADS, P + 1:P + m + 1],
                                         powers[0:HEADS, P + m:P + m + 1], None, ALU.mult))
                m *= 2
            dve.sem_inc(sem("powers"), 1)
            dve.wait_ge(sem("row_i"), 1)
            c.link(dve.tensor_scalar(row_i, row_i, DH, None, ALU.bitwise_and))
            c.link(dve.tensor_scalar(parity[:, 1:2], row_i, 1.0 / DH, None, ALU.mult))
            c.link(dve.tensor_scalar(parity[:, 0:1], parity[:, 1:2], -1.0, 1.0, ALU.mult, ALU.add))
            for h in range(H):
                normalise(0, h)
            dve.wait_ge(sem("w"), 16 * 9)
            for h in range(H):
                project(0, h)
            dve.wait_ge(sem("decay_ready"), GR)
            dve.sem_inc(sem("sc_read"), GR)
            dve.wait_ge(sem("decay"), 16 * 3 * CH)
            dve.wait_ge(sem("blocks"), 3)

            def chunks(b, last_one=False):
                for j in range(TB):
                    chunk(b, j)
                    if not last_one and j in (2, 5):
                        normalise(b + 1, j // 3)

            with dve.Fori(0, B - 1) as b:
                chunks(b)
                centre(b)
                project(b + 1, 0)
                variance(b)
                project(b + 1, 1)
                gated(b)
                output(b)
            chunks(B - 1, last_one=True)
            centre(B - 1)
            variance(B - 1)
            gated(B - 1)
            output(B - 1)
            dve.wait_ge(sem("rt_read"), 1 + RT_TURN * B)




class Kept:

    CONSTS = 7

    def __init__(self, nc, ctx):
        def sb(name, shape, dt):
            return ctx.enter_context(nc.sbuf_tensor(name, shape, dt))

        self.nc = nc
        self.ident = sb("ident", [P, P], F32)
        self.ones = sb("ones", [P, P], F32)
        self.ones_bf = sb("ones_bf", [P, P], BF16)
        self.tri_bf = sb("tri_bf", [P, P], BF16)
        self.iota64 = sb("iota64", [P, 64], F32)
        self.minus_half = sb("minus_half", [P, 64], F32)
        self.zero = sb("zero", [P, 1024], F32)
        self.const_made = ctx.enter_context(nc.semaphore("const_made"))
        self.const_ready = ctx.enter_context(nc.semaphore("const_ready"))
        self.res = sb("residual", [P, 32, 256], F32)
        self.slots = Slots(nc, 32 * P, 256, 64, 4)
        self.ZEROINGS = self.slots.tiles // 4
        self.slots_zeroed = ctx.enter_context(nc.semaphore("slots_zeroed"))
        floats = 43008
        self.arena = Arena(sb("arena", [P, floats], F32), floats)

    def zero_slots(self, sp):
        sp.wait_ge(self.const_ready, self.CONSTS)
        rows = self.slots.x.rearrange("(n p r) d -> n p (r d)", p=P, r=4)
        for n in range(self.ZEROINGS):
            sp.dma_start(rows[n], self.zero[:, :]).then_inc(self.slots_zeroed, 16)

    def make_constants(self, pool):
        made = self.const_made
        pool.memset(self.ident[:, :], 0.0).then_inc(made, 1)
        pool.memset(self.tri_bf[:, :], 1.0).then_inc(made, 1)
        pool.memset(self.ones[:, :], 1.0).then_inc(made, 1)
        pool.memset(self.ones_bf[:, :], 1.0).then_inc(made, 1)
        pool.memset(self.minus_half[:, :], -0.5).then_inc(made, 1)
        pool.memset(self.zero[:, :], 0.0).then_inc(made, 1)
        pool.iota(self.iota64[:, :], [[1, 64]], base=0, channel_multiplier=0,
                  allow_small_or_imprecise_dtypes=True).then_inc(made, 1)
        pool.wait_ge(made, self.CONSTS)
        pool.affine_select(out=self.ident[:, :], in_=self.ident[:, :], compare_op=ALU.not_equal, fill=1.0, base=0,
                           pattern=[[-1, P]], channel_multiplier=1).then_inc(self.const_ready, 1)
        pool.affine_select(out=self.tri_bf[:, :], in_=self.tri_bf[:, :], compare_op=ALU.is_gt, fill=0.0, base=0,
                           pattern=[[1, P]], channel_multiplier=-1).then_inc(self.const_ready, 1)
        pool.wait_ge(self.const_ready, 2)
        pool.sem_inc(self.const_ready, self.CONSTS - 2)




def program(nc, x, w_rvk, w_out, time_decay, time_first, w_qk, w_vg, w_o, b_q, b_k, b_vg, b_o, gn_w, gn_b, gamma,
            router_w, router_bias, w_gu, w_d, sw_gu, sw_d, out):
    with ExitStack() as ctx:
        k = Kept(nc, ctx)
        time_mix(nc, k, x, w_rvk, w_out, time_decay, time_first)
        experts(nc, k, "moe1", router_w, router_bias, w_gu, w_d, sw_gu, sw_d)
        retention(nc, k, w_qk, w_vg, w_o, b_q, b_k, b_vg, b_o, gn_w, gn_b, gamma, x.shape[0])
        experts(nc, k, "moe2", router_w, router_bias, w_gu, w_d, sw_gu, sw_d, out=out)


def kernel(**inputs):
    import numpy as np
    import concourse.bacc as bacc
    from concourse.bass_utils import run_bass_kernel_spmd

    a, b, f = "L0_attn_a_", "L0_attn_b_", "L0_ffn_"
    g = {n: np.asarray(v) for n, v in inputs.items()}
    D = g[a + "x"].shape[-1]

    def joined(w):
        return np.transpose(w, (1, 0, 2)).reshape(D, -1)

    arrays = {
        "x": g[a + "x"],
        "w_rvk": g[a + "W_rvk"].T,
        "w_out": g[a + "W_out"].T,
        "time_decay": g[a + "time_decay"],
        "time_first": g[a + "time_first"],
        "w_qk": np.concatenate([g[b + "wq"], g[b + "wk"]], axis=1),
        "w_vg": np.concatenate([g[b + "wv"], g[b + "wg"]], axis=1),
        "w_o": g[b + "wo"],
        "b_q": g[b + "bq"],
        "b_k": g[b + "bk"],
        "b_vg": np.concatenate([g[b + "bv"], g[b + "bg"]]),
        "b_o": g[b + "bo"],
        "gn_w": g[b + "gn_w"],
        "gn_b": g[b + "gn_b"],
        "gamma": g[b + "gamma"],
        "router_w": g[f + "router_w"],
        "router_bias": g[f + "router_bias"],
        "w_gu": np.transpose(np.concatenate([g[f + "wg"], g[f + "wu"]], axis=2), (1, 0, 2)),
        "w_d": g[f + "wd"],
        "sw_gu": np.concatenate([joined(g[f + "swg"]), joined(g[f + "swu"])], axis=1),
        "sw_d": g[f + "swd"].reshape(-1, D),
    }
    arrays = {n: np.ascontiguousarray(v) for n, v in arrays.items()}
    nc = bacc.Bacc("TRN2", target_bir_lowering=False, num_devices=1)
    aps = {n: nc.dram_tensor(n, v.shape, mybir.dt.from_np(v.dtype), kind="ExternalInput").ap()
           for n, v in arrays.items()}
    out = nc.dram_tensor("out", arrays["x"].shape, F32, kind="ExternalOutput").ap()
    program(nc, out=out, **aps)
    return run_bass_kernel_spmd(nc, [arrays], core_ids=[0]).results[0]["out"]
```

```python
from contextlib import ExitStack

import concourse.bass as bass
from concourse import mybir

P = 128
F32 = mybir.dt.float32
BF16 = mybir.dt.bfloat16
I32 = mybir.dt.int32
U32 = mybir.dt.uint32
ALU = mybir.AluOpType
ACT = mybir.ActivationFunctionType
AX_X = mybir.AxisListType.X
EPS = 1e-5


class Arena:

    def __init__(self, tensor, floats):
        self.tensor, self.floats, self.at = tensor, floats, 0

    def take(self, *shape, at=None):
        n = 1
        for s in shape:
            n *= s
        start = self.at if at is None else at
        assert start + n <= self.floats, (start, n, self.floats)
        if at is None:
            self.at += n
        piece = self.tensor[:, start:start + n]
        if len(shape) == 2:
            piece = piece.rearrange("p (a b) -> p a b", a=shape[0])
        if len(shape) == 3:
            piece = piece.rearrange("p (a b c) -> p a b c", a=shape[0], b=shape[1])
        if len(shape) == 4:
            piece = piece.rearrange("p (a b c d) -> p a b c d", a=shape[0], b=shape[1], c=shape[2])
        return piece


class Sems:

    def __init__(self, nc, ctx, phase):
        self.nc, self.phase, self.known = nc, phase, {}
        ctx.callback(self.release)

    def __call__(self, name):
        if name not in self.known:
            self.known[name] = self.nc.alloc_semaphore(name=f"{self.phase}_{name}")
        return self.known[name]

    def release(self):
        self.nc.clear_and_free_semaphores(list(self.known.values()))
        self.nc.all_engine_barrier()


class Chain:

    def __init__(self, engine, sem, per_turn=0, turn=0, before=0):
        self.engine, self.sem, self.n = engine, sem, 0
        self.base = per_turn * turn + before

    def step(self, instruction):
        self.n += 1
        instruction.then_inc(self.sem, 1)

    def settled(self):
        self.engine.wait_ge(self.sem, self.base + self.n)

    def link(self, instruction):
        self.step(instruction)
        self.settled()


def one_tile(ap, t):
    names = " ".join("abc"[:len(ap.shape) - 2])
    return ap[(slice(None), bass.ds(t, 1)) + (slice(None),) * (len(ap.shape) - 2)].rearrange(
        f"p o {names} -> p (o {names.split()[0]}) {' '.join(names.split()[1:])}")




def time_mix(nc, k, x, w_rvk, w_out, time_decay, time_first):
    B, T, C = x.shape
    TB = T // P
    CH = C // P
    N = 512
    H = T // N
    UNITS = H * CH
    arena = k.arena
    arena.at = 0
    wrvk = arena.take(CH, 3 * C)
    wout = arena.take(CH, C)
    decay = arena.take(CH)
    first = arena.take(CH)
    stats = arena.take(TB, 6)
    moments = arena.take(TB, 2)
    mean = arena.take(B * TB)
    rstd = arena.take(B * TB)
    xn = arena.take(TB, C)
    xnt = arena.take(CH, CH, N)
    o = arena.take(CH, T + 1)
    p = arena.take(CH, T + 1)
    q = arena.take(CH, T + 1)
    dif = arena.take(UNITS, N)
    neg = arena.take(UNITS, N)
    a2 = arena.take(UNITS, N)
    b2 = arena.take(UNITS, N)
    er = arena.take(UNITS, N)
    vs = arena.take(UNITS, N)
    num = arena.take(UNITS, N)
    bv2 = arena.take(CH, N)
    yt = arena.take(H, CH, N)

    xv = x.rearrange("b (t p) c -> b p t c", p=P)
    BLK = N // P
    assert H == 2 and CH == 2
    with ExitStack() as ctx:
        sem = Sems(nc, ctx, "mix")
        rkv = [[ctx.enter_context(nc.psum_tensor(f"mix_{g}{c}", [P, N], F32)) for g in "kvr"] for c in range(CH)]
        tp = ctx.enter_context(nc.psum_tensor("mix_tp", [P, N], F32))
        op = ctx.enter_context(nc.psum_tensor("mix_op", [P, 2, C], F32))
        block = ctx.enter_context(nc.Block())

        @block.sync
        def _(sp):
            for b in range(B):
                sp.dma_start(k.res[:, b * TB:(b + 1) * TB, :], xv[b]).then_inc(sem(f"x{b}"), 16)
                if b == 0:
                    sp.dma_start(wrvk, w_rvk.rearrange("(h p) n -> p h n", p=P)).then_inc(sem("w"), 16)
                    sp.dma_start(wout, w_out.rearrange("(h p) n -> p h n", p=P)).then_inc(sem("w"), 16)
            k.zero_slots(sp)

        @block.scalar
        def _(act):
            act.dma_start(decay, time_decay.rearrange("(h p) -> p h", p=P), allow_slow_non_contiguous=True)\
                .then_inc(sem("tm"), 16)
            act.dma_start(first, time_first.rearrange("(h p) -> p h", p=P), allow_slow_non_contiguous=True)\
                .then_inc(sem("tm"), 16)
            act.preload_act_table(ACT.Exp)
            act.sem_inc(sem("tp_read"), 1)
            act.sem_inc(sem("rkv_free"), CH)
            act.wait_ge(sem("tm"), 32)
            act.activation(decay, decay, ACT.Exp).then_inc(sem("exp_decay"), 1)

            def copy_transposes(b, h):
                for half in range(CH):
                    act.wait_ge(sem("tp_full"), UNITS * b + CH * h + half + 1)
                    act.activation(xnt[:, h, half, :], tp[:, :], ACT.Copy).then_inc(sem("tp_read"), 1)

            def exps(b, u):
                _, pv, pr = rkv[u % CH]
                act.wait_ge(sem("dif_ready"), UNITS * b + u + 1)
                act.activation(a2[:, u, :], a2[:, u, :], ACT.Exp)
                act.activation(b2[:, u, :], b2[:, u, :], ACT.Exp)
                act.activation(vs[:, u, :], pv[:, :], ACT.Copy).then_inc(sem("exp2"), 1)
                act.activation(neg[:, u, :], neg[:, u, :], ACT.Exp)
                act.activation(dif[:, u, :], dif[:, u, :], ACT.Exp).then_inc(sem("exp1"), 1)
                act.activation(er[:, u, :], pr[:, :], ACT.Exp, scale=-1.0).then_inc(sem("rkv_free"), 1)

            copy_transposes(0, 0)
            exps(0, 0)
            copy_transposes(0, 1)
            exps(0, 1)
            exps(0, 2)
            with act.Fori(1, B) as b:
                copy_transposes(b, 0)
                exps(b - 1, 3)
                exps(b, 0)
                copy_transposes(b, 1)
                exps(b, 1)
                exps(b, 2)
            exps(B - 1, 3)

        @block.tensor
        def _(pe):
            pe.wait_ge(k.const_ready, k.CONSTS)
            pe.wait_ge(sem("w"), 32)

            def transposes(b, h):
                for half in range(CH):
                    pe.wait_ge(sem("tp_read"), UNITS * b + CH * h + half + 1)
                    for j in range(BLK):
                        t = h * BLK + j
                        if half == 0:
                            pe.wait_ge(sem("xn_ready"), TB * b + t + 1)
                        last = pe.transpose(tp[:, j * P:(j + 1) * P], xn[:, t, half * P:(half + 1) * P], k.ident[:, :])
                    last.then_inc(sem("tp_full"), 1)

            def project(b, h):
                pe.wait_ge(sem("tp_read"), UNITS * b + CH * h + CH + 1)
                for c in range(CH):
                    pe.wait_ge(sem("rkv_free"), UNITS * b + CH * h + c + 1)
                    for g, bank in zip((2, 1, 0), rkv[c]):
                        at = g * C + c * P
                        for half in range(CH):
                            last = pe.matmul(bank[:, :], wrvk[:, half, at:at + P], xnt[:, h, half, :],
                                             start=half == 0, stop=half == CH - 1)
                    last.then_inc(sem("rkv_ready"), 1)

            def output(b, h):
                pe.wait_ge(sem("y_ready"), UNITS * b + CH * h + CH)
                for j in range(BLK):
                    if j % 2 == 0:
                        pe.wait_ge(sem("op_read"), TB // 2 * b + (h * BLK + j) // 2 + 1)
                    for half in range(CH):
                        last = pe.matmul(op[:, j % 2, :], yt[:, h, half, j * P:(j + 1) * P], wout[:, half, :],
                                         start=half == 0, stop=half == CH - 1)
                    if j % 2 == 1:
                        last.then_inc(sem("op_full"), 1)

            transposes(0, 0)
            project(0, 0)
            transposes(0, 1)
            project(0, 1)
            with pe.Fori(1, B) as b:
                transposes(b, 0)
                output(b - 1, 0)
                project(b, 0)
                transposes(b, 1)
                output(b - 1, 1)
                project(b, 1)
            output(B - 1, 0)
            output(B - 1, 1)

        @block.gpsimd
        def _(pool):
            k.make_constants(pool)
            pool.wait_ge(k.const_made, k.CONSTS)
            with pool.Fori(0, B) as b:
                pool.wait_ge(sem("var_ready"), b + 1)
                pool.tensor_tensor(rstd[:, bass.ds(b * TB, TB)], rstd[:, bass.ds(b * TB, TB)], k.minus_half[:, 0:TB],
                                   ALU.pow).then_inc(sem("rstd_ready"), 1)
            with pool.Fori(0, B) as b:
                for u in range(UNITS):
                    h, c = u // CH, u % CH
                    n = UNITS * b + u
                    before = slice(h * N, (h + 1) * N)
                    steps = Chain(pool, sem("pool_steps"), 5 * UNITS, b, 5 * u)
                    pool.wait_ge(sem("pq_ready"), n + 1)
                    pool.wait_ge(sem("exp1"), n + 1)
                    steps.step(pool.tensor_tensor(num[:, u, :], neg[:, u, :], p[:, c, before], ALU.mult))
                    steps.step(pool.tensor_tensor(vs[:, u, :], dif[:, u, :], vs[:, u, :], ALU.mult))
                    steps.step(pool.tensor_tensor(neg[:, u, :], neg[:, u, :], q[:, c, before], ALU.mult))
                    steps.settled()
                    steps.step(pool.tensor_tensor(num[:, u, :], num[:, u, :], vs[:, u, :], ALU.add))
                    steps.step(pool.tensor_tensor(neg[:, u, :], neg[:, u, :], dif[:, u, :], ALU.add))
                    steps.settled()
                    pool.sem_inc(sem("sums_ready"), 1)

        @block.vector
        def _(dve):
            dve.wait_ge(sem("exp_decay"), 1)
            dve.tensor_scalar(decay, decay, -1.0, None, ALU.mult).then_inc(sem("setup"), 1)
            for c in range(CH):
                dve.memset(o[:, c, 0:1], -1e38).then_inc(sem("setup"), 1)
                dve.memset(p[:, c, 0:1], 0.0).then_inc(sem("setup"), 1)
                dve.memset(q[:, c, 0:1], 0.0).then_inc(sem("setup"), 1)
            dve.wait_ge(sem("setup"), 1 + 3 * CH)
            dve.sem_inc(sem("op_read"), 1)

            def statistics(b):
                steps = Chain(dve, sem("stat_steps"), 2 * TB + 2, b)
                for t in range(TB):
                    steps.step(dve.bn_stats(stats[:, t, :], one_tile(k.res, b * TB + t)))
                steps.settled()
                dve.sem_inc(sem("stats_complete"), 1)
                for t in range(TB):
                    steps.step(dve.bn_aggr(moments[:, t, :], stats[:, t, :]))
                steps.settled()
                steps.step(dve.tensor_copy(mean[:, bass.ds(b * TB, TB)], moments[:, :, 0]))
                steps.step(dve.tensor_scalar(rstd[:, bass.ds(b * TB, TB)], moments[:, :, 1], EPS, None, ALU.add))
                steps.settled()
                dve.sem_inc(sem("var_ready"), 1)

            def normalise(b):
                dve.wait_ge(sem("rstd_ready"), b + 1)
                for t in range(TB):
                    dve.tensor_scalar(xn[:, t, :], one_tile(k.res, b * TB + t), mean[:, bass.ds(b * TB + t, 1)],
                                      rstd[:, bass.ds(b * TB + t, 1)], ALU.subtract, ALU.mult).then_inc(sem("xn_ready"), 1)

            def differences(b, u):
                h, c = u // CH, u % CH
                before, after = slice(h * N, (h + 1) * N), slice(h * N + 1, (h + 1) * N + 1)
                pk = rkv[c][0]
                steps = Chain(dve, sem("dif_steps"), 6 * UNITS, b, 6 * u)
                dve.wait_ge(sem("rkv_ready"), UNITS * b + u + 1)
                steps.link(dve.tensor_tensor_scan(o[:, c, after], decay[:, c:c + 1].to_broadcast([P, N]), pk[:, :],
                                                  o[:, c, h * N:h * N + 1], ALU.add, ALU.max))
                steps.step(dve.scalar_tensor_tensor(dif[:, u, :], pk[:, :], first[:, c:c + 1], o[:, c, before],
                                                    ALU.add, ALU.subtract))
                steps.step(dve.scalar_tensor_tensor(a2[:, u, :], o[:, c, before], decay[:, c:c + 1], o[:, c, after],
                                                    ALU.add, ALU.subtract))
                steps.step(dve.tensor_tensor(b2[:, u, :], pk[:, :], o[:, c, after], ALU.subtract))
                steps.settled()
                steps.step(dve.tensor_scalar(neg[:, u, :], dif[:, u, :], -1.0, 0.0, ALU.mult, ALU.min))
                steps.settled()
                steps.link(dve.tensor_scalar(dif[:, u, :], dif[:, u, :], 0.0, None, ALU.min))
                dve.sem_inc(sem("dif_ready"), 1)

            def states(b, u):
                h, c = u // CH, u % CH
                after, start = slice(h * N + 1, (h + 1) * N + 1), slice(h * N, h * N + 1)
                steps = Chain(dve, sem("state_steps"), 3 * UNITS, b, 3 * u)
                dve.wait_ge(sem("exp2"), UNITS * b + u + 1)
                steps.link(dve.tensor_tensor(bv2[:, c, :], b2[:, u, :], vs[:, u, :], ALU.mult))
                steps.step(dve.tensor_tensor_scan(p[:, c, after], a2[:, u, :], bv2[:, c, :], p[:, c, start],
                                                  ALU.mult, ALU.add))
                steps.step(dve.tensor_tensor_scan(q[:, c, after], a2[:, u, :], b2[:, u, :], q[:, c, start],
                                                  ALU.mult, ALU.add))
                steps.settled()
                dve.sem_inc(sem("pq_ready"), 1)

            def outputs(b, u):
                h, c = u // CH, u % CH
                steps = Chain(dve, sem("y_steps"), 3 * UNITS, b, 3 * u)
                dve.wait_ge(sem("sums_ready"), UNITS * b + u + 1)
                dve.wait_ge(sem("rkv_free"), CH + UNITS * b + u + 1)
                steps.link(dve.scalar_tensor_tensor(neg[:, u, :], er[:, u, :], 1.0, neg[:, u, :], ALU.add, ALU.mult))
                steps.link(dve.reciprocal(neg[:, u, :], neg[:, u, :]))
                steps.link(dve.tensor_tensor(yt[:, h, c, :], num[:, u, :], neg[:, u, :], ALU.mult))
                dve.sem_inc(sem("y_ready"), 1)

            def add_output(b, h):
                for j in range(BLK // 2):
                    pair = b * (TB // 2) + h * (BLK // 2) + j
                    dve.wait_ge(sem("op_full"), pair + 1)
                    tiles = k.res[:, bass.ds(2 * pair, 2), :]
                    dve.tensor_tensor(tiles, tiles, op[:, :, :], ALU.add).then_inc(sem("op_read"), 1)

            def batch(b, is_first=False, is_last=False):
                differences(b, 0)
                differences(b, 1)
                states(b, 0)
                if not is_first:
                    add_output(b - 1, 1)
                states(b, 1)
                differences(b, 2)
                outputs(b, 0)
                differences(b, 3)
                outputs(b, 1)
                if not is_last:
                    normalise(b + 1)
                states(b, 2)
                add_output(b, 0)
                states(b, 3)
                outputs(b, 2)
                outputs(b, 3)

            dve.wait_ge(sem("x0"), 16)
            statistics(0)
            normalise(0)
            for b in range(1, B):
                dve.wait_ge(sem(f"x{b}"), 16)
            with dve.Fori(1, B) as b:
                statistics(b)
            batch(0, is_first=True)
            with dve.Fori(1, B - 1) as b:
                batch(b)
            batch(B - 1, is_last=True)
            add_output(B - 1, 1)
            dve.wait_ge(sem("op_read"), 1 + B * TB // 2)




class Slots:

    NO_PAIR = 2.0
    TAIL = 4

    def __init__(self, nc, tokens, width, experts, choices):
        self.tiles = tokens * choices // P + experts
        self.pairs = tokens * choices
        self.width = width + self.TAIL
        self.x = nc.dram_tensor("slots_x", (self.tiles * P, self.width), F32, kind="Internal").ap()
        self.y = nc.dram_tensor("pairs_y", (self.pairs, width), F32, kind="Internal").ap()
        self.expert = nc.dram_tensor("slots_expert", (self.tiles,), I32, kind="Internal").ap()


def experts(nc, k, phase, zeroed, router_w, router_bias, w_gu, w_d, sw_gu, sw_d, out=None):
    NT, D = k.res.shape[1], k.res.shape[2]
    E = router_w.shape[1]
    F = w_d.shape[1]
    K = 4
    KH = D // P
    BLK = 4
    N = BLK * P
    NB = NT // BLK
    SH = sw_d.shape[0] // P
    NX = k.slots.tiles
    slots = k.slots
    arena = k.arena
    arena.at = 0
    W = slots.width
    xn = arena.take(NT, W)
    xnt = arena.take(KH, NT * P)
    wd = arena.take(E, D, at=0)
    assert NT * W + KH * NT * P >= E * D
    WD_LATE = -(-NT * W // D)
    big = arena.at
    wgu = arena.take(KH, E, 2 * F)
    after_big = arena.at
    arena.at = big
    hot = [arena.take(NT * E // 2).bitcast(BF16).rearrange("p (t e) -> p t e", e=E) for _ in range(K)]
    chosen = arena.take(NT * E // 2).bitcast(BF16)
    chosen_t = chosen.rearrange("p (t e) -> p t e", e=E)
    count = arena.take(E, NT)
    before = arena.take(E, NT)
    restart = arena.take(E, NT)
    pos = arena.take(NT, E)
    picked = arena.take(NT, E)
    assert arena.at <= after_big
    arena.at = after_big
    small = arena.at
    slot = arena.take(NT, K).bitcast(I32)
    pair = arena.take(NT, K).bitcast(I32)
    gate = arena.take(NT, K)
    expert_row = arena.take(NX).bitcast(I32)
    at_experts = arena.at
    logit = arena.take(NT, E)
    choice = arena.take(NT, 8)
    sgu = arena.take(KH, 2 * SH * P)
    sd = arena.take(SH, D)
    rw = arena.take(KH, E)
    bias = arena.take(BLK, E)
    at_work = arena.at
    stats = arena.take(BLK, 6)
    moments = arena.take(BLK, 2)
    rstd = arena.take(BLK)
    xs = arena.take(BLK, D)
    xst = arena.take(KH, N)
    biased = arena.take(BLK, E)
    row_max = arena.take(BLK)
    best = arena.take(BLK, 8)
    which = arena.take(BLK, 8).bitcast(U32)
    arena.at = at_work
    total = arena.take(E)
    tiles_f = arena.take(E)
    tiles_i = arena.take(E).bitcast(I32)
    ends = arena.take(E)
    base = arena.take(E)
    gate_sum = arena.take(NT)
    slot_f = arena.take(NT)
    tile_no = arena.take(2)
    tile_expert = arena.take(2)
    tile_expert_i = arena.take(2).bitcast(I32)
    passed = arena.take(2, E)
    sg = arena.take(2, N)
    sht = arena.take(SH, N)
    arena.at = at_experts
    XRING, YRING = 8, 4
    xin = arena.take(XRING, 2, W)
    goes_to = arena.take(XRING, 2).bitcast(I32)
    xt = arena.take(2, 2 * KH * P)
    sig = arena.take(2, 2, F)
    hid = arena.take(2, 2, P)
    ht = arena.take(2, 2 * P)
    ytile = arena.take(YRING, 2, D)
    arena.at = at_experts
    G = 8
    chosen_y = arena.take(G, K, D)

    with ExitStack() as ctx:
        sem = Sems(nc, ctx, phase + "_route")
        tp = [ctx.enter_context(nc.psum_tensor(f"{phase}_tp{h}", [P, N], F32)) for h in range(KH)]
        lg = ctx.enter_context(nc.psum_tensor(f"{phase}_lg", [P, BLK, E], F32))
        ranks = ctx.enter_context(nc.psum_tensor(f"{phase}_ranks", [P, 2, BLK * E], F32))
        SUMS = K - 1
        block = ctx.enter_context(nc.Block())

        @block.sync
        def _(sp):
            sp.dma_start(rw, router_w.rearrange("(h p) n -> p h n", p=P)).then_inc(sem("rw"), 16)
            for j in range(BLK):
                sp.dma_start(bias[:, j, :], router_bias.rearrange("(o e) -> o e", o=1).to_broadcast([P, E]))\
                    .then_inc(sem("rw"), 16)
            sp.dma_start(sgu, sw_gu.rearrange("(h p) n -> p h n", p=P)).then_inc(sem("shared_w"), 16)
            sp.dma_start(sd, sw_d.rearrange("(j p) n -> p j n", p=P)).then_inc(sem("shared_w"), 16)
            sp.wait_ge(sem("shared_w"), 32)

        @block.tensor
        def _(pe):
            pe.wait_ge(sem("rw"), 16 * (1 + BLK))

            def score(n):
                for h in range(KH):
                    pe.wait_ge(sem("tp_read"), KH * n + h + 1)
                    for j in range(BLK):
                        if h == 0:
                            pe.wait_ge(sem("xs_ready"), BLK * n + j + 1)
                        last = pe.transpose(tp[h][:, j * P:(j + 1) * P], xs[:, j, h * P:(h + 1) * P], k.ident[:, :])
                    last.then_inc(sem("tp_full"), 1)
                pe.wait_ge(sem("xst_ready"), KH * n + KH)
                pe.wait_ge(sem("lg_read"), n + 1)
                for j in range(BLK):
                    for h in range(KH):
                        last = pe.matmul(lg[:, j, :], xst[:, h, j * P:(j + 1) * P], rw[:, h, :],
                                         start=h == 0, stop=h == KH - 1)
                last.then_inc(sem("lg_full"), 1)

            def rank(n):
                pe.wait_ge(sem("sum_steps"), SUMS * (n + 1))
                pe.wait_ge(sem("counts_read"), 2 * n + 2)
                here = bass.ds(n * BLK * E, BLK * E)
                pe.matmul(ranks[:, 0, :], k.tri_bf[:, :], chosen[:, here], start=True, stop=True)
                pe.matmul(ranks[:, 1, :], k.ones_bf[:, :], chosen[:, here], start=True, stop=True)\
                    .then_inc(sem("counted"), 1)

            score(0)
            with pe.Fori(1, NB) as n:
                score(n)
                rank(n - 1)
            rank(NB - 1)

        @block.scalar
        def _(act):
            act.preload_act_table(ACT.Exp)
            act.sem_inc(sem("tp_read"), KH)

            def transposed(n):
                for h in range(KH):
                    act.wait_ge(sem("tp_full"), KH * n + h + 1)
                    act.wait_ge(sem("xst_free"), n + 1)
                    act.activation(xst[:, h, :], tp[h][:, :], ACT.Copy).then_inc(sem("xst_ready"), 1)
                    act.activation(xnt[:, h, bass.ds(N * n, N)], tp[h][:, :], ACT.Copy).then_inc(sem("tp_read"), 1)
                act.activation(xn[:, bass.ds(BLK * n, BLK), 0:D], xs[:, :, :], ACT.Copy).then_inc(sem("xn_kept"), 1)

            def exp(n):
                act.wait_ge(sem("shifted"), n + 1)
                tiles = logit[:, bass.ds(BLK * n, BLK), :]
                act.activation(tiles, tiles, ACT.Exp)

            transposed(0)
            with act.Fori(1, NB) as n:
                transposed(n)
                exp(n - 1)
            exp(NB - 1)

        @block.gpsimd
        def _(pool):
            pool.memset(restart, 1.0).then_inc(sem("restart"), 1)
            pool.wait_ge(sem("restart"), 1)
            pool.memset(restart[:, :, 0:1], 0.0).then_inc(sem("restart"), 1)

            def power(n):
                pool.wait_ge(sem("var_ready"), n + 1)
                pool.tensor_tensor(rstd, rstd, k.minus_half[:, 0:BLK], ALU.pow).then_inc(sem("rstd_ready"), 1)

            def add_choices(n):
                steps = Chain(pool, sem("sum_steps"), SUMS, n)
                tiles = bass.ds(BLK * n, BLK)
                pool.wait_ge(sem("hot_ready"), K * (n + 1))
                steps.step(pool.tensor_tensor(chosen_t[:, tiles, :], hot[0][:, tiles, :], hot[1][:, tiles, :], ALU.add))
                for i in range(2, K):
                    steps.settled()
                    steps.step(pool.tensor_tensor(chosen_t[:, tiles, :], chosen_t[:, tiles, :], hot[i][:, tiles, :],
                                                  ALU.add))

            power(0)
            with pool.Fori(0, NB - 1) as n:
                power(n + 1)
                add_choices(n)
            add_choices(NB - 1)
            pool.wait_ge(sem("sum_steps"), SUMS * NB)
            pool.wait_ge(sem("restart"), 2)

        @block.vector
        def _(dve):
            dve.sem_inc(sem("counts_read"), 2)
            dve.sem_inc(sem("lg_read"), 1)
            dve.sem_inc(sem("xst_free"), 1)

            def normalise(n):
                steps = Chain(dve, sem("ln_steps"), 2 * BLK + 1, n)
                for j in range(BLK):
                    steps.step(dve.bn_stats(stats[:, j, :], one_tile(k.res, BLK * n + j)))
                steps.settled()
                dve.sem_inc(sem("stats_complete"), 1)
                for j in range(BLK):
                    steps.step(dve.bn_aggr(moments[:, j, :], stats[:, j, :]))
                steps.settled()
                steps.step(dve.tensor_scalar(rstd, moments[:, :, 1], EPS, None, ALU.add))
                steps.settled()
                dve.sem_inc(sem("var_ready"), 1)
                dve.wait_ge(sem("rstd_ready"), n + 1)
                dve.wait_ge(sem("xs_free"), n + 1)
                for j in range(BLK):
                    dve.tensor_scalar(xs[:, j, :], one_tile(k.res, BLK * n + j), moments[:, j, 0:1], rstd[:, j:j + 1],
                                      ALU.subtract, ALU.mult).then_inc(sem("xs_ready"), 1)

            def choose(n):
                steps = Chain(dve, sem("top_steps"), 2 * BLK + 4, n)
                tiles = bass.ds(BLK * n, BLK)
                dve.wait_ge(sem("lg_full"), n + 1)
                steps.step(dve.tensor_tensor(biased, lg[:, :, :], bias, ALU.add))
                steps.step(dve.tensor_reduce(row_max, lg[:, :, :], AX_X, ALU.max))
                steps.settled()
                dve.sem_inc(sem("biased_complete"), 1)
                steps.step(dve.tensor_tensor(logit[:, tiles, :], lg[:, :, :],
                                             row_max.unsqueeze(2).to_broadcast([P, BLK, E]), ALU.subtract))
                for j in range(BLK):
                    steps.step(dve.max(best[:, j, :], biased[:, j, :]))
                steps.settled()
                dve.sem_inc(sem("lg_read"), 1)
                dve.sem_inc(sem("xst_free"), 1)
                dve.sem_inc(sem("shifted"), 1)
                for j in range(BLK):
                    steps.step(dve.max_index(which[:, j, :], best[:, j, :], biased[:, j, :]))
                steps.settled()
                dve.sem_inc(sem("which_complete"), 1)
                steps.step(dve.tensor_copy(choice[:, tiles, :], which))
                steps.settled()
                for i in range(K):
                    dve.tensor_tensor(hot[i][:, tiles, :], k.iota64[:, 0:E].unsqueeze(1).to_broadcast([P, BLK, E]),
                                      choice[:, tiles, i:i + 1].to_broadcast([P, BLK, E]), ALU.is_equal)\
                        .then_inc(sem("hot_ready"), 1)

            def keep_counts(n):
                tiles = bass.ds(BLK * n, BLK)
                dve.wait_ge(sem("counted"), n + 1)
                dve.tensor_copy(pos[:, tiles, :], ranks[:, 0, :].rearrange("p (t e) -> p t e", e=E))\
                    .then_inc(sem("counts_read"), 1)
                dve.tensor_copy(count[:, :, tiles], ranks[:, 1, :].rearrange("p (t e) -> p e t", e=E))\
                    .then_inc(sem("counts_read"), 1)

            def xs_is_free(n):
                dve.wait_ge(sem("tp_full"), KH * n + KH)
                dve.wait_ge(sem("xn_kept"), n + 1)
                dve.sem_inc(sem("xs_free"), 1)

            dve.sem_inc(sem("xs_free"), 1)
            normalise(0)
            xs_is_free(0)
            normalise(1)
            choose(0)
            with dve.Fori(1, NB - 1) as n:
                xs_is_free(n)
                normalise(n + 1)
                choose(n)
                keep_counts(n - 1)
            choose(NB - 1)
            keep_counts(NB - 2)
            keep_counts(NB - 1)
            dve.wait_ge(sem("top_steps"), NB * (2 * BLK + 4))
            dve.wait_ge(sem("counts_read"), 2 + 2 * NB)

    with ExitStack() as ctx:
        sem = Sems(nc, ctx, phase + "_disp")
        ps = [ctx.enter_context(nc.psum_tensor(f"{phase}_d{i}", [P, N], F32)) for i in range(8)]
        gate_ps, up_ps = ps[0:2], ps[2:4]
        down_ps = [x[:, :].rearrange("p (j d) -> p j d", d=D) for x in ps[4:6]]
        block = ctx.enter_context(nc.Block())

        @block.tensor
        def _(pe):
            with pe.Fori(0, NB) as n:
                for j in range(SH):
                    pe.wait_ge(sem("sht_ready"), SH * n + j + 1)
                    for bank, at in ((gate_ps[j % 2], j * P), (up_ps[j % 2], (SH + j) * P)):
                        for h in range(KH):
                            last = pe.matmul(bank[:, :], sgu[:, h, at:at + P], xnt[:, h, bass.ds(N * n, N)],
                                             start=h == 0, stop=h == KH - 1)
                    last.then_inc(sem("gu_full"), 1)
                for j, ms in ((0, range(SH - 1)), (2, range(SH - 1)), (0, [SH - 1]), (1, range(SH)),
                              (2, [SH - 1]), (3, range(SH))):
                    if ms[0] == 0 and j % 2 == 0:
                        pe.wait_ge(sem("down_read"), 2 * n + j // 2 + 1)
                    pe.wait_ge(sem("sht_ready"), 2 + SH * n + ms[-1] + 1)
                    for m in ms:
                        last = pe.matmul(down_ps[j // 2][:, j % 2, :], sht[:, m, j * P:(j + 1) * P], sd[:, m, :],
                                         start=m == 0, stop=m == SH - 1, skip_group_check=True)
                    if j % 2 == 1:
                        last.then_inc(sem("down_full"), 1)

        @block.scalar
        def _(act):
            act.preload_act_table(ACT.Silu)
            act.sem_inc(sem("sg_free"), 2)
            with act.Fori(0, NB) as n:
                for j in range(SH):
                    act.wait_ge(sem("gu_full"), SH * n + j + 1)
                    act.wait_ge(sem("sht_ready"), SH * n + j + 1)
                    act.activation(sg[:, j % 2, :], gate_ps[j % 2][:, :], ACT.Silu).then_inc(sem("sg_ready"), 1)

        @block.vector
        def _(dve):
            dve.sem_inc(sem("sht_ready"), 2)
            dve.sem_inc(sem("down_read"), 2)

            def multiply(n, j):
                dve.wait_ge(sem("sg_ready"), SH * n + j + 1)
                dve.tensor_tensor(sht[:, j, :], sg[:, j % 2, :], up_ps[j % 2][:, :], ALU.mult)\
                    .then_inc(sem("sht_ready"), 1)

            def add_down(n):
                for j in range(2):
                    dve.wait_ge(sem("down_full"), 2 * n + j + 1)
                    tiles = k.res[:, bass.ds(BLK * n + 2 * j, 2), :]
                    dve.tensor_tensor(tiles, tiles, down_ps[j], ALU.add).then_inc(sem("down_read"), 1)

            c = Chain(dve, sem("steps"))
            c.link(dve.tensor_tensor_scan(before.rearrange("p e t -> p (e t)"), restart.rearrange("p e t -> p (e t)"),
                                          count.rearrange("p e t -> p (e t)"), 0.0, ALU.mult, ALU.add))
            c.link(dve.tensor_scalar(tiles_i, before[:, :, NT - 1], float(P - 1), None, ALU.add))
            c.link(dve.tensor_scalar(tiles_i, tiles_i, P.bit_length() - 1, None, ALU.logical_shift_right))
            c.link(dve.tensor_copy(tiles_f, tiles_i))
            c.link(dve.tensor_tensor_scan(ends, restart[:, 0, 1:2].to_broadcast([P, E]), tiles_f, 0.0,
                                          ALU.mult, ALU.add))
            c.link(dve.tensor_tensor(base, ends, tiles_f, ALU.subtract))
            c.link(dve.tensor_scalar(base, base, float(P), None, ALU.mult))
            c.link(dve.tensor_tensor(before, before, count, ALU.subtract))
            c.link(dve.tensor_tensor(before, before, base.unsqueeze(2).to_broadcast([P, E, NT]), ALU.add))
            c.link(dve.tensor_tensor(pos, pos, before.rearrange("p e t -> p t e"), ALU.add))
            multiply(0, 0)
            for i in range(K):
                c.link(dve.tensor_tensor(picked, hot[i], pos, ALU.mult))
                c.link(dve.tensor_reduce(slot_f, picked, AX_X, ALU.add))
                c.link(dve.tensor_copy(slot[:, :, i], slot_f))
                dve.sem_inc(sem("slots_ready"), 1)
                if i == 0:
                    multiply(0, 1)
                    multiply(0, 2)
                if i == 1:
                    multiply(0, 3)
                if i == 2:
                    add_down(0)
                if i == 3:
                    multiply(1, 0)
                    multiply(1, 1)
            dve.wait_ge(sem("tile_no"), 1)
            HALF = NX // 2
            c.link(dve.tensor_tensor(passed[0:HALF], tile_no[0:HALF].unsqueeze(2).to_broadcast([HALF, 2, E]),
                                     ends[0:HALF].unsqueeze(1).to_broadcast([HALF, 2, E]), ALU.is_ge))
            c.link(dve.tensor_reduce(tile_expert[0:HALF], passed[0:HALF], AX_X, ALU.add))
            c.link(dve.tensor_scalar(tile_expert_i[0:HALF], tile_expert[0:HALF], float(E - 1), None, ALU.min))
            dve.sem_inc(sem("tile_expert"), 1)
            for i in range(K):
                c.link(dve.tensor_tensor(picked, hot[i], logit, ALU.mult))
                c.link(dve.tensor_reduce(gate[:, :, i], picked, AX_X, ALU.add))
                if i == 0:
                    multiply(1, 2)
                if i == 1:
                    multiply(1, 3)
            c.link(dve.tensor_reduce(gate_sum, gate, AX_X, ALU.add))
            c.link(dve.reciprocal(gate_sum, gate_sum))
            c.link(dve.tensor_tensor(gate, gate, gate_sum.unsqueeze(2).to_broadcast([P, NT, K]), ALU.mult))
            dve.sem_inc(sem("dispatched"), 1)
            add_down(1)
            with dve.Fori(2, NB) as n:
                for j in range(SH):
                    multiply(n, j)
                add_down(n)
            dve.wait_ge(sem("down_read"), 2 + 2 * NB)

        @block.sync
        def _(sp):
            sp.wait_ge(sem("tile_expert"), 1)
            sp.dma_start(slots.expert.rearrange("(p j) -> p j", j=2), tile_expert_i[0:NX // 2])\
                .then_inc(sem("expert_out"), 16)
            sp.wait_ge(sem("expert_out"), 16)
            sp.dma_start(expert_row[0:1], slots.expert.rearrange("(o n) -> o n", o=1)).then_inc(sem("expert_in"), 16)
            sp.wait_ge(sem("dispatched"), 1)
            sp.dma_start(wgu, w_gu.rearrange("(h p) e n -> p h e n", p=P)).then_inc(sem("wgu"), 16)
            sp.wait_ge(sem("gu_full"), SH * NB)
            sp.dma_start(wd[0:F, WD_LATE:E], w_d[WD_LATE:E].rearrange("e f d -> f e d")).then_inc(sem("wd_first"), 16)
            sp.wait_ge(sem("expert_in"), 16)
            sp.wait_ge(sem("wgu"), 16)
            sp.wait_ge(sem("wd_first"), 16)

        @block.gpsimd
        def _(pool):
            pool.iota(tile_no[0:NX // 2], [[1, 2]], base=0, channel_multiplier=2,
                      allow_small_or_imprecise_dtypes=True).then_inc(sem("tile_no_made"), 1)
            pool.wait_ge(sem("tile_no_made"), 1)
            pool.sem_inc(sem("tile_no"), 1)
            pool.wait_ge(k.slots_zeroed, zeroed)
            pool.iota(pair, [[K * P, NT], [1, K]], base=0, channel_multiplier=K).then_inc(sem("pair"), 1)
            pool.memset(xn[:, :, D + 1:W], 0.0).then_inc(sem("pair"), 1)
            pool.wait_ge(sem("pair"), 2)
            HALF = NT // 2
            for i in range(K):
                pool.wait_ge(sem("slots_ready"), i + 1)
                for half in range(2):
                    if i:
                        pool.wait_ge(sem(f"scattered{half}"), 16 * HALF * i)
                    tiles = slice(half * HALF, (half + 1) * HALF)
                    pool.tensor_copy(xn[:, tiles, D:D + 1].bitcast(I32), pair[:, tiles, i:i + 1])\
                        .then_inc(sem("numbered"), 1)
                    pool.wait_ge(sem("numbered"), 2 * i + half + 1)
                    for t in range(half * HALF, (half + 1) * HALF):
                        pool.indirect_dma_start(out=slots.x, in_=xn[:, t, :], in_offset=None,
                                                out_offset=bass.IndirectOffsetOnAxis(ap=slot[:, t, i:i + 1], axis=0))\
                            .then_inc(sem(f"scattered{half}"), 16)
            for half in range(2):
                pool.wait_ge(sem(f"scattered{half}"), 16 * K * HALF)

    with ExitStack() as ctx:
        sem = Sems(nc, ctx, phase + "_exp")
        xt_ps, h_ps, ht_ps, y_ps = [[ctx.enter_context(nc.psum_tensor(f"{phase}_{g}{i}", [P, 512], F32))
                                     for i in range(2)] for g in ("ext", "eh", "eht", "ey")]
        x_v = slots.x.rearrange("(s t p) d -> s p t d", p=P, t=2)
        NP = NX // 2
        RING = XRING
        LAG = 3
        assert NP % RING == 0
        block = ctx.enter_context(nc.Block())

        def all_steps(engine, step, lag):
            for s in range(RING):
                step(0, s, s)
            with engine.Fori(1, NP // RING) as g:
                for r in range(RING):
                    step(g, r, None)
            for s in range(NP, NP + lag):
                step(s // RING, s % RING, s)

        def pair_of(g, r, s, back):
            if s is not None and not 0 <= s - back < NP:
                return None
            turn = g if r >= back else g - 1
            place = (r - back) % RING
            return RING * turn + place, turn, place

        @block.sync
        def _(sp):
            sp.dma_start(wd[0:F, 0:WD_LATE], w_d[0:WD_LATE].rearrange("e f d -> f e d")).then_inc(sem("wd"), 16)

            def step(g, r, s):
                n, _, place = pair_of(g, r, s, 0)
                if s is None:
                    sp.wait_ge(sem("xt_full"), n + 1 - XRING)
                    sp.wait_ge(sem("numbers_kept"), n + 1 - XRING)
                sp.dma_start(xin[:, place], x_v[bass.ds(n, 1)].rearrange("s p t d -> p (s t) d"))\
                    .then_inc(sem(f"x_in{place}"), 16)

            all_steps(sp, step, 0)
            for place in range(YRING):
                sp.wait_ge(sem(f"y_out{place}"), 32 * NP // YRING)

        @block.gpsimd
        def _(pool):
            for n in range(NP):
                pool.wait_ge(sem("numbers_kept"), n + 1)
                pool.wait_ge(sem("y_read"), 2 + n + 1)
                for j in range(2):
                    pool.indirect_dma_start(
                        out=slots.y, in_=ytile[:, n % YRING, j, :], in_offset=None, bounds_check=slots.pairs - 1,
                        oob_is_err=False, out_offset=bass.IndirectOffsetOnAxis(
                            ap=goes_to[:, n % XRING, j:j + 1], axis=0))\
                        .then_inc(sem(f"y_out{n % YRING}"), 16)

        @block.tensor
        def _(pe):
            pe.wait_ge(sem("wd"), 16)

            held = {}

            def load_experts(g, pairs):
                row = expert_row[0:1, bass.ds(2 * (RING * g + pairs[0]), 2 * len(pairs))]
                _, values = nc.values_load_multi_w_load_instructions(
                    row, engines=[mybir.EngineType.PE], min_val=0, max_val=E - 1,
                    skip_runtime_bounds_check_because="tile_expert is a count of experts, cut off at E - 1")
                for at, pair in enumerate(pairs):
                    held[pair] = values[2 * at:2 * at + 2]

            def step(g, r, s):
                if r == 0 and s != 0:
                    load_experts(g, range(-LAG, 0))
                if r == 0 and (s is None or s < NP):
                    load_experts(g, range(0, 4))
                if r == 5:
                    load_experts(g, range(4, RING - 1))
                pair = pair_of(g, r, s, 0)
                if pair is not None:
                    n, turn, place = pair
                    pe.wait_ge(sem(f"x_in{place}"), 16 * turn + 16)
                    pe.wait_ge(sem("xt_read"), n + 1)
                    for j in range(2):
                        for h in range(KH):
                            last = pe.transpose(xt_ps[place % 2][:, (j * KH + h) * P:(j * KH + h + 1) * P],
                                                xin[:, place, j, h * P:(h + 1) * P], k.ident[:, :])
                    last.then_inc(sem("xt_full"), 1)
                pair = pair_of(g, r, s, 1)
                if pair is not None:
                    n, turn, place = pair
                    expert = held[r - 1]
                    pe.wait_ge(sem("xt_read"), 2 + n + 1)
                    pe.wait_ge(sem("hid_ready"), n + 1)
                    for j in range(2):
                        for h in range(KH):
                            last = pe.matmul(h_ps[place % 2][:, j * 2 * F:(j + 1) * 2 * F],
                                             xt[:, place % 2, (j * KH + h) * P:(j * KH + h + 1) * P],
                                             wgu[:, h].rearrange("p e n -> p (e n)")[:, bass.ds(expert[j] * (2 * F), 2 * F)],
                                             start=h == 0, stop=h == KH - 1)
                    last.then_inc(sem("h_full"), 1)
                pair = pair_of(g, r, s, 2)
                if pair is not None:
                    n, turn, place = pair
                    pe.wait_ge(sem("hid_ready"), 2 + n + 1)
                    pe.wait_ge(sem("ht_read"), n + 1)
                    for j in range(2):
                        last = pe.transpose(ht_ps[place % 2][:, j * P:(j + 1) * P], hid[:, place % 2, j, :], k.ident[:, :])
                    last.then_inc(sem("ht_full"), 1)
                pair = pair_of(g, r, s, 3)
                if pair is not None:
                    n, turn, place = pair
                    expert = held[r - 3]
                    pe.wait_ge(sem("ht_read"), 2 + n + 1)
                    pe.wait_ge(sem("y_read"), n + 1)
                    for j in range(2):
                        last = pe.matmul(y_ps[place % 2][:, j * D:(j + 1) * D], ht[0:F, place % 2, j * P:(j + 1) * P],
                                         wd[0:F].rearrange("f e d -> f (e d)")[:, bass.ds(expert[j] * D, D)],
                                         start=True, stop=True)
                    last.then_inc(sem("y_full"), 1)

            all_steps(pe, step, LAG)

        @block.scalar
        def _(act):
            act.preload_act_table(ACT.Silu)
            act.sem_inc(sem("xt_read"), 2)
            act.sem_inc(sem("ht_read"), 2)

            def step(g, r, s):
                pair = pair_of(g, r, s, 0)
                if pair is not None:
                    n, turn, place = pair
                    act.wait_ge(sem("xt_full"), n + 1)
                    if s is None or s >= 2:
                        act.wait_ge(sem("h_full"), n - 1)
                    act.activation(xt[:, place % 2], xt_ps[place % 2][:, :], ACT.Copy).then_inc(sem("xt_read"), 1)
                pair = pair_of(g, r, s, 1)
                if pair is not None:
                    n, turn, place = pair
                    act.wait_ge(sem("h_full"), n + 1)
                    act.wait_ge(sem("hid_ready"), n + 1)
                    act.activation(sig[:, place % 2], h_ps[place % 2][:, 0:4 * F].rearrange("p (j n) -> p j n", j=2)[:, :, 0:F],
                                   ACT.Silu).then_inc(sem("sig_ready"), 1)
                pair = pair_of(g, r, s, 2)
                if pair is not None:
                    n, turn, place = pair
                    act.wait_ge(sem("ht_full"), n + 1)
                    if s is None or s >= 4:
                        act.wait_ge(sem("y_full"), n - 1)
                    act.activation(ht[0:F, place % 2], ht_ps[place % 2][0:F, 0:2 * P], ACT.Copy).then_inc(sem("ht_read"), 1)

            all_steps(act, step, 2)

        @block.vector
        def _(dve):
            dve.memset(hid, 0.0).then_inc(sem("hid_cleared"), 1)
            dve.wait_ge(sem("hid_cleared"), 1)
            dve.sem_inc(sem("hid_ready"), 2)
            dve.sem_inc(sem("y_read"), 2)

            def step(g, r, s):
                pair = pair_of(g, r, s, 1)
                if pair is not None:
                    n, turn, place = pair
                    dve.wait_ge(sem(f"x_in{place}"), 16 * turn + 16)
                    dve.tensor_copy(goes_to[:, place, :], xin[:, place, :, D].bitcast(I32)).then_inc(sem("numbers_kept"), 1)
                    dve.wait_ge(sem("sig_ready"), n + 1)
                    if s is None or s >= 3:
                        dve.wait_ge(sem("ht_full"), n - 1)
                    dve.tensor_tensor(hid[:, place % 2, :, 0:F], sig[:, place % 2],
                                      h_ps[place % 2][:, 0:4 * F].rearrange("p (j n) -> p j n", j=2)[:, :, F:2 * F],
                                      ALU.mult).then_inc(sem("hid_ready"), 1)
                pair = pair_of(g, r, s, 3)
                if pair is not None:
                    n, turn, place = pair
                    dve.wait_ge(sem("y_full"), n + 1)
                    if s is None or s >= YRING + 3:
                        dve.wait_ge(sem(f"y_out{place % YRING}"), 32 * (RING // YRING * turn + place // YRING))
                    dve.tensor_copy(ytile[:, place % YRING].rearrange("p j d -> p (j d)"), y_ps[place % 2][:, :])\
                        .then_inc(sem("y_read"), 1)

            all_steps(dve, step, LAG)

    with ExitStack() as ctx:
        sem = Sems(nc, ctx, phase + "_sum")
        y_v = slots.y.rearrange("(t p i) d -> t p i d", p=P, i=K)
        block = ctx.enter_context(nc.Block())

        @block.vector
        def _(dve):
            with dve.Fori(0, NT // G) as g:
                for r in range(0, G, 2):
                    for i in range(K):
                        for j in range(2):
                            t = G * g + r + j
                            if i == 0:
                                dve.wait_ge(sem(f"in{r + j}"), 16 * g + 16)
                            else:
                                dve.wait_ge(sem("added"), K * G * g + K * r + 2 * i + j - 1)
                            dve.scalar_tensor_tensor(one_tile(k.res, t), chosen_y[:, r + j, i, :],
                                                     gate[:, bass.ds(t, 1), i:i + 1].rearrange("p o i -> p (o i)"),
                                                     one_tile(k.res, t), ALU.mult, ALU.add).then_inc(sem("added"), 1)

        @block.sync
        def _(sp):
            OUTS = NT // G
            view = None if out is None else out.rearrange("b (t p) c -> p (b t) c", p=P)
            for t in range(NT):
                if t >= G:
                    sp.wait_ge(sem("added"), K * 2 * ((t - G) // 2 + 1))
                sp.dma_start(chosen_y[:, t % G], y_v[t]).then_inc(sem(f"in{t % G}"), 16)
            if out is not None:
                for g in range(OUTS):
                    tiles = slice(g * G, (g + 1) * G)
                    sp.wait_ge(sem("added"), K * G * (g + 1))
                    sp.dma_start(view[:, tiles, :], k.res[:, tiles, :]).then_inc(sem("stored"), 16)
                sp.wait_ge(sem("stored"), 16 * OUTS)




def retention(nc, k, w_qk, w_vg, w_o, b_q, b_k, b_vg, b_o, gn_w, gn_b, gamma, batches):
    B = batches
    NT, D = k.res.shape[1], k.res.shape[2]
    TB = NT // B
    HEADS = gamma.shape[0]
    DH = D // HEADS
    CH = D // P
    HC = HEADS // CH
    GR = 4
    BLK = 4
    N = BLK * P
    H = TB // BLK
    COUNT = float(TB * P * DH)
    assert DH * 2 * GR == P and H == 2 and CH == 2

    arena = k.arena
    arena.at = 0
    wqk = arena.take(CH, 2 * D)
    wvg = arena.take(CH, 2 * D)
    wo = arena.take(CH, D)
    bias_qk = arena.take(2, CH)
    bias_vg = arena.take(2 * D)
    bias_o = arena.take(D)
    gnw = arena.take(D)
    gnb = arena.take(D)
    decay = arena.take(GR, CH, 2, P)
    q_decay = arena.take(CH, P)
    powers = arena.take(2 * P + 1)
    parity = arena.take(2)
    row_i = arena.take(1).bitcast(I32)
    blocks = arena.take(P)
    stats = arena.take(BLK, 6)
    moments = arena.take(BLK, 2)
    rstd = arena.take(BLK)
    xn = arena.take(TB, D)
    xnt = arena.take(H, CH, N)
    qt = arena.take(CH, TB * P)
    qst = arena.take(CH, TB * P)
    kt = arena.take(CH, TB * P)
    ktp = arena.take(2, CH, TB * P)
    vg = arena.take(TB, 2 * D)
    gates = arena.take(NT, D)
    kd = arena.take(2, D)
    masked_at = arena.at
    masked = arena.take(2, GR, 4 * P)
    turned = arena.take(GR, CH, 2, P, at=masked_at)
    reverse = arena.take(P, at=masked_at + GR * 4 * P)
    state = arena.take(2, CH, P)
    update = arena.take(CH, P)
    ret = arena.take(TB, D)
    square = arena.take(TB, D, at=masked_at)
    sums = arena.take(HEADS)
    group_scale = arena.take(HEADS)
    scale = arena.take(D)
    rnt = arena.take(2, 2, CH, P)
    powers_dram = nc.dram_tensor("gamma_powers", (HEADS, 2 * P + 1), F32, kind="Internal").ap()

    with ExitStack() as ctx:
        sem = Sems(nc, ctx, "ret")

        def bank(name):
            return ctx.enter_context(nc.psum_tensor(f"ret_{name}", [P, N], F32))

        tp, rt = bank("tp"), bank("rt")
        pj = [bank(f"pj{i}") for i in range(2)]
        sc = [bank(f"sc{g}") for g in range(GR)]

        TP_CHUNKS, TP_TURN = 2 * TB - 1, 2 * TB - 1 + 2 * H + TB // 2

        def tp_chunks(b):
            return 2 * H + TP_TURN * b

        def tp_project(b, first):
            return 0 if first else 2 * H + TP_TURN * (b - 1) + TP_CHUNKS

        def tp_output(b, last):
            return 2 * H + TP_TURN * b + TP_CHUNKS + (0 if last else 2 * H)

        PJ_TURN = H * (2 * CH + BLK)
        RT_TURN = TB + 2 + TB // 2
        block = ctx.enter_context(nc.Block())

        @block.sync
        def _(sp):
            def rows(dst, src, width):
                sp.dma_start(dst, src.rearrange("(o n) -> o n", o=1).to_broadcast([P, width])).then_inc(sem("w"), 16)

            sp.dma_start(powers[0:HEADS, P + 1:P + 2], gamma.rearrange("(h o) -> h o", o=1),
                         allow_slow_non_contiguous=True).then_inc(sem("gamma"), 16)
            sp.dma_start(wqk, w_qk.rearrange("(h p) n -> p h n", p=P)).then_inc(sem("w"), 16)
            sp.dma_start(wvg, w_vg.rearrange("(h p) n -> p h n", p=P)).then_inc(sem("w"), 16)
            sp.dma_start(wo, w_o.rearrange("(h p) n -> p h n", p=P)).then_inc(sem("w"), 16)
            sp.dma_start(bias_qk[:, 0, :], b_q.rearrange("(h p) -> p h", p=P), allow_slow_non_contiguous=True)\
                .then_inc(sem("w"), 16)
            sp.dma_start(bias_qk[:, 1, :], b_k.rearrange("(h p) -> p h", p=P), allow_slow_non_contiguous=True)\
                .then_inc(sem("w"), 16)
            rows(bias_vg, b_vg, 2 * D)
            rows(bias_o, b_o, D)
            rows(gnw, gn_w, D)
            rows(gnb, gn_b, D)
            sp.wait_ge(sem("powers"), 1)
            sp.dma_start(powers_dram, powers[0:HEADS, :]).then_inc(sem("powers_out"), 16)
            sp.wait_ge(sem("powers_out"), 16)
            W = 2 * P + 1
            for c in range(CH):
                for par in range(2):
                    src = bass.AP(tensor=powers_dram.tensor, offset=(c * HC + par) * W + 1,
                                  ap=[[1, P], [2 * W, GR], [1, P]])
                    sp.dma_start(turned[:, :, c, par, :], src).then_inc(sem("decay"), 16)
                src = bass.AP(tensor=powers_dram.tensor, offset=c * HC * W + P + 1, ap=[[W, HC], [0, DH], [1, P]])
                sp.dma_start(q_decay[:, c, :], src).then_inc(sem("decay"), 16)
            sp.wait_ge(sem("decay"), 16 * 3 * CH)
            k.zero_slots(sp)

        @block.tensor
        def _(pe):
            pe.wait_ge(sem("w"), 16 * 9)

            def project(b, h, first=False):
                at = tp_project(b, first) + CH * h
                for c in range(CH):
                    pe.wait_ge(sem("tp_read"), at + c + 1)
                    for j in range(BLK):
                        if c == 0:
                            pe.wait_ge(sem("xn_ready"), TB * b + BLK * h + j + 1)
                        last = pe.transpose(tp[:, j * P:(j + 1) * P], xn[:, BLK * h + j, c * P:(c + 1) * P], k.ident[:, :])
                    last.then_inc(sem("tp_full"), 1)
                pe.wait_ge(sem("xnt_ready"), CH * (H * b + h + 1))
                use = PJ_TURN * b + (2 * CH + BLK) * h
                for m in range(2 * CH):
                    pe.wait_ge(sem("pj_read"), use + m + 1)
                    for c in range(CH):
                        last = pe.matmul(pj[m % 2][:, :], wqk[:, c, m * P:(m + 1) * P], xnt[:, h, c, :],
                                         start=c == 0, stop=c == CH - 1)
                    last.then_inc(sem("pj_full"), 1)
                for j in range(BLK):
                    pe.wait_ge(sem("pj_read"), use + 2 * CH + j + 1)
                    for c in range(CH):
                        last = pe.matmul(pj[j % 2][:, :], xnt[:, h, c, j * P:(j + 1) * P], wvg[:, c, :],
                                         start=c == 0, stop=c == CH - 1)
                    last.then_inc(sem("pj_full"), 1)

            def chunks(b):
                def output_of(j):
                    pe.wait_ge(sem("rt_read"), RT_TURN * b + j + 1)
                    pe.wait_ge(sem("masked_ready"), GR * (TB * b + j + 1))
                    if j:
                        pe.wait_ge(sem("state_ready"), TB * b + j + 1)
                        pe.wait_ge(sem("qst_ready"), CH * H * b + CH * (j // BLK + 1))
                    for c in range(CH):
                        cols = slice(c * P, (c + 1) * P)
                        if j:
                            pe.matmul(rt[:, cols], qst[:, c, j * P:(j + 1) * P], state[:, j % 2, c, :],
                                      start=True, stop=False, skip_group_check=True)
                        for g in range(GR):
                            for par in range(2):
                                head = c * HC + 2 * g + par
                                cols = slice(head * DH, (head + 1) * DH)
                                last = pe.matmul(rt[:, cols], masked[:, j % 2, g, (2 * c + par) * P:(2 * c + par + 1) * P],
                                                 vg[:, j, cols], start=j == 0, stop=True, skip_group_check=True)
                    last.then_inc(sem("rt_full"), 1)

                pe.wait_ge(sem("pj_read"), 2 + PJ_TURN * (b + 1))
                pe.wait_ge(sem("ktp_ready"), CH * H * (b + 1))
                for j in range(TB):
                    here = slice(j * P, (j + 1) * P)
                    pe.wait_ge(sem("tp_read"), tp_chunks(b) + 2 * j + 1)
                    for c in range(CH):
                        last = pe.transpose(tp[:, c * P:(c + 1) * P], kt[:, c, here], k.ident[:, :])
                    last.then_inc(sem("tp_full"), 1)
                    for g in range(GR):
                        pe.wait_ge(sem("sc_read"), GR * (TB * b + j) + g + 1)
                        rows = slice(32 * g, 32 * (g + 1))
                        for c in range(CH):
                            for par in range(2):
                                last = pe.matmul(sc[g][:, (2 * c + par) * P:(2 * c + par + 1) * P],
                                                 ktp[rows, par, c, here], qt[rows, c, here], start=True, stop=True)
                        last.then_inc(sem("sc_full"), 1)
                    if j:
                        output_of(j - 1)
                    if j < TB - 1:
                        pe.wait_ge(sem("tp_read"), tp_chunks(b) + 2 * j + 2)
                        for c in range(CH):
                            cols = slice(c * P, (c + 1) * P)
                            last = pe.matmul(tp[:, 2 * P + c * P:2 * P + (c + 1) * P], kd[:, j % 2, cols], vg[:, j, cols],
                                             start=True, stop=True)
                        last.then_inc(sem("tp_full"), 1)
                output_of(TB - 1)

            def group_sum(b, i, src, ready):
                pe.wait_ge(sem("rt_read"), RT_TURN * b + TB + i + 1)
                pe.wait_ge(ready, b + 1)
                for j in range(TB):
                    last = pe.matmul(rt[:, 0:D], k.ones[:, :], src[:, j, :], start=j == 0, stop=j == TB - 1)
                last.then_inc(sem("rt_full"), 1)

            def output(b, last_one=False):
                def project_pair(i):
                    pe.wait_ge(sem("rt_read"), RT_TURN * b + TB + 2 + i + 1)
                    pe.wait_ge(sem("rnt_ready"), TB // 2 * b + i + 1)
                    for j in range(2):
                        for c in range(CH):
                            last = pe.matmul(rt[:, j * D:(j + 1) * D], rnt[:, i % 2, j, c, :], wo[:, c, :],
                                             start=c == 0, stop=c == CH - 1)
                    last.then_inc(sem("rt_full"), 1)

                pe.wait_ge(sem("gated"), b + 1)
                for i in range(TB // 2):
                    pe.wait_ge(sem("tp_read"), tp_output(b, last_one) + i + 1)
                    for j in range(2):
                        for c in range(CH):
                            last = pe.transpose(tp[:, (2 * j + c) * P:(2 * j + c + 1) * P],
                                                ret[:, 2 * i + j, c * P:(c + 1) * P], k.ident[:, :])
                    last.then_inc(sem("tp_full"), 1)
                    if i:
                        project_pair(i - 1)
                project_pair(TB // 2 - 1)

            project(0, 0, first=True)
            project(0, 1, first=True)
            pe.wait_ge(sem("decay"), 16 * 3 * CH)
            pe.wait_ge(sem("reverse"), 2)
            for g in range(GR):
                pe.matmul(sc[g][:, :], reverse, turned[:, g].rearrange("p c q n -> p (c q n)"), start=True, stop=True)\
                    .then_inc(sem("decay_turned"), 1)
            with pe.Fori(0, B - 1) as b:
                chunks(b)
                group_sum(b, 0, ret, sem("ret_kept"))
                project(b + 1, 0)
                group_sum(b, 1, square, sem("squared"))
                project(b + 1, 1)
                output(b)
            chunks(B - 1)
            group_sum(B - 1, 0, ret, sem("ret_kept"))
            group_sum(B - 1, 1, square, sem("squared"))
            output(B - 1, last_one=True)

        @block.scalar
        def _(act):
            act.preload_act_table(ACT.Silu)
            act.wait_ge(sem("w"), 16 * 9)
            act.sem_inc(sem("pj_read"), 2)

            def project(b, h, first=False):
                at = tp_project(b, first) + CH * h
                for c in range(CH):
                    act.wait_ge(sem("tp_full"), at + c + 1)
                    act.activation(xnt[:, h, c, :], tp[:, :], ACT.Copy).then_inc(sem("tp_read"), 1)
                    act.wait_ge(sem("tp_read"), at + c + 2)
                    act.sem_inc(sem("xnt_ready"), 1)
                use = PJ_TURN * b + (2 * CH + BLK) * h
                for m in range(2 * CH):
                    act.wait_ge(sem("pj_full"), use + m + 1)
                    dst = (qt if m < CH else kt)[:, m % CH, h * N:(h + 1) * N]
                    act.activation(dst, pj[m % 2][:, :], ACT.Identity, bias=bias_qk[:, m // CH, m % CH:m % CH + 1])\
                        .then_inc(sem("pj_read"), 1)
                for j in range(BLK):
                    act.wait_ge(sem("pj_read"), 2 + use + 2 * CH + j + 1)
                    act.sem_inc(sem("gate_in"), 1)
                    t = BLK * h + j
                    act.activation(one_tile(gates, TB * b + t), vg[:, t, D:2 * D], ACT.Silu).then_inc(sem("gates"), 1)

            def chunks(b):
                for j in range(TB):
                    act.wait_ge(sem("rt_full"), RT_TURN * b + j + 1)
                    act.activation(ret[:, j, :], rt[:, 0:D], ACT.Copy).then_inc(sem("rt_read"), 1)
                act.wait_ge(sem("rt_read"), 1 + RT_TURN * b + TB)
                act.sem_inc(sem("ret_kept"), 1)

            def squares(b):
                act.wait_ge(sem("centred"), b + 1)
                act.activation(square, ret, ACT.Square).then_inc(sem("squared"), 1)

            def output(b, last_one=False):
                for i in range(TB // 2):
                    act.wait_ge(sem("tp_full"), tp_output(b, last_one) + i + 1)
                    act.activation(rnt[:, i % 2].rearrange("p j c n -> p (j c n)"), tp[:, :], ACT.Copy)\
                        .then_inc(sem("tp_read"), 1)
                    act.wait_ge(sem("tp_read"), tp_output(b, last_one) + i + 2)
                    act.sem_inc(sem("rnt_ready"), 1)

            project(0, 0, first=True)
            project(0, 1, first=True)
            for g in range(GR):
                act.wait_ge(sem("decay_turned"), g + 1)
                act.activation(decay[:, g].rearrange("p c q n -> p (c q n)"), sc[g][:, :], ACT.Copy)\
                    .then_inc(sem("decay_ready"), 1)
            with act.Fori(0, B - 1) as b:
                chunks(b)
                squares(b)
                project(b + 1, 0)
                project(b + 1, 1)
                output(b)
            chunks(B - 1)
            squares(B - 1)
            output(B - 1, last_one=True)

        @block.gpsimd
        def _(pool):
            pool.iota(row_i, [[0, 1]], base=0, channel_multiplier=1).then_inc(sem("row_i"), 1)
            pool.memset(blocks, 1.0).then_inc(sem("blocks"), 1)
            pool.memset(reverse, 0.0).then_inc(sem("reverse"), 1)
            pool.wait_ge(sem("reverse"), 1)
            pool.affine_select(out=reverse, in_=reverse, compare_op=ALU.not_equal, fill=1.0, base=1 - P,
                               pattern=[[1, P]], channel_multiplier=1).then_inc(sem("reverse"), 1)
            pool.wait_ge(sem("blocks"), 1)
            cells = blocks.rearrange("p (a b) -> p a b", b=DH)
            pool.affine_select(out=cells, in_=cells, compare_op=ALU.is_ge, fill=0.0, base=0,
                               pattern=[[-DH, HC], [0, DH]], channel_multiplier=1).then_inc(sem("blocks"), 1)
            pool.wait_ge(sem("blocks"), 2)
            pool.affine_select(out=cells, in_=cells, compare_op=ALU.is_ge, fill=0.0, base=DH - 1,
                               pattern=[[DH, HC], [0, DH]], channel_multiplier=-1).then_inc(sem("blocks"), 1)
            pool.wait_ge(sem("decay"), 16 * 3 * CH)
            pool.wait_ge(sem("w"), 16 * 9)

            def layernorm_power(n):
                pool.wait_ge(sem("var_ready"), n + 1)
                pool.tensor_tensor(rstd, rstd, k.minus_half[:, 0:BLK], ALU.pow).then_inc(sem("rstd_ready"), 1)

            def decay_q(b, h):
                pool.wait_ge(sem("pj_read"), 2 + PJ_TURN * b + (2 * CH + BLK) * h + CH)
                for c in range(CH):
                    q4 = qt[:, c, h * N:(h + 1) * N].rearrange("p (j n) -> p j n", n=P)
                    s4 = qst[:, c, h * N:(h + 1) * N].rearrange("p (j n) -> p j n", n=P)
                    pool.tensor_tensor(s4, q4, q_decay[:, c, :].unsqueeze(1).to_broadcast([P, BLK, P]), ALU.mult)\
                        .then_inc(sem("qst_ready"), 1)

            def group_power(b):
                pool.wait_ge(sem("group_var"), b + 1)
                pool.tensor_tensor(group_scale, group_scale, k.minus_half[:, 0:HEADS], ALU.pow)\
                    .then_inc(sem("group_rstd"), 1)

            for h in range(H):
                layernorm_power(h)
            for h in range(H):
                decay_q(0, h)
            with pool.Fori(0, B - 1) as b:
                for h in range(H):
                    layernorm_power(H * (b + 1) + h)
                decay_q(b + 1, 0)
                group_power(b)
                decay_q(b + 1, 1)
            group_power(B - 1)

        @block.vector
        def _(dve):
            dve.sem_inc(sem("tp_read"), 1)
            dve.sem_inc(sem("rt_read"), 1)

            def normalise(b, h):
                steps = Chain(dve, sem("ln_steps"), (2 * BLK + 1) * H, b, (2 * BLK + 1) * h)
                for j in range(BLK):
                    steps.step(dve.bn_stats(stats[:, j, :], one_tile(k.res, TB * b + BLK * h + j)))
                steps.settled()
                dve.sem_inc(sem("stats_complete"), 1)
                for j in range(BLK):
                    steps.step(dve.bn_aggr(moments[:, j, :], stats[:, j, :]))
                steps.settled()
                steps.step(dve.tensor_scalar(rstd, moments[:, :, 1], EPS, None, ALU.add))
                steps.settled()
                dve.sem_inc(sem("var_ready"), 1)
                dve.wait_ge(sem("rstd_ready"), H * b + h + 1)
                for j in range(BLK):
                    t = BLK * h + j
                    dve.tensor_scalar(xn[:, t, :], one_tile(k.res, TB * b + t), moments[:, j, 0:1], rstd[:, j:j + 1],
                                      ALU.subtract, ALU.mult).then_inc(sem("xn_ready"), 1)

            def project(b, h):
                use = PJ_TURN * b + (2 * CH + BLK) * h
                here = slice(h * N, (h + 1) * N)
                dve.wait_ge(sem("pj_read"), 2 + use + 2 * CH)
                for c in range(CH):
                    dve.tensor_scalar(ktp[:, 0, c, here], kt[:, c, here], parity[:, 0:1], None, ALU.mult)
                    dve.tensor_scalar(ktp[:, 1, c, here], kt[:, c, here], parity[:, 1:2], None, ALU.mult)\
                        .then_inc(sem("ktp_ready"), 1)
                for j in range(BLK):
                    dve.wait_ge(sem("pj_full"), use + 2 * CH + j + 1)
                    dve.tensor_tensor(vg[:, BLK * h + j, :], pj[j % 2][:, :], bias_vg, ALU.add)\
                        .then_inc(sem("pj_read"), 1)

            def chunk(b, j):
                dve.wait_ge(sem("tp_full"), tp_chunks(b) + 2 * j + 1)
                for c in range(CH):
                    last = dve.tensor_tensor(
                        kd[:, j % 2, c * P:(c + 1) * P].rearrange("p (g q d) -> p g q d", g=GR, q=2),
                        tp[:, c * P:(c + 1) * P].rearrange("p (g q d) -> p g q d", g=GR, q=2),
                        decay[:, :, c, :, P - 1:P].to_broadcast([P, GR, 2, DH]), ALU.mult)
                last.then_inc(sem("tp_read"), 1)
                for g in range(GR):
                    dve.wait_ge(sem("sc_full"), GR * (TB * b + j) + g + 1)
                    dve.tensor_tensor(masked[:, j % 2, g, :], sc[g][:, :], decay[:, g].rearrange("p c q n -> p (c q n)"),
                                      ALU.mult).then_inc(sem("sc_read"), 1)
                dve.wait_ge(sem("sc_read"), GR + GR * (TB * b + j + 1))
                dve.sem_inc(sem("masked_ready"), GR)
                steps = Chain(dve, sem("state_steps"), 2 * (TB - 1), b, 2 * j)
                if j < TB - 1:
                    dve.wait_ge(sem("tp_full"), tp_chunks(b) + 2 * j + 2)
                    dve.tensor_tensor(update, tp[:, 2 * P:4 * P].rearrange("p (c n) -> p c n", c=CH),
                                      blocks.unsqueeze(1).to_broadcast([P, CH, P]), ALU.mult).then_inc(sem("tp_read"), 1)
                    dve.wait_ge(sem("tp_read"), 1 + tp_chunks(b) + 2 * j + 2)
                    for c in range(CH):
                        if j == 0:
                            steps.step(dve.tensor_copy(state[:, 1, c, :], update[:, c, :]))
                        else:
                            steps.step(dve.scalar_tensor_tensor(state[:, (j + 1) % 2, c, :], state[:, j % 2, c, :],
                                                                q_decay[:, c, P - 1:P], update[:, c, :],
                                                                ALU.mult, ALU.add))
                    steps.settled()
                if j == 0:
                    dve.sem_inc(sem("state_ready"), 1)
                if j < TB - 1:
                    dve.sem_inc(sem("state_ready"), 1)

            def group_reduce(b, i):
                dve.wait_ge(sem("rt_full"), RT_TURN * b + TB + i + 1)
                dve.tensor_reduce(sums, rt[:, 0:D].rearrange("p (h d) -> p h d", d=DH), AX_X, ALU.add)\
                    .then_inc(sem("rt_read"), 1)
                dve.wait_ge(sem("rt_read"), 1 + RT_TURN * b + TB + i + 1)

            by_head = ret.rearrange("p t (h d) -> p t h d", d=DH)

            def centre(b):
                steps = Chain(dve, sem("centre_steps"), 1 + TB, b)
                group_reduce(b, 0)
                steps.link(dve.tensor_scalar(sums, sums, 1.0 / COUNT, None, ALU.mult))
                for t in range(TB):
                    steps.step(dve.tensor_tensor(by_head[:, t], by_head[:, t],
                                                 sums.unsqueeze(2).to_broadcast([P, HEADS, DH]), ALU.subtract))
                steps.settled()
                dve.sem_inc(sem("centred"), 1)

            def variance(b):
                steps = Chain(dve, sem("var_steps"), 1, b)
                group_reduce(b, 1)
                steps.link(dve.tensor_scalar(group_scale, sums, 1.0 / COUNT, EPS, ALU.mult, ALU.add))
                dve.sem_inc(sem("group_var"), 1)

            def gated(b):
                steps = Chain(dve, sem("gate_steps"), 4, b)
                dve.wait_ge(sem("group_rstd"), b + 1)
                steps.link(dve.tensor_tensor(scale.rearrange("p (h d) -> p h d", d=DH), gnw.rearrange("p (h d) -> p h d", d=DH),
                                             group_scale.unsqueeze(2).to_broadcast([P, HEADS, DH]), ALU.mult))
                steps.link(dve.tensor_tensor(ret, ret, scale.unsqueeze(1).to_broadcast([P, TB, D]), ALU.mult))
                steps.link(dve.tensor_tensor(ret, ret, gnb.unsqueeze(1).to_broadcast([P, TB, D]), ALU.add))
                dve.wait_ge(sem("gates"), TB * (b + 1))
                steps.link(dve.tensor_tensor(ret, ret, gates[:, bass.ds(TB * b, TB), :], ALU.mult))
                dve.sem_inc(sem("gated"), 1)
                tiles = k.res[:, bass.ds(TB * b, TB), :]
                dve.tensor_tensor(tiles, tiles, bias_o.unsqueeze(1).to_broadcast([P, TB, D]), ALU.add)\
                    .then_inc(sem("bias_added"), 1)
                dve.wait_ge(sem("bias_added"), b + 1)

            def output(b):
                for i in range(TB // 2):
                    dve.wait_ge(sem("rt_full"), RT_TURN * b + TB + 2 + i + 1)
                    tiles = k.res[:, bass.ds(TB * b + 2 * i, 2), :]
                    dve.tensor_tensor(tiles, tiles, rt[:, :].rearrange("p (j d) -> p j d", d=D), ALU.add)\
                        .then_inc(sem("rt_read"), 1)

            dve.wait_ge(sem("gamma"), 16)
            c = Chain(dve, sem("setup"))
            c.step(dve.memset(powers[0:HEADS, 0:P], 0.0))
            c.step(dve.memset(powers[0:HEADS, P:P + 1], 1.0))
            m = 1
            while m < P:
                c.link(dve.tensor_scalar(powers[0:HEADS, P + m + 1:P + 2 * m + 1], powers[0:HEADS, P + 1:P + m + 1],
                                         powers[0:HEADS, P + m:P + m + 1], None, ALU.mult))
                m *= 2
            dve.sem_inc(sem("powers"), 1)
            dve.wait_ge(sem("row_i"), 1)
            c.link(dve.tensor_scalar(row_i, row_i, DH, None, ALU.bitwise_and))
            c.link(dve.tensor_scalar(parity[:, 1:2], row_i, 1.0 / DH, None, ALU.mult))
            c.link(dve.tensor_scalar(parity[:, 0:1], parity[:, 1:2], -1.0, 1.0, ALU.mult, ALU.add))
            for h in range(H):
                normalise(0, h)
            dve.wait_ge(sem("w"), 16 * 9)
            for h in range(H):
                project(0, h)
            dve.wait_ge(sem("decay_ready"), GR)
            dve.sem_inc(sem("sc_read"), GR)
            dve.wait_ge(sem("decay"), 16 * 3 * CH)
            dve.wait_ge(sem("blocks"), 3)

            def chunks(b, last_one=False):
                for j in range(TB):
                    chunk(b, j)
                    if not last_one and j in (2, 5):
                        normalise(b + 1, j // 3)

            with dve.Fori(0, B - 1) as b:
                chunks(b)
                centre(b)
                project(b + 1, 0)
                variance(b)
                project(b + 1, 1)
                gated(b)
                output(b)
            chunks(B - 1, last_one=True)
            centre(B - 1)
            variance(B - 1)
            gated(B - 1)
            output(B - 1)
            dve.wait_ge(sem("rt_read"), 1 + RT_TURN * B)




class Kept:

    CONSTS = 7

    def __init__(self, nc, ctx):
        def sb(name, shape, dt):
            return ctx.enter_context(nc.sbuf_tensor(name, shape, dt))

        self.nc = nc
        self.ident = sb("ident", [P, P], F32)
        self.ones = sb("ones", [P, P], F32)
        self.ones_bf = sb("ones_bf", [P, P], BF16)
        self.tri_bf = sb("tri_bf", [P, P], BF16)
        self.iota64 = sb("iota64", [P, 64], F32)
        self.minus_half = sb("minus_half", [P, 64], F32)
        self.zero = sb("empty_slots", [P, 4 * (256 + Slots.TAIL)], F32)
        self.const_made = ctx.enter_context(nc.semaphore("const_made"))
        self.const_ready = ctx.enter_context(nc.semaphore("const_ready"))
        self.res = sb("residual", [P, 32, 256], F32)
        self.slots = Slots(nc, 32 * P, 256, 64, 4)
        self.ZEROINGS = self.slots.tiles // 4
        self.slots_zeroed = ctx.enter_context(nc.semaphore("slots_zeroed"))
        floats = 43008
        self.arena = Arena(sb("arena", [P, floats], F32), floats)

    def zero_slots(self, sp):
        sp.wait_ge(self.const_ready, self.CONSTS)
        rows = self.slots.x.rearrange("(n p r) d -> n p (r d)", p=P, r=4)
        for n in range(self.ZEROINGS):
            sp.dma_start(rows[n], self.zero[:, :]).then_inc(self.slots_zeroed, 16)

    def make_constants(self, pool):
        made = self.const_made
        pool.memset(self.ident[:, :], 0.0).then_inc(made, 1)
        pool.memset(self.tri_bf[:, :], 1.0).then_inc(made, 1)
        pool.memset(self.ones[:, :], 1.0).then_inc(made, 1)
        pool.memset(self.ones_bf[:, :], 1.0).then_inc(made, 1)
        pool.memset(self.minus_half[:, :], -0.5).then_inc(made, 1)
        pool.memset(self.zero[:, :], 0.0).then_inc(made, 1)
        pool.iota(self.iota64[:, :], [[1, 64]], base=0, channel_multiplier=0,
                  allow_small_or_imprecise_dtypes=True).then_inc(made, 1)
        pool.wait_ge(made, self.CONSTS)
        pool.affine_select(out=self.ident[:, :], in_=self.ident[:, :], compare_op=ALU.not_equal, fill=1.0, base=0,
                           pattern=[[-1, P]], channel_multiplier=1).then_inc(self.const_ready, 1)
        pool.affine_select(out=self.tri_bf[:, :], in_=self.tri_bf[:, :], compare_op=ALU.is_gt, fill=0.0, base=0,
                           pattern=[[1, P]], channel_multiplier=-1).then_inc(self.const_ready, 1)
        pool.memset(self.zero[:, :].rearrange("p (r d) -> p r d", r=4)[:, :, 256:], Slots.NO_PAIR)\
            .then_inc(self.const_ready, 1)
        pool.wait_ge(self.const_ready, 3)
        pool.sem_inc(self.const_ready, self.CONSTS - 3)




def program(nc, x, w_rvk, w_out, time_decay, time_first, w_qk, w_vg, w_o, b_q, b_k, b_vg, b_o, gn_w, gn_b, gamma,
            router_w, router_bias, w_gu, w_d, sw_gu, sw_d, out):
    with ExitStack() as ctx:
        k = Kept(nc, ctx)
        time_mix(nc, k, x, w_rvk, w_out, time_decay, time_first)
        experts(nc, k, "moe1", 16 * k.ZEROINGS, router_w, router_bias, w_gu, w_d, sw_gu, sw_d)
        retention(nc, k, w_qk, w_vg, w_o, b_q, b_k, b_vg, b_o, gn_w, gn_b, gamma, x.shape[0])
        experts(nc, k, "moe2", 2 * 16 * k.ZEROINGS, router_w, router_bias, w_gu, w_d, sw_gu, sw_d, out=out)


def kernel(**inputs):
    import numpy as np
    import concourse.bacc as bacc
    from concourse.bass_utils import run_bass_kernel_spmd

    a, b, f = "L0_attn_a_", "L0_attn_b_", "L0_ffn_"
    g = {n: np.asarray(v) for n, v in inputs.items()}
    D = g[a + "x"].shape[-1]

    def joined(w):
        return np.transpose(w, (1, 0, 2)).reshape(D, -1)

    arrays = {
        "x": g[a + "x"],
        "w_rvk": g[a + "W_rvk"].T,
        "w_out": g[a + "W_out"].T,
        "time_decay": g[a + "time_decay"],
        "time_first": g[a + "time_first"],
        "w_qk": np.concatenate([g[b + "wq"], g[b + "wk"]], axis=1),
        "w_vg": np.concatenate([g[b + "wv"], g[b + "wg"]], axis=1),
        "w_o": g[b + "wo"],
        "b_q": g[b + "bq"],
        "b_k": g[b + "bk"],
        "b_vg": np.concatenate([g[b + "bv"], g[b + "bg"]]),
        "b_o": g[b + "bo"],
        "gn_w": g[b + "gn_w"],
        "gn_b": g[b + "gn_b"],
        "gamma": g[b + "gamma"],
        "router_w": g[f + "router_w"],
        "router_bias": g[f + "router_bias"],
        "w_gu": np.transpose(np.concatenate([g[f + "wg"], g[f + "wu"]], axis=2), (1, 0, 2)),
        "w_d": g[f + "wd"],
        "sw_gu": np.concatenate([joined(g[f + "swg"]), joined(g[f + "swu"])], axis=1),
        "sw_d": g[f + "swd"].reshape(-1, D),
    }
    arrays = {n: np.ascontiguousarray(v) for n, v in arrays.items()}
    nc = bacc.Bacc("TRN2", target_bir_lowering=False, num_devices=1)
    aps = {n: nc.dram_tensor(n, v.shape, mybir.dt.from_np(v.dtype), kind="ExternalInput").ap()
           for n, v in arrays.items()}
    out = nc.dram_tensor("out", arrays["x"].shape, F32, kind="ExternalOutput").ap()
    program(nc, out=out, **aps)
    return run_bass_kernel_spmd(nc, [arrays], core_ids=[0]).results[0]["out"]
```

```python
from contextlib import ExitStack

import concourse.bass as bass
from concourse import mybir

P = 128
F32 = mybir.dt.float32
BF16 = mybir.dt.bfloat16
I32 = mybir.dt.int32
U32 = mybir.dt.uint32
ALU = mybir.AluOpType
ACT = mybir.ActivationFunctionType
AX_X = mybir.AxisListType.X
EPS = 1e-5


class Arena:

    def __init__(self, tensor, floats):
        self.tensor, self.floats, self.at = tensor, floats, 0

    def take(self, *shape, at=None):
        n = 1
        for s in shape:
            n *= s
        start = self.at if at is None else at
        assert start + n <= self.floats, (start, n, self.floats)
        if at is None:
            self.at += n
        piece = self.tensor[:, start:start + n]
        if len(shape) == 2:
            piece = piece.rearrange("p (a b) -> p a b", a=shape[0])
        if len(shape) == 3:
            piece = piece.rearrange("p (a b c) -> p a b c", a=shape[0], b=shape[1])
        if len(shape) == 4:
            piece = piece.rearrange("p (a b c d) -> p a b c d", a=shape[0], b=shape[1], c=shape[2])
        return piece


class Sems:

    def __init__(self, nc, ctx, phase):
        self.nc, self.phase, self.known = nc, phase, {}
        ctx.callback(self.release)

    def __call__(self, name):
        if name not in self.known:
            self.known[name] = self.nc.alloc_semaphore(name=f"{self.phase}_{name}")
        return self.known[name]

    def release(self):
        self.nc.clear_and_free_semaphores(list(self.known.values()))
        self.nc.all_engine_barrier()


class Chain:

    def __init__(self, engine, sem, per_turn=0, turn=0, before=0):
        self.engine, self.sem, self.n = engine, sem, 0
        self.base = per_turn * turn + before

    def step(self, instruction):
        self.n += 1
        instruction.then_inc(self.sem, 1)

    def settled(self):
        self.engine.wait_ge(self.sem, self.base + self.n)

    def link(self, instruction):
        self.step(instruction)
        self.settled()


def one_tile(ap, t):
    names = " ".join("abc"[:len(ap.shape) - 2])
    return ap[(slice(None), bass.ds(t, 1)) + (slice(None),) * (len(ap.shape) - 2)].rearrange(
        f"p o {names} -> p (o {names.split()[0]}) {' '.join(names.split()[1:])}")




def time_mix(nc, k, x, w_rvk, w_out, time_decay, time_first):
    B, T, C = x.shape
    TB = T // P
    CH = C // P
    N = 512
    H = T // N
    UNITS = H * CH
    arena = k.arena
    arena.at = 0
    wrvk = arena.take(CH, 3 * C)
    wout = arena.take(CH, C)
    decay = arena.take(CH)
    first = arena.take(CH)
    stats = arena.take(TB, 6)
    moments = arena.take(TB, 2)
    mean = arena.take(B * TB)
    rstd = arena.take(B * TB)
    xn = arena.take(TB, C)
    xnt = arena.take(CH, CH, N)
    o = arena.take(CH, T + 1)
    p = arena.take(CH, T + 1)
    q = arena.take(CH, T + 1)
    dif = arena.take(UNITS, N)
    neg = arena.take(UNITS, N)
    a2 = arena.take(UNITS, N)
    b2 = arena.take(UNITS, N)
    er = arena.take(UNITS, N)
    vs = arena.take(UNITS, N)
    num = arena.take(UNITS, N)
    bv2 = arena.take(CH, N)
    yt = arena.take(H, CH, N)

    xv = x.rearrange("b (t p) c -> b p t c", p=P)
    BLK = N // P
    assert H == 2 and CH == 2
    with ExitStack() as ctx:
        sem = Sems(nc, ctx, "mix")
        rkv = [[ctx.enter_context(nc.psum_tensor(f"mix_{g}{c}", [P, N], F32)) for g in "kvr"] for c in range(CH)]
        tp = ctx.enter_context(nc.psum_tensor("mix_tp", [P, N], F32))
        op = [ctx.enter_context(nc.psum_tensor("mix_op", [P, N], F32)), tp]
        assert BLK == 4 and 2 * C == N
        block = ctx.enter_context(nc.Block())

        @block.sync
        def _(sp):
            for b in range(B):
                sp.dma_start(k.res[:, b * TB:(b + 1) * TB, :], xv[b]).then_inc(sem(f"x{b}"), 16)
                if b == 0:
                    sp.dma_start(wrvk, w_rvk.rearrange("(h p) n -> p h n", p=P)).then_inc(sem("w"), 16)
                    sp.dma_start(wout, w_out.rearrange("(h p) n -> p h n", p=P)).then_inc(sem("w"), 16)
            k.zero_slots(sp)

        @block.scalar
        def _(act):
            act.dma_start(decay, time_decay.rearrange("(h p) -> p h", p=P), allow_slow_non_contiguous=True)\
                .then_inc(sem("tm"), 16)
            act.dma_start(first, time_first.rearrange("(h p) -> p h", p=P), allow_slow_non_contiguous=True)\
                .then_inc(sem("tm"), 16)
            act.preload_act_table(ACT.Exp)
            act.sem_inc(sem("tp_read"), 1)
            act.sem_inc(sem("rkv_free"), CH)
            act.wait_ge(sem("tm"), 32)
            act.activation(decay, decay, ACT.Exp).then_inc(sem("exp_decay"), 1)

            def copy_transposes(b, h):
                for half in range(CH):
                    act.wait_ge(sem("tp_full"), UNITS * b + CH * h + half + 1)
                    act.activation(xnt[:, h, half, :], tp[:, :], ACT.Copy).then_inc(sem("tp_read"), 1)

            def exps(b, u):
                _, pv, pr = rkv[u % CH]
                steps = Chain(act, sem("exp_steps"), 3 * UNITS, b, 3 * u)
                act.wait_ge(sem("dif_ready"), UNITS * b + u + 1)
                act.activation(a2[:, u, :], a2[:, u, :], ACT.Exp)
                act.activation(b2[:, u, :], b2[:, u, :], ACT.Exp)
                act.activation(vs[:, u, :], pv[:, :], ACT.Copy).then_inc(sem("exp2"), 1)
                steps.step(act.activation(neg[:, u, :], dif[:, u, :], ACT.Relu))
                steps.step(act.activation(er[:, u, :], pr[:, :], ACT.Exp, scale=-1.0))
                steps.settled()
                act.sem_inc(sem("rkv_free"), 1)
                steps.step(act.activation(dif[:, u, :], dif[:, u, :], ACT.Relu, scale=-1.0))
                act.activation(neg[:, u, :], neg[:, u, :], ACT.Exp, scale=-1.0)
                act.activation(er[:, u, :], er[:, u, :], ACT.Identity, bias=1.0)
                steps.settled()
                act.activation(dif[:, u, :], dif[:, u, :], ACT.Exp, scale=-1.0).then_inc(sem("exp1"), 1)

            copy_transposes(0, 0)
            exps(0, 0)
            copy_transposes(0, 1)
            exps(0, 1)
            exps(0, 2)
            with act.Fori(1, B) as b:
                exps(b - 1, 3)
                copy_transposes(b, 0)
                exps(b, 0)
                copy_transposes(b, 1)
                exps(b, 1)
                exps(b, 2)
            exps(B - 1, 3)

        @block.tensor
        def _(pe):
            pe.wait_ge(k.const_ready, k.CONSTS)
            pe.wait_ge(sem("w"), 32)

            def transposes(b, h, outputs_before):
                if outputs_before:
                    pe.wait_ge(sem("op_read"), 1 + TB // 2 * (b - 1) + BLK // 2 * h)
                for half in range(CH):
                    pe.wait_ge(sem("tp_read"), UNITS * b + CH * h + half + 1)
                    for j in range(BLK):
                        t = h * BLK + j
                        if half == 0:
                            pe.wait_ge(sem("xn_ready"), TB * b + t + 1)
                        last = pe.transpose(tp[:, j * P:(j + 1) * P], xn[:, t, half * P:(half + 1) * P], k.ident[:, :])
                    last.then_inc(sem("tp_full"), 1)

            def project(b, h, halves=range(CH)):
                pe.wait_ge(sem("tp_read"), UNITS * b + CH * h + CH + 1)
                for c in halves:
                    pe.wait_ge(sem("rkv_free"), UNITS * b + CH * h + c + 1)
                    for g, bank in zip((2, 1, 0), rkv[c]):
                        at = g * C + c * P
                        for half in range(CH):
                            last = pe.matmul(bank[:, :], wrvk[:, half, at:at + P], xnt[:, h, half, :],
                                             start=half == 0, stop=half == CH - 1)
                    last.then_inc(sem("rkv_ready"), 1)

            def output(b, h, transposed=True):
                pe.wait_ge(sem("y_ready"), UNITS * b + CH * h + CH)
                for i, bank in enumerate(op):
                    pe.wait_ge(sem("op_read"), 1 + TB // 2 * b + BLK // 2 * h)
                    if i == 1 and transposed:
                        pe.wait_ge(sem("tp_read"), UNITS * (b + 1) + CH * h + CH + 1)
                    for j in range(2):
                        at = (2 * i + j) * P
                        for half in range(CH):
                            last = pe.matmul(bank[:, j * C:(j + 1) * C], yt[:, h, half, at:at + P], wout[:, half, :],
                                             start=half == 0, stop=half == CH - 1)
                    last.then_inc(sem("op_full"), 1)

            transposes(0, 0, False)
            project(0, 0)
            transposes(0, 1, False)
            project(0, 1)
            with pe.Fori(1, B) as b:
                for h in range(H):
                    transposes(b, h, True)
                    project(b, h, [0])
                    output(b - 1, h)
                    project(b, h, [1])
            output(B - 1, 0, transposed=False)
            output(B - 1, 1, transposed=False)

        @block.gpsimd
        def _(pool):
            k.make_constants(pool)
            pool.wait_ge(k.const_made, k.CONSTS)
            with pool.Fori(0, B) as b:
                pool.wait_ge(sem("var_ready"), b + 1)
                pool.tensor_tensor(rstd[:, bass.ds(b * TB, TB)], rstd[:, bass.ds(b * TB, TB)], k.minus_half[:, 0:TB],
                                   ALU.pow).then_inc(sem("rstd_ready"), 1)
            with pool.Fori(0, B) as b:
                for u in range(UNITS):
                    h, c = u // CH, u % CH
                    n = UNITS * b + u
                    before = slice(h * N, (h + 1) * N)
                    steps = Chain(pool, sem("pool_steps"), 6 * UNITS, b, 6 * u)
                    pool.wait_ge(sem("pq_ready"), n + 1)
                    pool.wait_ge(sem("exp1"), n + 1)
                    steps.step(pool.tensor_tensor(num[:, u, :], neg[:, u, :], p[:, c, before], ALU.mult))
                    steps.step(pool.tensor_tensor(vs[:, u, :], dif[:, u, :], vs[:, u, :], ALU.mult))
                    steps.step(pool.tensor_tensor(neg[:, u, :], neg[:, u, :], q[:, c, before], ALU.mult))
                    steps.settled()
                    steps.step(pool.tensor_tensor(num[:, u, :], num[:, u, :], vs[:, u, :], ALU.add))
                    steps.step(pool.tensor_tensor(neg[:, u, :], neg[:, u, :], dif[:, u, :], ALU.add))
                    steps.settled()
                    steps.link(pool.tensor_tensor(neg[:, u, :], neg[:, u, :], er[:, u, :], ALU.mult))
                    pool.sem_inc(sem("sums_ready"), 1)

        @block.vector
        def _(dve):
            dve.wait_ge(sem("exp_decay"), 1)
            dve.tensor_scalar(decay, decay, -1.0, None, ALU.mult).then_inc(sem("setup"), 1)
            for c in range(CH):
                dve.memset(o[:, c, 0:1], -1e38).then_inc(sem("setup"), 1)
                dve.memset(p[:, c, 0:1], 0.0).then_inc(sem("setup"), 1)
                dve.memset(q[:, c, 0:1], 0.0).then_inc(sem("setup"), 1)
            dve.wait_ge(sem("setup"), 1 + 3 * CH)
            dve.sem_inc(sem("op_read"), 1)

            def statistics(b):
                steps = Chain(dve, sem("stat_steps"), 2 * TB + 2, b)
                for t in range(TB):
                    steps.step(dve.bn_stats(stats[:, t, :], one_tile(k.res, b * TB + t)))
                steps.settled()
                dve.sem_inc(sem("stats_complete"), 1)
                for t in range(TB):
                    steps.step(dve.bn_aggr(moments[:, t, :], stats[:, t, :]))
                steps.settled()
                steps.step(dve.tensor_copy(mean[:, bass.ds(b * TB, TB)], moments[:, :, 0]))
                steps.step(dve.tensor_scalar(rstd[:, bass.ds(b * TB, TB)], moments[:, :, 1], EPS, None, ALU.add))
                steps.settled()
                dve.sem_inc(sem("var_ready"), 1)

            def normalise(b):
                dve.wait_ge(sem("rstd_ready"), b + 1)
                for t in range(TB):
                    dve.tensor_scalar(xn[:, t, :], one_tile(k.res, b * TB + t), mean[:, bass.ds(b * TB + t, 1)],
                                      rstd[:, bass.ds(b * TB + t, 1)], ALU.subtract, ALU.mult).then_inc(sem("xn_ready"), 1)

            def differences(b, u):
                h, c = u // CH, u % CH
                before, after = slice(h * N, (h + 1) * N), slice(h * N + 1, (h + 1) * N + 1)
                pk = rkv[c][0]
                steps = Chain(dve, sem("dif_steps"), 4 * UNITS, b, 4 * u)
                dve.wait_ge(sem("rkv_ready"), UNITS * b + u + 1)
                steps.link(dve.tensor_tensor_scan(o[:, c, after], decay[:, c:c + 1].to_broadcast([P, N]), pk[:, :],
                                                  o[:, c, h * N:h * N + 1], ALU.add, ALU.max))
                steps.step(dve.scalar_tensor_tensor(dif[:, u, :], pk[:, :], first[:, c:c + 1], o[:, c, before],
                                                    ALU.add, ALU.subtract))
                steps.step(dve.scalar_tensor_tensor(a2[:, u, :], o[:, c, before], decay[:, c:c + 1], o[:, c, after],
                                                    ALU.add, ALU.subtract))
                steps.step(dve.tensor_tensor(b2[:, u, :], pk[:, :], o[:, c, after], ALU.subtract))
                steps.settled()
                dve.sem_inc(sem("dif_ready"), 1)

            def states(b, u):
                h, c = u // CH, u % CH
                after, start = slice(h * N + 1, (h + 1) * N + 1), slice(h * N, h * N + 1)
                steps = Chain(dve, sem("state_steps"), 3 * UNITS, b, 3 * u)
                dve.wait_ge(sem("exp2"), UNITS * b + u + 1)
                steps.link(dve.tensor_tensor(bv2[:, c, :], b2[:, u, :], vs[:, u, :], ALU.mult))
                steps.step(dve.tensor_tensor_scan(p[:, c, after], a2[:, u, :], bv2[:, c, :], p[:, c, start],
                                                  ALU.mult, ALU.add))
                steps.step(dve.tensor_tensor_scan(q[:, c, after], a2[:, u, :], b2[:, u, :], q[:, c, start],
                                                  ALU.mult, ALU.add))
                steps.settled()
                dve.sem_inc(sem("pq_ready"), 1)

            def outputs(b, u):
                h, c = u // CH, u % CH
                steps = Chain(dve, sem("y_steps"), 2 * UNITS, b, 2 * u)
                dve.wait_ge(sem("sums_ready"), UNITS * b + u + 1)
                steps.link(dve.reciprocal(neg[:, u, :], neg[:, u, :]))
                steps.link(dve.tensor_tensor(yt[:, h, c, :], num[:, u, :], neg[:, u, :], ALU.mult))
                dve.sem_inc(sem("y_ready"), 1)

            def add_output(b, h):
                for j in range(BLK // 2):
                    pair = b * (TB // 2) + h * (BLK // 2) + j
                    dve.wait_ge(sem("op_full"), pair + 1)
                    tiles = k.res[:, bass.ds(2 * pair, 2), :]
                    dve.tensor_tensor(tiles, tiles, op[j][:, :].rearrange("p (j c) -> p j c", c=C), ALU.add)\
                        .then_inc(sem("op_read"), 1)

            def batch(b, is_first=False, is_last=False):
                if not is_first:
                    outputs(b - 1, 3)
                differences(b, 1)
                states(b, 0)
                states(b, 1)
                differences(b, 2)
                if not is_first:
                    add_output(b - 1, 1)
                outputs(b, 0)
                differences(b, 3)
                if not is_last:
                    normalise(b + 1)
                outputs(b, 1)
                states(b, 2)
                states(b, 3)
                if not is_last:
                    differences(b + 1, 0)
                add_output(b, 0)
                outputs(b, 2)

            dve.wait_ge(sem("x0"), 16)
            statistics(0)
            normalise(0)
            for b in range(1, B):
                dve.wait_ge(sem(f"x{b}"), 16)
            with dve.Fori(1, B) as b:
                statistics(b)
            differences(0, 0)
            batch(0, is_first=True)
            with dve.Fori(1, B - 1) as b:
                batch(b)
            batch(B - 1, is_last=True)
            outputs(B - 1, 3)
            add_output(B - 1, 1)
            dve.wait_ge(sem("op_read"), 1 + B * TB // 2)




class Slots:

    NO_PAIR = 2.0
    TAIL = 4

    def __init__(self, nc, tokens, width, experts, choices):
        self.tiles = tokens * choices // P + experts
        self.pairs = tokens * choices
        self.width = width + self.TAIL
        self.x = nc.dram_tensor("slots_x", (self.tiles * P, self.width), F32, kind="Internal").ap()
        self.y = nc.dram_tensor("pairs_y", (self.pairs, width), F32, kind="Internal").ap()
        self.expert = nc.dram_tensor("slots_expert", (self.tiles,), I32, kind="Internal").ap()


class Choices:

    def __init__(self, k, sem, ring):
        self.k, self.sem, self.ring = k, sem, ring
        self.G, self.K = ring.shape[1], ring.shape[2]
        self.y = k.slots.y.rearrange("(t p i) d -> t p i d", p=P, i=self.K)

    def load(self, sp, t):
        if t >= self.G:
            sp.wait_ge(self.sem("added"), 2 * self.K * ((t - self.G) // 2 + 1))
        sp.dma_start(self.ring[:, t % self.G], self.y[t]).then_inc(self.sem(f"in{t % self.G}"), 16)

    def add_pair(self, dve, pair, turn, place):
        k = self.k
        for i in range(self.K):
            for j in range(2):
                if i == 0:
                    dve.wait_ge(self.sem(f"in{place + j}"), 16 * turn + 16)
                else:
                    dve.wait_ge(self.sem("added"), 2 * self.K * pair + 2 * i + j - 1)
                tile = one_tile(k.res, 2 * pair + j)
                weight = k.gate[:, bass.ds(2 * pair + j, 1), i:i + 1].rearrange("p o i -> p (o i)")
                dve.scalar_tensor_tensor(tile, self.ring[:, place + j, i, :], weight, tile, ALU.mult, ALU.add)\
                    .then_inc(self.sem("added"), 1)

    def settled(self, dve, pairs):
        dve.wait_ge(self.sem("added"), 2 * self.K * pairs)


def experts(nc, k, phase, zeroed, router_w, router_bias, w_gu, w_d, sw_gu, sw_d, out=None):
    NT, D = k.res.shape[1], k.res.shape[2]
    E = router_w.shape[1]
    F = w_d.shape[1]
    K = 4
    KH = D // P
    BLK = 4
    N = BLK * P
    NB = NT // BLK
    SH = sw_d.shape[0] // P
    NX = k.slots.tiles
    slots = k.slots
    arena = k.arena
    arena.at = 0
    W = slots.width
    xn = arena.take(NT, W)
    xnt = arena.take(KH, NT * P)
    wd = arena.take(E, D, at=0)
    assert NT * W + KH * NT * P >= E * D
    WD_HALF = NT // 2 * W // D
    WD_XNT = -(-NT * W // D)
    WD_LAST = (NT * W + (NB - 1) * N) // D
    big = arena.at
    wgu = arena.take(KH, E, 2 * F)
    after_big = arena.at
    arena.at = big
    hot = [arena.take(NT * E // 2).bitcast(BF16).rearrange("p (t e) -> p t e", e=E) for _ in range(K)]
    chosen = arena.take(NT * E // 2).bitcast(BF16)
    chosen_t = chosen.rearrange("p (t e) -> p t e", e=E)
    count = arena.take(E, NT)
    before = arena.take(E, NT)
    restart = arena.take(E, NT)
    pos = arena.take(NT, E)
    picked = arena.take(NT, E)
    tiles_f = arena.take(E)
    tiles_i = arena.take(E).bitcast(I32)
    ends = arena.take(E)
    base = arena.take(E)
    gate_sum = arena.take(NT)
    slot_f = arena.take(NT)
    tile_no = arena.take(2)
    tile_expert = arena.take(2)
    tile_expert_i = arena.take(2).bitcast(I32)
    passed = arena.take(2, E)
    assert arena.at <= after_big
    arena.at = after_big
    slot = arena.take(NT, K).bitcast(I32)
    pair = arena.take(NT, K).bitcast(I32)
    gate = k.gate
    expert_row = arena.take(NX).bitcast(I32)
    at_experts = arena.at
    logit = arena.take(NT, E)
    choice = arena.take(NT, 8)
    sgu = arena.take(KH, 2 * SH * P)
    sd = arena.take(SH, D)
    rw = arena.take(KH, E)
    bias = arena.take(BLK, E)
    stats = arena.take(BLK, 6)
    moments = arena.take(2, BLK, 2)
    rstd = arena.take(2, BLK)
    xs_at = arena.at
    xs = arena.take(2, BLK, D)
    xst_at = arena.at
    xst = arena.take(KH, N)
    biased = arena.take(BLK, E)
    row_max = arena.take(BLK)
    best = arena.take(BLK, 8)
    which = arena.take(BLK, 8).bitcast(U32)
    assert SH <= 2 * BLK * D // N
    sg = arena.take(2, N, at=xst_at)
    sht = arena.take(SH, N, at=xs_at)
    arena.at = at_experts
    XRING, YRING = 8, 4
    xin = arena.take(XRING, 2, W)
    goes_to = arena.take(XRING, 2).bitcast(I32)
    xt = arena.take(2, 2 * KH * P)
    weights = arena.take(2, 2, KH, 2 * F)
    sig = arena.take(2, 2 * P)
    ht = arena.take(2, 2 * P)
    ytile = arena.take(YRING, 2, D)
    arena.at = at_experts
    G = 8
    chosen_y = arena.take(G, K, D)

    with ExitStack() as ctx:
        sem = Sems(nc, ctx, phase + "_route")
        tp = [ctx.enter_context(nc.psum_tensor(f"{phase}_tp{h}", [P, N], F32)) for h in range(KH)]
        lg = ctx.enter_context(nc.psum_tensor(f"{phase}_lg", [P, BLK, E], F32))
        ranks = ctx.enter_context(nc.psum_tensor(f"{phase}_ranks", [P, 2, BLK * E], F32))
        gate_ps = [ctx.enter_context(nc.psum_tensor(f"{phase}_gate{i}", [P, N], F32)) for i in range(2)]
        up_ps = [ctx.enter_context(nc.psum_tensor(f"{phase}_up{i}", [P, N], F32)) for i in range(2)]
        down_ps = [bank[:, :].rearrange("p (j d) -> p j d", d=D) for bank in tp]
        SUMS = K - 1
        block = ctx.enter_context(nc.Block())

        @block.sync
        def _(sp):
            sp.dma_start(rw, router_w.rearrange("(h p) n -> p h n", p=P)).then_inc(sem("rw"), 16)
            for j in range(BLK):
                sp.dma_start(bias[:, j, :], router_bias.rearrange("(o e) -> o e", o=1).to_broadcast([P, E]))\
                    .then_inc(sem("rw"), 16)
            sp.dma_start(sgu, sw_gu.rearrange("(h p) n -> p h n", p=P)).then_inc(sem("shared_w"), 16)
            sp.dma_start(sd, sw_d.rearrange("(j p) n -> p j n", p=P)).then_inc(sem("shared_w"), 16)
            sp.wait_ge(sem("tile_expert"), 1)
            sp.dma_start(slots.expert.rearrange("(p j) -> p j", j=2), tile_expert_i[0:NX // 2])\
                .then_inc(sem("expert_out"), 16)
            sp.wait_ge(sem("expert_out"), 16)
            sp.dma_start(expert_row[0:1], slots.expert.rearrange("(o n) -> o n", o=1)).then_inc(sem("expert_in"), 16)
            sp.wait_ge(sem("dispatched"), 1)
            sp.dma_start(wgu, w_gu.rearrange("(h p) e n -> p h e n", p=P)).then_inc(sem("wgu"), 16)
            def load_down(first, end):
                sp.dma_start(wd[0:F, first:end], w_d[first:end].rearrange("e f d -> f e d")).then_inc(sem("wd"), 16)

            sp.wait_ge(sem("scattered0"), 16 * K * NT // 2)
            load_down(0, WD_HALF)
            sp.wait_ge(sem("gu_full"), SH * (NB - 1))
            load_down(WD_XNT, WD_LAST)
            sp.wait_ge(sem("gu_full"), SH * NB)
            load_down(WD_LAST, E)
            sp.wait_ge(sem("scattered1"), 16 * K * NT // 2)
            load_down(WD_HALF, WD_XNT)
            sp.wait_ge(sem("expert_in"), 16)
            sp.wait_ge(sem("wgu"), 16)
            sp.wait_ge(sem("wd"), 4 * 16)

        @block.tensor
        def _(pe):
            pe.wait_ge(sem("rw"), 16 * (1 + BLK))

            def score(n, place):
                for h in range(KH):
                    pe.wait_ge(sem("tp_read"), KH * n + h + 1)
                    for j in range(BLK):
                        if h == 0:
                            pe.wait_ge(sem("xs_ready"), BLK * n + j + 1)
                        last = pe.transpose(tp[h][:, j * P:(j + 1) * P], xs[:, place, j, h * P:(h + 1) * P], k.ident[:, :])
                    last.then_inc(sem("tp_full"), 1)
                pe.wait_ge(sem("xst_ready"), KH * n + KH)
                pe.wait_ge(sem("lg_read"), n + 1)
                for j in range(BLK):
                    for h in range(KH):
                        last = pe.matmul(lg[:, j, :], xst[:, h, j * P:(j + 1) * P], rw[:, h, :],
                                         start=h == 0, stop=h == KH - 1)
                last.then_inc(sem("lg_full"), 1)

            def rank(n):
                pe.wait_ge(sem("sum_steps"), SUMS * (n + 1))
                pe.wait_ge(sem("counts_read"), 2 * n + 2)
                here = bass.ds(n * BLK * E, BLK * E)
                pe.matmul(ranks[:, 0, :], k.tri_bf[:, :], chosen[:, here], start=True, stop=True)
                pe.matmul(ranks[:, 1, :], k.ones_bf[:, :], chosen[:, here], start=True, stop=True)\
                    .then_inc(sem("counted"), 1)

            def gate_up(n, j):
                pe.wait_ge(sem("sht_ready"), SH * n + j + 1)
                for bank, at in ((gate_ps[j % 2], j * P), (up_ps[j % 2], (SH + j) * P)):
                    for h in range(KH):
                        last = pe.matmul(bank[:, :], sgu[:, h, at:at + P], xnt[:, h, bass.ds(N * n, N)],
                                         start=h == 0, stop=h == KH - 1)
                last.then_inc(sem("gu_full"), 1)

            def down(n):
                for j, ms in ((0, range(SH - 1)), (2, range(SH - 1)), (0, [SH - 1]), (1, range(SH)),
                              (2, [SH - 1]), (3, range(SH))):
                    if ms[0] == 0 and j % 2 == 0:
                        pe.wait_ge(sem("down_read"), 2 * n + j // 2 + 1)
                    pe.wait_ge(sem("sht_ready"), 2 + SH * n + ms[-1] + 1)
                    for m in ms:
                        last = pe.matmul(down_ps[j // 2][:, j % 2, :], sht[:, m, j * P:(j + 1) * P], sd[:, m, :],
                                         start=m == 0, stop=m == SH - 1, skip_group_check=True)
                    if j % 2 == 1:
                        last.then_inc(sem("down_full"), 1)

            score(0, 0)
            score(1, 1)
            rank(0)
            with pe.Fori(1, NB // 2) as g:
                for place in range(2):
                    score(2 * g + place, place)
                    rank(2 * g + place - 1)
            pe.wait_ge(sem("tp_read"), KH * (NB + 1))
            pe.wait_ge(sem("shared_w"), 32)
            for j in range(2):
                gate_up(0, j)
            rank(NB - 1)
            for j in range(2, SH):
                gate_up(0, j)
            down(0)
            with pe.Fori(1, NB) as n:
                for j in range(SH):
                    gate_up(n, j)
                down(n)

        @block.scalar
        def _(act):
            act.preload_act_table(ACT.Exp)
            act.sem_inc(sem("tp_read"), KH)
            act.sem_inc(sem("counts_read"), 2)

            def transposed(n, place, is_first=False):
                if not is_first:
                    act.wait_ge(sem("lg_full"), n)
                for h in range(KH):
                    act.wait_ge(sem("tp_full"), KH * n + h + 1)
                    act.activation(xst[:, h, :], tp[h][:, :], ACT.Copy).then_inc(sem("xst_ready"), 1)
                    act.activation(xnt[:, h, bass.ds(N * n, N)], tp[h][:, :], ACT.Copy).then_inc(sem("tp_read"), 1)
                act.activation(xn[:, bass.ds(BLK * n, BLK), 0:D], xs[:, place], ACT.Copy).then_inc(sem("xn_kept"), 1)

            def exp(n):
                act.wait_ge(sem("shifted"), n + 1)
                tiles = logit[:, bass.ds(BLK * n, BLK), :]
                act.activation(tiles, tiles, ACT.Exp).then_inc(sem("exps"), 1)

            def keep_counts(n):
                tiles = bass.ds(BLK * n, BLK)
                act.wait_ge(sem("counted"), n + 1)
                act.sem_inc(sem("counts_come"), 1)
                act.activation(pos[:, tiles, :], ranks[:, 0, :].rearrange("p (t e) -> p t e", e=E), ACT.Copy)\
                    .then_inc(sem("counts_read"), 1)
                act.activation(count[:, :, tiles], ranks[:, 1, :].rearrange("p (t e) -> p e t", e=E), ACT.Copy)\
                    .then_inc(sem("counts_read"), 1)

            transposed(0, 0, is_first=True)
            transposed(1, 1)
            exp(0)
            with act.Fori(1, NB // 2) as g:
                for place in range(2):
                    n = 2 * g + place
                    transposed(n, place)
                    exp(n - 1)
                    keep_counts(n - 2)
            exp(NB - 1)
            act.preload_act_table(ACT.Silu)

            def silu(n, j):
                act.wait_ge(sem("gu_full"), SH * n + j + 1)
                act.wait_ge(sem("sht_ready"), SH * n + j + 1)
                act.activation(sg[:, j % 2, :], gate_ps[j % 2][:, :], ACT.Silu).then_inc(sem("sg_ready"), 1)

            keep_counts(NB - 2)
            for j in range(2):
                silu(0, j)
            keep_counts(NB - 1)
            for j in range(2, SH):
                silu(0, j)
            with act.Fori(1, NB) as n:
                for j in range(SH):
                    silu(n, j)

        @block.gpsimd
        def _(pool):
            pool.memset(restart, 1.0).then_inc(sem("restart"), 1)
            pool.wait_ge(sem("restart"), 1)
            pool.memset(restart[:, :, 0:1], 0.0).then_inc(sem("restart"), 1)

            def power(n, place):
                pool.wait_ge(sem("var_ready"), n + 1)
                pool.tensor_tensor(rstd[:, place], rstd[:, place], k.minus_half[:, 0:BLK], ALU.pow)\
                    .then_inc(sem("rstd_ready"), 1)

            def add_choices(n):
                steps = Chain(pool, sem("sum_steps"), SUMS, n)
                tiles = bass.ds(BLK * n, BLK)
                pool.wait_ge(sem("hot_ready"), K * (n + 1))
                steps.step(pool.tensor_tensor(chosen_t[:, tiles, :], hot[0][:, tiles, :], hot[1][:, tiles, :], ALU.add))
                for i in range(2, K):
                    steps.settled()
                    steps.step(pool.tensor_tensor(chosen_t[:, tiles, :], chosen_t[:, tiles, :], hot[i][:, tiles, :],
                                                  ALU.add))

            power(0, 0)
            power(1, 1)
            with pool.Fori(0, NB // 2 - 1) as g:
                for place in range(2):
                    power(2 * g + place + 2, place)
                    add_choices(2 * g + place)
            add_choices(NB - 2)
            add_choices(NB - 1)
            pool.iota(tile_no[0:NX // 2], [[1, 2]], base=0, channel_multiplier=2,
                      allow_small_or_imprecise_dtypes=True).then_inc(sem("tile_no_made"), 1)
            pool.wait_ge(sem("tile_no_made"), 1)
            pool.sem_inc(sem("tile_no"), 1)
            pool.wait_ge(k.slots_zeroed, zeroed)
            pool.iota(pair, [[K * P, NT], [1, K]], base=0, channel_multiplier=K).then_inc(sem("pair"), 1)
            pool.memset(xn[:, :, D + 1:W], 0.0).then_inc(sem("pair"), 1)
            pool.wait_ge(sem("pair"), 2)
            pool.wait_ge(sem("xn_kept"), NB)
            HALF = NT // 2
            for i in range(K):
                pool.wait_ge(sem("slots_ready"), i + 1)
                for half in range(2):
                    if i:
                        pool.wait_ge(sem(f"scattered{half}"), 16 * HALF * i)
                    tiles = slice(half * HALF, (half + 1) * HALF)
                    pool.tensor_copy(xn[:, tiles, D:D + 1].bitcast(I32), pair[:, tiles, i:i + 1])\
                        .then_inc(sem("numbered"), 1)
                    pool.wait_ge(sem("numbered"), 2 * i + half + 1)
                    for t in range(half * HALF, (half + 1) * HALF):
                        pool.indirect_dma_start(out=slots.x, in_=xn[:, t, :], in_offset=None,
                                                out_offset=bass.IndirectOffsetOnAxis(ap=slot[:, t, i:i + 1], axis=0))\
                            .then_inc(sem(f"scattered{half}"), 16)
            for half in range(2):
                pool.wait_ge(sem(f"scattered{half}"), 16 * K * HALF)

        @block.vector
        def _(dve):
            dve.sem_inc(sem("lg_read"), 1)
            dve.sem_inc(sem("sht_ready"), 2)
            dve.sem_inc(sem("down_read"), 2)

            def statistics(n, place):
                steps = Chain(dve, sem("ln_steps"), 2 * BLK + 1, n)
                for j in range(BLK):
                    steps.step(dve.bn_stats(stats[:, j, :], one_tile(k.res, BLK * n + j)))
                steps.settled()
                dve.sem_inc(sem("stats_complete"), 1)
                for j in range(BLK):
                    steps.step(dve.bn_aggr(moments[:, place, j], stats[:, j, :]))
                steps.settled()
                steps.step(dve.tensor_scalar(rstd[:, place], moments[:, place, :, 1], EPS, None, ALU.add))
                steps.settled()
                dve.sem_inc(sem("var_ready"), 1)

            def normalise(n, place, xs_used=True):
                dve.wait_ge(sem("rstd_ready"), n + 1)
                if xs_used:
                    dve.wait_ge(sem("tp_full"), KH * (n - 1))
                    dve.wait_ge(sem("xn_kept"), n - 1)
                    dve.sem_inc(sem("xs_free"), 1)
                for j in range(BLK):
                    dve.tensor_scalar(xs[:, place, j, :], one_tile(k.res, BLK * n + j), moments[:, place, j, 0:1],
                                      rstd[:, place, j:j + 1], ALU.subtract, ALU.mult).then_inc(sem("xs_ready"), 1)

            def choose(n):
                steps = Chain(dve, sem("top_steps"), 2 * BLK + 4, n)
                tiles = bass.ds(BLK * n, BLK)
                dve.wait_ge(sem("lg_full"), n + 1)
                steps.step(dve.tensor_tensor(biased, lg[:, :, :], bias, ALU.add))
                steps.step(dve.tensor_reduce(row_max, lg[:, :, :], AX_X, ALU.max))
                steps.settled()
                dve.sem_inc(sem("biased_complete"), 1)
                steps.step(dve.tensor_tensor(logit[:, tiles, :], lg[:, :, :],
                                             row_max.unsqueeze(2).to_broadcast([P, BLK, E]), ALU.subtract))
                for j in range(BLK):
                    steps.step(dve.max(best[:, j, :], biased[:, j, :]))
                steps.settled()
                dve.sem_inc(sem("lg_read"), 1)
                dve.sem_inc(sem("shifted"), 1)
                for j in range(BLK):
                    steps.step(dve.max_index(which[:, j, :], best[:, j, :], biased[:, j, :]))
                steps.settled()
                dve.sem_inc(sem("which_complete"), 1)
                steps.step(dve.tensor_copy(choice[:, tiles, :], which))
                steps.settled()
                for i in range(K):
                    dve.tensor_tensor(hot[i][:, tiles, :], k.iota64[:, 0:E].unsqueeze(1).to_broadcast([P, BLK, E]),
                                      choice[:, tiles, i:i + 1].to_broadcast([P, BLK, E]), ALU.is_equal)\
                        .then_inc(sem("hot_ready"), 1)

            def multiply(n, j):
                dve.wait_ge(sem("sg_ready"), SH * n + j + 1)
                dve.tensor_tensor(sht[:, j, :], sg[:, j % 2, :], up_ps[j % 2][:, :], ALU.mult)\
                    .then_inc(sem("sht_ready"), 1)

            def add_down(n):
                for j in range(2):
                    dve.wait_ge(sem("down_full"), 2 * n + j + 1)
                    tiles = k.res[:, bass.ds(BLK * n + 2 * j, 2), :]
                    dve.tensor_tensor(tiles, tiles, down_ps[j], ALU.add).then_inc(sem("down_read"), 1)

            statistics(0, 0)
            normalise(0, 0, xs_used=False)
            statistics(1, 1)
            normalise(1, 1, xs_used=False)
            statistics(2, 0)
            choose(0)
            normalise(2, 0)
            statistics(3, 1)
            choose(1)
            with dve.Fori(1, NB // 2 - 1) as g:
                for place in range(2):
                    n = 2 * g + place
                    normalise(n + 1, 1 - place)
                    statistics(n + 2, place)
                    choose(n)
            normalise(NB - 1, 1)
            choose(NB - 2)
            choose(NB - 1)
            dve.wait_ge(sem("xn_kept"), NB)
            multiply(0, 0)
            multiply(0, 1)
            dve.wait_ge(sem("counts_read"), 2 + 2 * NB)
            dve.wait_ge(sem("restart"), 2)
            dve.wait_ge(sem("hot_ready"), K * NB)
            c = Chain(dve, sem("steps"))
            c.link(dve.tensor_tensor_scan(before.rearrange("p e t -> p (e t)"), restart.rearrange("p e t -> p (e t)"),
                                          count.rearrange("p e t -> p (e t)"), 0.0, ALU.mult, ALU.add))
            multiply(0, 2)
            c.link(dve.tensor_scalar(tiles_i, before[:, :, NT - 1], float(P - 1), None, ALU.add))
            c.link(dve.tensor_scalar(tiles_i, tiles_i, P.bit_length() - 1, None, ALU.logical_shift_right))
            c.link(dve.tensor_copy(tiles_f, tiles_i))
            c.link(dve.tensor_tensor_scan(ends, restart[:, 0, 1:2].to_broadcast([P, E]), tiles_f, 0.0,
                                          ALU.mult, ALU.add))
            c.link(dve.tensor_tensor(base, ends, tiles_f, ALU.subtract))
            c.link(dve.tensor_scalar(base, base, float(P), None, ALU.mult))
            c.link(dve.tensor_tensor(before, before, count, ALU.subtract))
            multiply(0, 3)
            c.link(dve.tensor_tensor(before, before, base.unsqueeze(2).to_broadcast([P, E, NT]), ALU.add))
            c.link(dve.tensor_tensor(pos, pos, before.rearrange("p e t -> p t e"), ALU.add))
            for i in range(K):
                c.link(dve.tensor_tensor(picked, hot[i], pos, ALU.mult))
                if i == 1:
                    multiply(1, 1)
                if i == 2:
                    multiply(1, 3)
                c.link(dve.tensor_reduce(slot_f, picked, AX_X, ALU.add))
                c.link(dve.tensor_copy(slot[:, :, i], slot_f))
                dve.sem_inc(sem("slots_ready"), 1)
                if i == 0:
                    add_down(0)
                    multiply(1, 0)
                if i == 1:
                    multiply(1, 2)
                if i == 3:
                    add_down(1)
                    multiply(2, 0)
            dve.wait_ge(sem("tile_no"), 1)
            HALF = NX // 2
            c.link(dve.tensor_tensor(passed[0:HALF], tile_no[0:HALF].unsqueeze(2).to_broadcast([HALF, 2, E]),
                                     ends[0:HALF].unsqueeze(1).to_broadcast([HALF, 2, E]), ALU.is_ge))
            c.link(dve.tensor_reduce(tile_expert[0:HALF], passed[0:HALF], AX_X, ALU.add))
            c.link(dve.tensor_scalar(tile_expert_i[0:HALF], tile_expert[0:HALF], float(E - 1), None, ALU.min))
            dve.sem_inc(sem("tile_expert"), 1)
            dve.wait_ge(sem("exps"), NB)
            for i in range(K):
                if i < 2:
                    multiply(2, i + 1)
                c.link(dve.tensor_tensor(picked, hot[i], logit, ALU.mult))
                if i == 1:
                    multiply(2, 3)
                if i == 3:
                    multiply(3, 0)
                c.link(dve.tensor_reduce(gate[:, :, i], picked, AX_X, ALU.add))
                if i == 2:
                    add_down(2)
            multiply(3, 1)
            multiply(3, 2)
            c.link(dve.tensor_reduce(gate_sum, gate, AX_X, ALU.add))
            c.link(dve.reciprocal(gate_sum, gate_sum))
            multiply(3, 3)
            c.link(dve.tensor_tensor(gate, gate, gate_sum.unsqueeze(2).to_broadcast([P, NT, K]), ALU.mult))
            dve.sem_inc(sem("dispatched"), 1)
            add_down(3)
            with dve.Fori(4, NB) as n:
                for j in range(SH):
                    multiply(n, j)
                add_down(n)
            dve.wait_ge(sem("down_read"), 2 + 2 * NB)

    with ExitStack() as ctx:
        sem = Sems(nc, ctx, phase + "_exp")
        xt_ps, h_ps, y_ps = [[ctx.enter_context(nc.psum_tensor(f"{phase}_{g}{i}", [P, 512], F32))
                              for i in range(2)] for g in ("ext", "eh", "ey")]
        x_v = slots.x.rearrange("(s t p) d -> s p t d", p=P, t=2)
        NP = NX // 2
        RING = XRING
        LAG = 3
        assert NP % RING == 0
        block = ctx.enter_context(nc.Block())

        def all_steps(engine, step, lag):
            for s in range(RING):
                step(0, s, s)
            with engine.Fori(1, NP // RING) as g:
                for r in range(RING):
                    step(g, r, None)
            for s in range(NP, NP + lag):
                step(s // RING, s % RING, s)

        def pair_of(g, r, s, back):
            if s is not None and not 0 <= s - back < NP:
                return None
            turn = g if r >= back else g - 1
            place = (r - back) % RING
            return RING * turn + place, turn, place

        def load_experts(engine, held, g, pairs):
            row = expert_row[0:1, bass.ds(2 * (RING * g + pairs[0]), 2 * len(pairs))]
            _, values = nc.values_load_multi_w_load_instructions(
                row, engines=[engine], min_val=0, max_val=E - 1,
                skip_runtime_bounds_check_because="tile_expert is a count of experts, cut off at E - 1")
            for at, pair in enumerate(pairs):
                held[pair] = values[2 * at:2 * at + 2]

        @block.sync
        def _(sp):
            def step(g, r, s):
                n, _, place = pair_of(g, r, s, 0)
                if s is None:
                    sp.wait_ge(sem("xt_full"), n + 1 - XRING)
                    sp.wait_ge(sem("numbers_kept"), n + 1 - XRING)
                sp.dma_start(xin[:, place], x_v[bass.ds(n, 1)].rearrange("s p t d -> p (s t) d"))\
                    .then_inc(sem(f"x_in{place}"), 16)

            all_steps(sp, step, 0)
            for place in range(YRING):
                sp.wait_ge(sem(f"y_out{place}"), 32 * NP // YRING)

        @block.gpsimd
        def _(pool):
            for n in range(NP):
                pool.wait_ge(sem("numbers_kept"), n + 1)
                pool.wait_ge(sem("y_read"), 2 + n + 1)
                for j in range(2):
                    pool.indirect_dma_start(
                        out=slots.y, in_=ytile[:, n % YRING, j, :], in_offset=None, bounds_check=slots.pairs - 1,
                        oob_is_err=False, out_offset=bass.IndirectOffsetOnAxis(
                            ap=goes_to[:, n % XRING, j:j + 1], axis=0))\
                        .then_inc(sem(f"y_out{n % YRING}"), 16)

        @block.tensor
        def _(pe):
            held = {}

            def step(g, r, s):
                if r == 0 and s != 0:
                    load_experts(mybir.EngineType.PE, held, g, range(-LAG, 0))
                if r == 0 and (s is None or s < NP):
                    load_experts(mybir.EngineType.PE, held, g, range(0, RING - LAG))
                pair = pair_of(g, r, s, 0)
                if pair is not None:
                    n, turn, place = pair
                    pe.wait_ge(sem(f"x_in{place}"), 16 * turn + 16)
                    pe.wait_ge(sem("xt_read"), n + 1)
                    for j in range(2):
                        for h in range(KH):
                            last = pe.transpose(xt_ps[place % 2][:, (j * KH + h) * P:(j * KH + h + 1) * P],
                                                xin[:, place, j, h * P:(h + 1) * P], k.ident[:, :])
                    last.then_inc(sem("xt_full"), 1)
                pair = pair_of(g, r, s, 1)
                if pair is not None:
                    n, turn, place = pair
                    pe.wait_ge(sem("weights_ready"), 2 * (n + 1))
                    pe.wait_ge(sem("xt_read"), 2 + n + 1)
                    pe.wait_ge(sem("ht_ready"), n + 1)
                    for j in range(2):
                        for h in range(KH):
                            last = pe.matmul(h_ps[place % 2][:, j * P:(j + 1) * P], weights[:, place % 2, j, h, :],
                                             xt[:, place % 2, (j * KH + h) * P:(j * KH + h + 1) * P],
                                             start=h == 0, stop=h == KH - 1)
                    last.then_inc(sem("h_full"), 1)
                pair = pair_of(g, r, s, 3)
                if pair is not None:
                    n, turn, place = pair
                    expert = held[r - 3]
                    pe.wait_ge(sem("ht_ready"), 2 + n + 1)
                    pe.wait_ge(sem("y_read"), n + 1)
                    for j in range(2):
                        last = pe.matmul(y_ps[place % 2][:, j * D:(j + 1) * D], ht[0:F, place % 2, j * P:(j + 1) * P],
                                         wd[0:F].rearrange("f e d -> f (e d)")[:, bass.ds(expert[j] * D, D)],
                                         start=True, stop=True)
                    last.then_inc(sem("y_full"), 1)

            all_steps(pe, step, LAG)

        @block.scalar
        def _(act):
            act.preload_act_table(ACT.Silu)
            act.sem_inc(sem("xt_read"), 2)

            def step(g, r, s):
                pair = pair_of(g, r, s, 0)
                if pair is not None:
                    n, turn, place = pair
                    act.wait_ge(sem("xt_full"), n + 1)
                    if s is None or s >= 2:
                        act.wait_ge(sem("h_full"), n - 1)
                    act.activation(xt[:, place % 2], xt_ps[place % 2][:, :], ACT.Copy).then_inc(sem("xt_read"), 1)
                pair = pair_of(g, r, s, 1)
                if pair is not None:
                    n, turn, place = pair
                    act.wait_ge(sem("h_full"), n + 1)
                    act.wait_ge(sem("ht_ready"), n + 1)
                    act.activation(sig[F:2 * F, place % 2], h_ps[place % 2][0:F, 0:2 * P], ACT.Silu)\
                        .then_inc(sem("sig_ready"), 1)

            all_steps(act, step, 1)

        @block.vector
        def _(dve):
            dve.sem_inc(sem("ht_ready"), 2)
            dve.sem_inc(sem("y_read"), 2)
            held = {}

            def step(g, r, s):
                if r in (0, RING // 2) and (s is None or s < NP):
                    load_experts(mybir.EngineType.DVE, held, g, range(r, r + RING // 2))
                pair = pair_of(g, r, s, 0)
                if pair is not None:
                    n, turn, place = pair
                    if s is None or s >= 2:
                        dve.wait_ge(sem("h_full"), n - 1)
                        dve.sem_inc(sem("weights_free"), 1)
                    for j in range(2):
                        dve.tensor_copy(weights[:, place % 2, j],
                                        wgu[:, :, bass.ds(held[r][j], 1), :].rearrange("p h o n -> p h (o n)"))\
                            .then_inc(sem("weights_ready"), 1)
                pair = pair_of(g, r, s, 1)
                if pair is not None:
                    n, turn, place = pair
                    dve.wait_ge(sem(f"x_in{place}"), 16 * turn + 16)
                    dve.tensor_copy(goes_to[:, place, :], xin[:, place, :, D].bitcast(I32)).then_inc(sem("numbers_kept"), 1)
                    dve.wait_ge(sem("sig_ready"), n + 1)
                    if s is None or s >= 3:
                        dve.wait_ge(sem("y_full"), n - 1)
                    dve.tensor_tensor(ht[0:F, place % 2], sig[F:2 * F, place % 2], h_ps[place % 2][F:2 * F, 0:2 * P],
                                      ALU.mult).then_inc(sem("ht_ready"), 1)
                pair = pair_of(g, r, s, 3)
                if pair is not None:
                    n, turn, place = pair
                    dve.wait_ge(sem("y_full"), n + 1)
                    if s is None or s >= YRING + 3:
                        dve.wait_ge(sem(f"y_out{place % YRING}"), 32 * (RING // YRING * turn + place // YRING))
                    dve.tensor_copy(ytile[:, place % YRING].rearrange("p j d -> p (j d)"), y_ps[place % 2][:, :])\
                        .then_inc(sem("y_read"), 1)

            all_steps(dve, step, LAG)

    if out is None:
        return

    with ExitStack() as ctx:
        sem = Sems(nc, ctx, phase + "_sum")
        choices = Choices(k, sem, chosen_y)
        block = ctx.enter_context(nc.Block())

        @block.vector
        def _(dve):
            with dve.Fori(0, NT // G) as g:
                for pair in range(G // 2):
                    choices.add_pair(dve, G // 2 * g + pair, g, 2 * pair)

        @block.sync
        def _(sp):
            OUTS = NT // G
            view = out.rearrange("b (t p) c -> p (b t) c", p=P)
            for t in range(NT):
                choices.load(sp, t)
            for g in range(OUTS):
                tiles = slice(g * G, (g + 1) * G)
                sp.wait_ge(sem("added"), K * G * (g + 1))
                sp.dma_start(view[:, tiles, :], k.res[:, tiles, :]).then_inc(sem("stored"), 16)
            sp.wait_ge(sem("stored"), 16 * OUTS)




def retention(nc, k, w_qk, w_vg, w_o, b_q, b_k, b_vg, b_o, gn_w, gn_b, gamma, batches):
    B = batches
    NT, D = k.res.shape[1], k.res.shape[2]
    TB = NT // B
    HEADS = gamma.shape[0]
    DH = D // HEADS
    CH = D // P
    HC = HEADS // CH
    GR = 4
    BLK = 4
    N = BLK * P
    T = TB * P
    H = TB // BLK
    COUNT = float(T * DH)
    assert DH * 2 * GR == P and H == 2 and CH == 2

    arena = k.arena
    arena.at = 0
    wqk = arena.take(CH, 2 * D)
    wvg = arena.take(CH, 2 * D)
    wo = arena.take(CH, D)
    bias_t = arena.take(3, CH)
    bias_v = arena.take(D)
    bias_o = arena.take(D)
    gnw = arena.take(CH)
    gnb = arena.take(CH)
    decay = arena.take(GR, CH, 2, P)
    q_decay = arena.take(CH, P)
    powers = arena.take(2 * P + 1)
    blocks = arena.take(P)
    stats = arena.take(BLK, 6)
    moments = arena.take(BLK, 2)
    rstd = arena.take(BLK)
    xn = arena.take(TB, D)
    xnt = arena.take(H, CH, N)
    qt = arena.take(CH, T)
    qst = arena.take(CH, T)
    kt = arena.take(CH, T)
    keys = arena.take(2, CH, HC, P)
    values = arena.take(TB, HEADS // 2, 3 * DH)
    gates = arena.take(CH, NT * P)
    kd = arena.take(2, D)
    masked_at = arena.at
    masked = arena.take(2, GR, 4 * P)
    turned = arena.take(GR, CH, 2, P, at=masked_at)
    reverse = arena.take(P, at=masked_at + GR * 4 * P)
    state = arena.take(2, CH, P)
    update = arena.take(CH, P)
    ret = arena.take(CH, T)
    square = arena.take(CH, T, at=masked_at)
    sums = arena.take(2, CH)
    minus_mean = arena.take(CH)
    group_scale = arena.take(CH)
    G = 4
    chosen_y = arena.take(G, k.gate.shape[2], D)
    powers_dram = nc.dram_tensor("gamma_powers", (HEADS, 2 * P + 1), F32, kind="Internal").ap()

    with ExitStack() as ctx:
        sem = Sems(nc, ctx, "ret")
        choices = Choices(k, sem, chosen_y)

        def bank(name):
            return ctx.enter_context(nc.psum_tensor(f"ret_{name}", [P, N], F32))

        tp, rt = bank("tp"), bank("rt")
        pj = [bank(f"pj{i}") for i in range(2)]
        sc = [bank(f"sc{g}") for g in range(GR)]
        rts = [rt, pj[0]]
        up = pj[1]
        tpx = [tp, sc[GR - 1]]
        outs = [rt, sc[0]]
        LOADS = 12

        TP_TURN = TB + H

        def tp_chunks(b):
            return H + TP_TURN * b

        def tp_project(b, h, first):
            return h if first else H + TP_TURN * (b - 1) + TB + h

        UP_TURN = TB - 1

        PJ_T = 3 * CH
        PJ_USES = PJ_T + BLK // 2

        def pj_project(b, h):
            return PJ_USES * (H * b + h)

        def pjt_project(b, h):
            return PJ_T * (H * b + h)

        def pjv_project(b, h):
            return (PJ_USES - PJ_T) * (H * b + h)

        RT_TURN = TB + 2 + TB // 2
        block = ctx.enter_context(nc.Block())

        @block.sync
        def _(sp):
            def rows(dst, src, width):
                sp.dma_start(dst, src.rearrange("(o n) -> o n", o=1).to_broadcast([P, width])).then_inc(sem("w"), 16)

            def column(dst, src):
                sp.dma_start(dst, src.rearrange("(h p) -> p h", p=P), allow_slow_non_contiguous=True)\
                    .then_inc(sem("w"), 16)

            sp.dma_start(powers[0:HEADS, P + 1:P + 2], gamma.rearrange("(h o) -> h o", o=1),
                         allow_slow_non_contiguous=True).then_inc(sem("gamma"), 16)
            for t in range(G):
                choices.load(sp, t)
            for h in range(CH):
                sp.dma_start(wqk[:, h], w_qk[h * P:(h + 1) * P]).then_inc(sem("w"), 16)
                sp.dma_start(wvg[:, h], w_vg[h * P:(h + 1) * P]).then_inc(sem("w"), 16)
            sp.dma_start(wo, w_o.rearrange("(h p) n -> p h n", p=P)).then_inc(sem("w"), 16)
            column(bias_t[:, 0], b_q)
            column(bias_t[:, 1], b_k)
            column(bias_t[:, 2], b_vg[D:2 * D])
            column(gnw, gn_w)
            column(gnb, gn_b)
            rows(bias_v, b_vg[0:D], D)
            rows(bias_o, b_o, D)
            sp.wait_ge(sem("powers"), 1)
            sp.dma_start(powers_dram, powers[0:HEADS, :]).then_inc(sem("powers_out"), 16)
            sp.wait_ge(sem("powers_out"), 16)
            W = 2 * P + 1
            for c in range(CH):
                for par in range(2):
                    src = bass.AP(tensor=powers_dram.tensor, offset=(c * HC + par) * W + 1,
                                  ap=[[1, P], [2 * W, GR], [1, P]])
                    sp.dma_start(turned[:, :, c, par, :], src).then_inc(sem("decay"), 16)
                src = bass.AP(tensor=powers_dram.tensor, offset=c * HC * W + P + 1, ap=[[W, HC], [0, DH], [1, P]])
                sp.dma_start(q_decay[:, c, :], src).then_inc(sem("decay"), 16)
            for t in range(G, NT):
                choices.load(sp, t)
                if t >= TB:
                    k.zero_slots(sp, range(k.ZEROINGS * (t - TB) // (NT - TB), k.ZEROINGS * (t + 1 - TB) // (NT - TB)))

        @block.tensor
        def _(pe):
            pe.wait_ge(sem("w"), 16 * LOADS)

            def transpose_x(b, h, first=False):
                pe.wait_ge(sem("tp_read"), tp_project(b, h, first) + 1)
                for c in range(CH):
                    for j in range(BLK):
                        if c == 0:
                            pe.wait_ge(sem("xn_ready"), TB * b + BLK * h + j + 1)
                        last = pe.transpose(tpx[c][:, j * P:(j + 1) * P], xn[:, BLK * h + j, c * P:(c + 1) * P],
                                            k.ident[:, :])
                    last.then_inc(sem("tp_full") if c == 0 else sem("tx_full"), 1)

            def project(b, h, uses):
                pe.wait_ge(sem("xnt_ready"), CH * (H * b + h + 1))
                for m in uses:
                    if m < 2:
                        pe.wait_ge(sem("pjv_read"), pjv_project(b, h) + m + 1)
                    else:
                        pe.wait_ge(sem("pjt_read"), pjt_project(b, h) + m - 1)
                    if m < PJ_T:
                        weights = wqk[:, :, m * P:(m + 1) * P] if m < 2 * CH else wvg[:, :, D + (m - 2 * CH) * P:][:, :, 0:P]
                        for c in range(CH):
                            last = pe.matmul(pj[m % 2][:, :], weights[:, c], xnt[:, h, c, :], start=c == 0, stop=c == CH - 1)
                    else:
                        for i in range(2):
                            j = 2 * (m - PJ_T) + i
                            for c in range(CH):
                                last = pe.matmul(pj[m % 2][:, i * D:(i + 1) * D], xnt[:, h, c, j * P:(j + 1) * P],
                                                 wvg[:, c, 0:D], start=c == 0, stop=c == CH - 1)
                    last.then_inc(sem("pj_full"), 1)

            def chunks(b):
                def output_of(j):
                    bank = rts[j % 2]
                    if j != 1:
                        pe.wait_ge(sem("rt_read"), RT_TURN * b + max(j, 1))
                    pe.wait_ge(sem("masked_ready"), GR * (TB * b + j + 1))
                    pe.wait_ge(sem("state_ready"), TB * b + j + 1)
                    pe.wait_ge(sem("qst_ready"), CH * H * b + CH * (j // BLK + 1))
                    for c in range(CH):
                        cols = slice(c * P, (c + 1) * P)
                        pe.matmul(bank[:, cols], state[:, j % 2, c, :], qst[:, c, j * P:(j + 1) * P],
                                  start=True, stop=False, skip_group_check=True)
                        for g in range(GR):
                            for par in range(2):
                                last = pe.matmul(bank[32 * g:32 * (g + 1), cols],
                                                 values[:, j, GR * c + g, par * DH:(par + 2) * DH],
                                                 masked[:, j % 2, g, (2 * c + par) * P:(2 * c + par + 1) * P],
                                                 start=False, stop=True, skip_group_check=True)
                    last.then_inc(sem("rt_full"), 1)

                pe.wait_ge(sem("rt_read"), RT_TURN * b + 1)
                pe.wait_ge(sem("pjt_read"), pjt_project(b, H))
                pe.wait_ge(sem("pjv_read"), 2 + pjv_project(b, H))
                for j in range(TB):
                    here = slice(j * P, (j + 1) * P)
                    pe.wait_ge(sem("tp_read"), tp_chunks(b) + j + 1)
                    for c in range(CH):
                        last = pe.transpose(tp[:, c * P:(c + 1) * P], kt[:, c, here], k.ident[:, :])
                    last.then_inc(sem("tp_full"), 1)
                    pe.wait_ge(sem("keys_ready"), CH * (TB * b + j + 1))
                    for g in range(GR):
                        pe.wait_ge(sem("sc_read"), GR * (TB * b + j) + g + 1)
                        for c in range(CH):
                            for par in range(2):
                                last = pe.matmul(sc[g][:, (2 * c + par) * P:(2 * c + par + 1) * P],
                                                 keys[:, j % 2, c, 2 * g + par, :], qt[:, c, here], start=True, stop=True)
                        last.then_inc(sem("sc_full"), 1)
                    if j:
                        output_of(j - 1)
                    if j < TB - 1:
                        pe.wait_ge(sem("up_read"), UP_TURN * b + j + 1)
                        pe.wait_ge(sem("kd_ready"), TB * b + j + 1)
                        for c in range(CH):
                            v_of_half = values[:, j, GR * c:GR * (c + 1), :].rearrange("p g (s d) -> p g s d", d=DH)[:, :, 0:3:2, :]
                            last = pe.matmul(up[:, c * P:(c + 1) * P], kd[:, j % 2, c * P:(c + 1) * P],
                                             v_of_half, start=True, stop=True)
                        last.then_inc(sem("up_full"), 1)
                output_of(TB - 1)

            def group_sum(b, i):
                pe.wait_ge(sem("rt_read"), RT_TURN * b + TB + i + 1)
                pe.wait_ge(sem("row_sums") if i == 0 else sem("squared"), (b + 1) if i == 0 else CH * (b + 1))
                pe.matmul(rt[:, 0:CH], blocks, sums[:, i, :], start=True, stop=True).then_inc(sem("rt_full"), 1)

            def output(b):
                for i in range(TB // 2):
                    pe.wait_ge(sem("rt_read"), RT_TURN * b + TB + 2 + max(i, 1))
                    if i == 0:
                        pe.wait_ge(sem("gated"), CH * (b + 1))
                    for j in range(2):
                        for c in range(CH):
                            at = (2 * i + j) * P
                            last = pe.matmul(outs[i % 2][:, j * D:(j + 1) * D], ret[:, c, at:at + P], wo[:, c, :],
                                             start=c == 0, stop=c == CH - 1)
                    last.then_inc(sem("rt_full"), 1)

            for h in range(H):
                transpose_x(0, h, first=True)
                project(0, h, range(PJ_USES))
            pe.wait_ge(sem("decay"), 16 * 3 * CH)
            pe.wait_ge(sem("reverse"), 2)
            for g in range(GR):
                pe.matmul(sc[g][:, :], reverse, turned[:, g].rearrange("p c q n -> p (c q n)"), start=True, stop=True)\
                    .then_inc(sem("decay_turned"), 1)
            with pe.Fori(0, B - 1) as b:
                chunks(b)
                transpose_x(b + 1, 0)
                pe.wait_ge(sem("rt_read"), RT_TURN * b + TB + 1)
                pe.wait_ge(sem("up_read"), 1 + UP_TURN * (b + 1))
                project(b + 1, 0, range(2 * CH))
                group_sum(b, 0)
                project(b + 1, 0, range(2 * CH, PJ_USES))
                transpose_x(b + 1, 1)
                group_sum(b, 1)
                project(b + 1, 1, range(PJ_USES))
                output(b)
            chunks(B - 1)
            group_sum(B - 1, 0)
            group_sum(B - 1, 1)
            output(B - 1)

        @block.scalar
        def _(act):
            act.preload_act_table(ACT.Silu)
            act.wait_ge(sem("w"), 16 * LOADS)

            def copy_xt(b, h, first=False):
                act.wait_ge(sem("tp_full"), tp_project(b, h, first) + 1)
                act.activation(xnt[:, h, 0, :], tpx[0][:, :], ACT.Copy).then_inc(sem("tp_read"), 1)
                act.wait_ge(sem("tx_full"), H * b + h + 1)
                act.activation(xnt[:, h, 1, :], tpx[1][:, :], ACT.Copy).then_inc(sem("tx_read"), 1)
                act.wait_ge(sem("tp_read"), tp_project(b, h, first) + 2)
                act.wait_ge(sem("tx_read"), H * b + h + 1)
                act.sem_inc(sem("xnt_ready"), CH)

            def add_bias(b, h, uses):
                for m in uses:
                    act.wait_ge(sem("pj_full"), pj_project(b, h) + m + 1)
                    bias = bias_t[:, m // CH, m % CH:m % CH + 1]
                    if m < 2 * CH:
                        dst = (qt if m < CH else kt)[:, m % CH, h * N:(h + 1) * N]
                        act.activation(dst, pj[m % 2][:, :], ACT.Identity, bias=bias).then_inc(sem("pjt_read"), 1)
                    else:
                        act.activation(gates[:, m % CH, bass.ds(T * b + h * N, N)], pj[m % 2][:, :], ACT.Silu, bias=bias)\
                            .then_inc(sem("pjt_read"), 1)

            def chunks(b):
                for j in range(TB):
                    act.wait_ge(sem("rt_full"), RT_TURN * b + j + 1)
                    act.activation(ret[:, :, j * P:(j + 1) * P], rts[j % 2][:, 0:D].rearrange("p (c n) -> p c n", c=CH), ACT.Copy)\
                        .then_inc(sem("rt_read"), 1)
                act.wait_ge(sem("rt_read"), 1 + RT_TURN * b + TB)
                act.sem_inc(sem("ret_kept"), 1)

            def squares(b):
                act.wait_ge(sem("mean_ready"), b + 1)
                for c in range(CH):
                    act.activation(square[:, c, :], ret[:, c, :], ACT.Square, bias=minus_mean[:, c:c + 1],
                                   accum_out=sums[:, 1, c:c + 1]).then_inc(sem("squared"), 1)

            for h in range(H):
                copy_xt(0, h, first=True)
                add_bias(0, h, range(PJ_T))
            for g in range(GR):
                act.wait_ge(sem("decay_turned"), g + 1)
                act.activation(decay[:, g].rearrange("p c q n -> p (c q n)"), sc[g][:, :], ACT.Copy)\
                    .then_inc(sem("decay_ready"), 1)
            with act.Fori(0, B - 1) as b:
                chunks(b)
                copy_xt(b + 1, 0)
                add_bias(b + 1, 0, range(PJ_T))
                squares(b)
                copy_xt(b + 1, 1)
                add_bias(b + 1, 1, range(PJ_T))
            chunks(B - 1)
            squares(B - 1)

        @block.gpsimd
        def _(pool):
            thirds = values.rearrange("p t g (s d) -> p (t g) s d", d=DH)
            pool.memset(thirds[:, :, 1, :], 0.0).then_inc(sem("values_cleared"), 1)
            pool.memset(blocks, 1.0).then_inc(sem("blocks"), 1)
            pool.memset(reverse, 0.0).then_inc(sem("reverse"), 1)
            pool.wait_ge(sem("reverse"), 1)
            pool.affine_select(out=reverse, in_=reverse, compare_op=ALU.not_equal, fill=1.0, base=1 - P,
                               pattern=[[1, P]], channel_multiplier=1).then_inc(sem("reverse"), 1)
            pool.wait_ge(sem("blocks"), 1)
            cells = blocks.rearrange("p (a b) -> p a b", b=DH)
            pool.affine_select(out=cells, in_=cells, compare_op=ALU.is_ge, fill=0.0, base=0,
                               pattern=[[-DH, HC], [0, DH]], channel_multiplier=1).then_inc(sem("blocks"), 1)
            pool.wait_ge(sem("blocks"), 2)
            pool.affine_select(out=cells, in_=cells, compare_op=ALU.is_ge, fill=0.0, base=DH - 1,
                               pattern=[[DH, HC], [0, DH]], channel_multiplier=-1).then_inc(sem("blocks"), 1)
            pool.wait_ge(sem("w"), 16 * LOADS)

            def layernorm_power(n):
                pool.wait_ge(sem("var_ready"), n + 1)
                pool.tensor_tensor(rstd, rstd, k.minus_half[:, 0:BLK], ALU.pow).then_inc(sem("rstd_ready"), 1)

            def decay_q(b, h):
                pool.wait_ge(sem("pjt_read"), pjt_project(b, h) + CH)
                for c in range(CH):
                    q4 = qt[:, c, h * N:(h + 1) * N].rearrange("p (j n) -> p j n", n=P)
                    s4 = qst[:, c, h * N:(h + 1) * N].rearrange("p (j n) -> p j n", n=P)
                    pool.tensor_tensor(s4, q4, q_decay[:, c, :].unsqueeze(1).to_broadcast([P, BLK, P]), ALU.mult)\
                        .then_inc(sem("qst_ready"), 1)

            def add_output_bias(b):
                pool.wait_ge(sem("choices_added"), b + 1)
                tiles = k.res[:, bass.ds(TB * b, TB), :]
                pool.tensor_tensor(tiles, tiles, bias_o.unsqueeze(1).to_broadcast([P, TB, D]), ALU.add)\
                    .then_inc(sem("bias_added"), 1)

            def split_keys(b, chunks):
                for j in chunks:
                    if j == 0:
                        pool.wait_ge(sem("pjt_read"), pjt_project(b, H))
                    if j >= 2:
                        pool.wait_ge(sem("sc_full"), GR * (TB * b + j - 1))
                    for c in range(CH):
                        pool.tensor_tensor(keys[:, j % 2, c], kt[:, c, j * P:(j + 1) * P].unsqueeze(1).to_broadcast([P, HC, P]),
                                           cells[:, :, 0:1].to_broadcast([P, HC, P]), ALU.mult)\
                            .then_inc(sem("keys_ready"), 1)

            def group_power(b):
                pool.wait_ge(sem("group_var"), b + 1)
                pool.tensor_tensor(group_scale, group_scale, k.minus_half[:, 0:CH], ALU.pow)\
                    .then_inc(sem("group_rstd"), 1)

            for h in range(H):
                layernorm_power(h)
            pool.wait_ge(sem("decay"), 16 * 3 * CH)
            for h in range(H):
                decay_q(0, h)
            pool.wait_ge(sem("blocks"), 3)
            with pool.Fori(0, B - 1) as b:
                split_keys(b, range(0, 7))
                layernorm_power(H * (b + 1))
                split_keys(b, range(7, TB))
                layernorm_power(H * (b + 1) + 1)
                decay_q(b + 1, 0)
                group_power(b)
                decay_q(b + 1, 1)
                add_output_bias(b)
            split_keys(B - 1, range(TB))
            add_output_bias(B - 1)
            group_power(B - 1)

        @block.vector
        def _(dve):
            dve.sem_inc(sem("tp_read"), 1)
            dve.sem_inc(sem("rt_read"), 1)
            dve.sem_inc(sem("up_read"), 1)
            dve.sem_inc(sem("pjv_read"), 2)

            def statistics(b, h):
                choices.settled(dve, TB // 2 * b + BLK // 2 * (h + 1))
                steps = Chain(dve, sem("ln_steps"), (2 * BLK + 1) * H, b, (2 * BLK + 1) * h)
                for j in range(BLK):
                    steps.step(dve.bn_stats(stats[:, j, :], one_tile(k.res, TB * b + BLK * h + j)))
                steps.settled()
                dve.sem_inc(sem("stats_complete"), 1)
                for j in range(BLK):
                    steps.step(dve.bn_aggr(moments[:, j, :], stats[:, j, :]))
                steps.settled()
                steps.step(dve.tensor_scalar(rstd, moments[:, :, 1], EPS, None, ALU.add))
                steps.settled()
                dve.sem_inc(sem("var_ready"), 1)

            def normalise(b, h):
                dve.wait_ge(sem("rstd_ready"), H * b + h + 1)
                for j in range(BLK):
                    t = BLK * h + j
                    dve.tensor_scalar(xn[:, t, :], one_tile(k.res, TB * b + t), moments[:, j, 0:1], rstd[:, j:j + 1],
                                      ALU.subtract, ALU.mult).then_inc(sem("xn_ready"), 1)
                if h == H - 1:
                    dve.wait_ge(sem("xn_ready"), TB * (b + 1))
                    dve.sem_inc(sem("choices_added"), 1)

            def add_choices(b, pair):
                choices.add_pair(dve, TB // 2 * b + pair, TB // G * b + 2 * pair // G, 2 * pair % G)

            def keep_values(b, h):
                for m in range(PJ_T, PJ_USES):
                    dve.wait_ge(sem("pj_full"), pj_project(b, h) + m + 1)
                    for i in range(2):
                        t = BLK * h + 2 * (m - PJ_T) + i
                        place = values[:, t].rearrange("p g (s d) -> p g s d", d=DH)[:, :, 0:3:2, :]
                        last = dve.tensor_tensor(place, pj[m % 2][:, i * D:(i + 1) * D].rearrange("p (g s d) -> p g s d", s=2, d=DH),
                                                 bias_v.rearrange("p (g s d) -> p g s d", s=2, d=DH), ALU.add)
                    last.then_inc(sem("pjv_read"), 1)

            def chunk(b, j):
                steps = Chain(dve, sem("state_steps"), 1 + 2 * (TB - 1), b, 0 if j == 0 else 1 + 2 * j)
                dve.wait_ge(sem("tp_full"), tp_chunks(b) + j + 1)
                if j == 0:
                    steps.step(dve.memset(state[:, 0], 0.0))
                for c in range(CH):
                    last = dve.tensor_tensor(
                        kd[:, j % 2, c * P:(c + 1) * P].rearrange("p (g q d) -> p g q d", g=GR, q=2),
                        tp[:, c * P:(c + 1) * P].rearrange("p (g q d) -> p g q d", g=GR, q=2),
                        decay[:, :, c, :, P - 1:P].to_broadcast([P, GR, 2, DH]), ALU.mult)
                last.then_inc(sem("tp_read"), 1)
                dve.wait_ge(sem("tp_read"), 1 + tp_chunks(b) + j + 1)
                dve.sem_inc(sem("kd_ready"), 1)
                for g in range(GR):
                    dve.wait_ge(sem("sc_full"), GR * (TB * b + j) + g + 1)
                    dve.tensor_tensor(masked[:, j % 2, g, :], sc[g][:, :], decay[:, g].rearrange("p c q n -> p (c q n)"),
                                      ALU.mult).then_inc(sem("sc_read"), 1)
                dve.wait_ge(sem("sc_read"), GR + GR * (TB * b + j + 1))
                dve.sem_inc(sem("masked_ready"), GR)
                if j == 0:
                    steps.settled()
                    dve.sem_inc(sem("state_ready"), 1)
                if j < TB - 1:
                    dve.wait_ge(sem("up_full"), UP_TURN * b + j + 1)
                    dve.tensor_tensor(update, up[:, 0:2 * P].rearrange("p (c n) -> p c n", c=CH),
                                      blocks.unsqueeze(1).to_broadcast([P, CH, P]), ALU.mult).then_inc(sem("up_read"), 1)
                    dve.wait_ge(sem("up_read"), 1 + UP_TURN * b + j + 1)
                    for c in range(CH):
                        steps.step(dve.scalar_tensor_tensor(state[:, (j + 1) % 2, c, :], state[:, j % 2, c, :],
                                                            q_decay[:, c, P - 1:P], update[:, c, :], ALU.mult, ALU.add))
                    steps.settled()
                    dve.sem_inc(sem("state_ready"), 1)

            def sum_rows(b):
                dve.wait_ge(sem("ret_kept"), b + 1)
                dve.tensor_reduce(sums[:, 0, :], ret, AX_X, ALU.add).then_inc(sem("row_sums"), 1)

            def mean(b):
                dve.wait_ge(sem("rt_full"), RT_TURN * b + TB + 1)
                dve.tensor_scalar(minus_mean, rt[:, 0:CH], -1.0 / COUNT, None, ALU.mult).then_inc(sem("rt_read"), 1)
                dve.wait_ge(sem("rt_read"), 1 + RT_TURN * b + TB + 1)
                dve.sem_inc(sem("mean_ready"), 1)

            def variance(b):
                dve.wait_ge(sem("rt_full"), RT_TURN * b + TB + 2)
                dve.tensor_scalar(group_scale, rt[:, 0:CH], 1.0 / COUNT, EPS, ALU.mult, ALU.add)\
                    .then_inc(sem("rt_read"), 1)
                dve.wait_ge(sem("rt_read"), 1 + RT_TURN * b + TB + 2)
                dve.sem_inc(sem("group_var"), 1)

            def gate(b):
                steps = Chain(dve, sem("gate_steps"), 1 + CH, b)
                dve.wait_ge(sem("group_rstd"), b + 1)
                steps.link(dve.tensor_tensor(group_scale, group_scale, gnw, ALU.mult))
                for c in range(CH):
                    steps.step(dve.tensor_scalar(ret[:, c], ret[:, c], minus_mean[:, c:c + 1], group_scale[:, c:c + 1],
                                                 ALU.add, ALU.mult))
                steps.settled()
                for c in range(CH):
                    dve.scalar_tensor_tensor(ret[:, c], ret[:, c], gnb[:, c:c + 1], gates[:, c, bass.ds(T * b, T)],
                                             ALU.add, ALU.mult).then_inc(sem("gated"), 1)

            def output(b):
                dve.wait_ge(sem("bias_added"), b + 1)
                for i in range(TB // 2):
                    dve.wait_ge(sem("rt_full"), RT_TURN * b + TB + 2 + i + 1)
                    tiles = k.res[:, bass.ds(TB * b + 2 * i, 2), :]
                    dve.tensor_tensor(tiles, tiles, outs[i % 2][:, :].rearrange("p (j d) -> p j d", d=D), ALU.add)\
                        .then_inc(sem("rt_read"), 1)

            dve.wait_ge(sem("gamma"), 16)
            c = Chain(dve, sem("setup"))
            c.step(dve.memset(powers[0:HEADS, 0:P], 0.0))
            c.step(dve.memset(powers[0:HEADS, P:P + 1], 1.0))
            m = 1
            while m < P:
                c.link(dve.tensor_scalar(powers[0:HEADS, P + m + 1:P + 2 * m + 1], powers[0:HEADS, P + 1:P + m + 1],
                                         powers[0:HEADS, P + m:P + m + 1], None, ALU.mult))
                m *= 2
            dve.sem_inc(sem("powers"), 1)
            for h in range(H):
                for pair in range(BLK // 2):
                    add_choices(0, BLK // 2 * h + pair)
                statistics(0, h)
                normalise(0, h)
            dve.wait_ge(sem("w"), 16 * LOADS)
            for h in range(H):
                keep_values(0, h)
            dve.wait_ge(sem("values_cleared"), 1)
            dve.wait_ge(sem("decay_ready"), GR)
            dve.sem_inc(sem("sc_read"), GR)
            dve.wait_ge(sem("decay"), 16 * 3 * CH)
            dve.wait_ge(sem("blocks"), 3)

            def chunks(b, last_one=False):
                for j in range(TB):
                    chunk(b, j)
                    if last_one:
                        continue
                    if j in (1, 3):
                        add_choices(b + 1, j // 2)
                    if j == 4:
                        statistics(b + 1, 0)
                    if j == 5:
                        normalise(b + 1, 0)

            with dve.Fori(0, B - 1) as b:
                chunks(b)
                sum_rows(b)
                add_choices(b + 1, 2)
                add_choices(b + 1, 3)
                mean(b)
                statistics(b + 1, 1)
                normalise(b + 1, 1)
                keep_values(b + 1, 0)
                variance(b)
                gate(b)
                keep_values(b + 1, 1)
                output(b)
            chunks(B - 1, last_one=True)
            sum_rows(B - 1)
            mean(B - 1)
            variance(B - 1)
            gate(B - 1)
            output(B - 1)
            dve.wait_ge(sem("rt_read"), 1 + RT_TURN * B)




class Kept:

    CONSTS = 6

    def __init__(self, nc, ctx):
        def sb(name, shape, dt):
            return ctx.enter_context(nc.sbuf_tensor(name, shape, dt))

        self.nc = nc
        self.ident = sb("ident", [P, P], F32)
        self.gate = sb("gate", [P, 32, 4], F32)[:, :, :]
        self.ones_bf = sb("ones_bf", [P, P], BF16)
        self.tri_bf = sb("tri_bf", [P, P], BF16)
        self.iota64 = sb("iota64", [P, 64], F32)
        self.minus_half = sb("minus_half", [P, 64], F32)
        self.zero = sb("empty_slots", [P, 4 * (256 + Slots.TAIL)], F32)
        self.const_made = ctx.enter_context(nc.semaphore("const_made"))
        self.const_ready = ctx.enter_context(nc.semaphore("const_ready"))
        self.res = sb("residual", [P, 32, 256], F32)
        self.slots = Slots(nc, 32 * P, 256, 64, 4)
        self.ZEROINGS = self.slots.tiles // 4
        self.slots_zeroed = ctx.enter_context(nc.semaphore("slots_zeroed"))
        floats = 43008
        self.arena = Arena(sb("arena", [P, floats], F32), floats)

    def zero_slots(self, sp, parts=None):
        sp.wait_ge(self.const_ready, self.CONSTS)
        rows = self.slots.x.rearrange("(n p r) d -> n p (r d)", p=P, r=4)
        for n in range(self.ZEROINGS) if parts is None else parts:
            sp.dma_start(rows[n], self.zero[:, :]).then_inc(self.slots_zeroed, 16)

    def make_constants(self, pool):
        made = self.const_made
        pool.memset(self.ident[:, :], 0.0).then_inc(made, 1)
        pool.memset(self.tri_bf[:, :], 1.0).then_inc(made, 1)
        pool.memset(self.ones_bf[:, :], 1.0).then_inc(made, 1)
        pool.memset(self.minus_half[:, :], -0.5).then_inc(made, 1)
        pool.memset(self.zero[:, :], 0.0).then_inc(made, 1)
        pool.iota(self.iota64[:, :], [[1, 64]], base=0, channel_multiplier=0,
                  allow_small_or_imprecise_dtypes=True).then_inc(made, 1)
        pool.wait_ge(made, self.CONSTS)
        pool.affine_select(out=self.ident[:, :], in_=self.ident[:, :], compare_op=ALU.not_equal, fill=1.0, base=0,
                           pattern=[[-1, P]], channel_multiplier=1).then_inc(self.const_ready, 1)
        pool.affine_select(out=self.tri_bf[:, :], in_=self.tri_bf[:, :], compare_op=ALU.is_gt, fill=0.0, base=0,
                           pattern=[[1, P]], channel_multiplier=-1).then_inc(self.const_ready, 1)
        pool.memset(self.zero[:, :].rearrange("p (r d) -> p r d", r=4)[:, :, 256:], Slots.NO_PAIR)\
            .then_inc(self.const_ready, 1)
        pool.wait_ge(self.const_ready, 3)
        pool.sem_inc(self.const_ready, self.CONSTS - 3)




def program(nc, x, w_rvk, w_out, time_decay, time_first, w_qk, w_vg, w_o, b_q, b_k, b_vg, b_o, gn_w, gn_b, gamma,
            router_w, router_bias, w_gu, w_d, sw_gu, sw_d, out):
    with ExitStack() as ctx:
        k = Kept(nc, ctx)
        time_mix(nc, k, x, w_rvk, w_out, time_decay, time_first)
        experts(nc, k, "moe1", 16 * k.ZEROINGS, router_w, router_bias, w_gu, w_d, sw_gu, sw_d)
        retention(nc, k, w_qk, w_vg, w_o, b_q, b_k, b_vg, b_o, gn_w, gn_b, gamma, x.shape[0])
        experts(nc, k, "moe2", 2 * 16 * k.ZEROINGS, router_w, router_bias, w_gu, w_d, sw_gu, sw_d, out=out)


def kernel(**inputs):
    import numpy as np
    import concourse.bacc as bacc
    from concourse.bass_utils import run_bass_kernel_spmd

    a, b, f = "L0_attn_a_", "L0_attn_b_", "L0_ffn_"
    g = {n: np.asarray(v) for n, v in inputs.items()}
    D = g[a + "x"].shape[-1]

    def joined(w):
        return np.transpose(w, (1, 0, 2)).reshape(D, -1)

    arrays = {
        "x": g[a + "x"],
        "w_rvk": g[a + "W_rvk"].T,
        "w_out": g[a + "W_out"].T,
        "time_decay": g[a + "time_decay"],
        "time_first": g[a + "time_first"],
        "w_qk": np.concatenate([g[b + "wq"], g[b + "wk"]], axis=1),
        "w_vg": np.concatenate([g[b + "wv"], g[b + "wg"]], axis=1),
        "w_o": g[b + "wo"],
        "b_q": g[b + "bq"],
        "b_k": g[b + "bk"],
        "b_vg": np.concatenate([g[b + "bv"], g[b + "bg"]]),
        "b_o": g[b + "bo"],
        "gn_w": g[b + "gn_w"],
        "gn_b": g[b + "gn_b"],
        "gamma": g[b + "gamma"],
        "router_w": g[f + "router_w"],
        "router_bias": g[f + "router_bias"],
        "w_gu": np.transpose(np.concatenate([g[f + "wg"], g[f + "wu"]], axis=2), (1, 0, 2)),
        "w_d": g[f + "wd"],
        "sw_gu": np.concatenate([joined(g[f + "swg"]), joined(g[f + "swu"])], axis=1),
        "sw_d": g[f + "swd"].reshape(-1, D),
    }
    arrays = {n: np.ascontiguousarray(v) for n, v in arrays.items()}
    nc = bacc.Bacc("TRN2", target_bir_lowering=False, num_devices=1)
    aps = {n: nc.dram_tensor(n, v.shape, mybir.dt.from_np(v.dtype), kind="ExternalInput").ap()
           for n, v in arrays.items()}
    out = nc.dram_tensor("out", arrays["x"].shape, F32, kind="ExternalOutput").ap()
    program(nc, out=out, **aps)
    return run_bass_kernel_spmd(nc, [arrays], core_ids=[0]).results[0]["out"]
```
